# Optimizing a Trainium2 kernel written in Bass

```python
import numpy as np
import jax
import jax.numpy as jnp

def _softmax(x, axis=-1):
    return jax.nn.softmax(x, axis=axis)

def _gelu(x):
    return jax.nn.gelu(x, approximate=True)

def _silu(x):
    return jax.nn.silu(x)

def _sigmoid(x):
    return jax.nn.sigmoid(x)

def _layernorm(x, axis=-1, eps=1e-05):
    m = jnp.mean(x, axis=axis, keepdims=True)
    v = jnp.var(x, axis=axis, keepdims=True)
    return (x - m) / jnp.sqrt(v + eps)

def _scatter_add(tgt, idx, src, axis=0):
    return tgt.at[idx].add(src)

def _segment_sum(src, seg, n):
    return jax.ops.segment_sum(src, seg, n)
kernel_name = 'mk_macaron_d1_jaxref_r8_f5131b'

def setup_inputs(seed: int=0):
    np.random.seed(seed)
    _w = jnp.asarray

    def _L0_attn_setup():
        import jax, jax.numpy as jnp
        import numpy as np
        E2M1_GRID = jnp.array([0.0, 0.5, 1.0, 1.5, 2.0, 3.0, 4.0, 6.0], dtype=jnp.float32)
        E2M1_MIDS = (E2M1_GRID[1:] + E2M1_GRID[:-1]) / 2.0
        FP4_MAX = 6.0
        FP8_E4M3_MAX = 448.0

        def nvfp4_quant_dequant(w):
            O, I = w.shape
            w16 = w.reshape(O, I // 128, 8, 16)
            amax128 = jnp.max(jnp.abs(w16), axis=(-2, -1))
            outer = amax128 / (FP4_MAX * FP8_E4M3_MAX)
            outer = jnp.where(outer > 0, outer, 1.0)
            amax16 = jnp.max(jnp.abs(w16), axis=-1)
            inner = amax16 / FP4_MAX / outer[..., None]
            inner = inner.astype(jnp.float8_e4m3fn).astype(jnp.float32)
            scale = outer[..., None] * inner
            safe = jnp.where(scale > 0, scale, 1.0)[..., None]
            code = w16 / safe
            a = jnp.abs(code)
            idx = jnp.searchsorted(E2M1_MIDS, a)
            q = E2M1_GRID[idx] * jnp.sign(code)
            return (q * scale[..., None]).reshape(O, I)
        key = jax.random.key(seed)
        k0, k1, k2 = jax.random.split(key, 3)
        B, S, H = (2, 256, 256)
        hidden_states = jax.random.normal(k0, (B, S, H), dtype=jnp.float32)
        w_qkv = jax.random.normal(k1, (3 * H, H), dtype=jnp.float32) * 0.023
        w_o = jax.random.normal(k2, (H, H), dtype=jnp.float32) * 0.023
        w_qkv = nvfp4_quant_dequant(w_qkv)
        w_o = nvfp4_quant_dequant(w_o)
        return {'hidden_states': hidden_states, 'w_qkv': w_qkv, 'w_o': w_o}
    _L0_attn_in = _L0_attn_setup()

    def _L0_ffn_setup():
        import jax, jax.numpy as jnp
        import numpy as np
        import math
        D_MODEL = 256
        D_FF = 1024
        NUM_EXPERTS = 8
        TOP_K = 2
        CAPACITY_FACTOR = 1.25
        BATCH, SEQ = (4, 256)

        def _moe_forward(x, Wg, w1, w2):
            B, T, d = x.shape
            S = B * T
            E, K = (NUM_EXPERTS, TOP_K)
            C = math.ceil(CAPACITY_FACTOR * S * K / E)
            xr = x.reshape(S, d)
            probs = jax.nn.softmax(xr @ Wg, axis=-1)
            gate_vals, expert_idx = jax.lax.top_k(probs, K)
            flat_e = expert_idx.reshape(-1)
            oh = jax.nn.one_hot(flat_e, E, dtype=jnp.int32)
            pos = jnp.sum((jnp.cumsum(oh, axis=0) - 1) * oh, axis=1)
            kept = pos < C
            i = jnp.arange(S * K)
            slot = i % K * S + i // K
            sentinel = S * K
            pos_w = jnp.where(kept, pos, C)
            dispatch_mask = jnp.full((E, C), sentinel, dtype=jnp.int32)
            dispatch_mask = dispatch_mask.at[flat_e, pos_w].set(slot.astype(jnp.int32), mode='drop')
            combine_weights = (gate_vals * kept.reshape(S, K)).T
            dispatched = xr[dispatch_mask.reshape(-1) % S].reshape(E, C, d)
            h = jax.nn.relu(jnp.einsum('ecd,edf->ecf', dispatched, w1))
            expert_out = jnp.einsum('ecf,efd->ecd', h, w2)
            rerouted = jnp.zeros((S * K + 1, d), dtype=expert_out.dtype)
            rerouted = rerouted.at[dispatch_mask.reshape(-1)].set(expert_out.reshape(-1, d))
            rerouted = rerouted[:-1].reshape(K, S, d)
            out = jnp.einsum('ks,ksm->sm', combine_weights, rerouted)
            return out.reshape(B, T, d)
        key = jax.random.key(seed)
        k1, k2, k3, k4 = jax.random.split(key, 4)
        x = jax.random.normal(k1, (BATCH, SEQ, D_MODEL), dtype=jnp.float32)
        Wg = jax.random.normal(k2, (D_MODEL, NUM_EXPERTS), dtype=jnp.float32) * 0.02
        w1 = jax.random.normal(k3, (NUM_EXPERTS, D_MODEL, D_FF), dtype=jnp.float32) * 0.02
        w2 = jax.random.normal(k4, (NUM_EXPERTS, D_FF, D_MODEL), dtype=jnp.float32) * 0.02
        return {'x': x, 'Wg': Wg, 'w1': w1, 'w2': w2}
    _L0_ffn_in = _L0_ffn_setup()
    _d = {'L0_attn_hidden_states': _L0_attn_in['hidden_states'], 'L0_attn_w_qkv': _L0_attn_in['w_qkv'], 'L0_attn_w_o': _L0_attn_in['w_o'], 'L0_ffn_Wg': _L0_ffn_in['Wg'], 'L0_ffn_w1': _L0_ffn_in['w1'], 'L0_ffn_w2': _L0_ffn_in['w2']}
    _x0 = _d['L0_attn_hidden_states']
    _d['L0_attn_hidden_states'] = jax.random.normal(jax.random.fold_in(jax.random.key(seed), 1), (4, 512, 256), dtype=_x0.dtype)
    del _x0
    return _d

def reference(L0_attn_hidden_states, L0_attn_w_qkv, L0_attn_w_o, L0_ffn_Wg, L0_ffn_w1, L0_ffn_w2):

    def _L0_attn_ref(hidden_states, w_qkv, w_o):
        import jax, jax.numpy as jnp
        import numpy as np
        E2M1_GRID = jnp.array([0.0, 0.5, 1.0, 1.5, 2.0, 3.0, 4.0, 6.0], dtype=jnp.float32)
        E2M1_MIDS = (E2M1_GRID[1:] + E2M1_GRID[:-1]) / 2.0
        FP4_MAX = 6.0
        FP8_E4M3_MAX = 448.0

        def nvfp4_quant_dequant(w):
            O, I = w.shape
            w16 = w.reshape(O, I // 128, 8, 16)
            amax128 = jnp.max(jnp.abs(w16), axis=(-2, -1))
            outer = amax128 / (FP4_MAX * FP8_E4M3_MAX)
            outer = jnp.where(outer > 0, outer, 1.0)
            amax16 = jnp.max(jnp.abs(w16), axis=-1)
            inner = amax16 / FP4_MAX / outer[..., None]
            inner = inner.astype(jnp.float8_e4m3fn).astype(jnp.float32)
            scale = outer[..., None] * inner
            safe = jnp.where(scale > 0, scale, 1.0)[..., None]
            code = w16 / safe
            a = jnp.abs(code)
            idx = jnp.searchsorted(E2M1_MIDS, a)
            q = E2M1_GRID[idx] * jnp.sign(code)
            return (q * scale[..., None]).reshape(O, I)
        B, S, H = hidden_states.shape
        num_heads = 16
        head_dim = H // num_heads
        qkv = jnp.einsum('bsh,oh->bso', hidden_states, w_qkv)
        qkv = qkv.reshape(B, S, 3, num_heads, head_dim)
        qkv = jnp.transpose(qkv, (2, 0, 3, 1, 4))
        q, k, v = (qkv[0], qkv[1], qkv[2])
        scale = 1.0 / jnp.sqrt(jnp.float32(head_dim))
        scores = jnp.einsum('bhqd,bhkd->bhqk', q, k) * scale
        causal = jnp.tril(jnp.ones((S, S), dtype=bool))
        scores = jnp.where(causal, scores, jnp.finfo(scores.dtype).min)
        probs = jax.nn.softmax(scores, axis=-1)
        attn = jnp.einsum('bhqk,bhkd->bhqd', probs, v)
        attn = jnp.transpose(attn, (0, 2, 1, 3)).reshape(B, S, H)
        return jnp.einsum('bsh,oh->bso', attn, w_o)

    def _L0_ffn_ref(x, Wg, w1, w2):
        import jax, jax.numpy as jnp
        import numpy as np
        import math
        D_MODEL = 256
        D_FF = 1024
        NUM_EXPERTS = 8
        TOP_K = 2
        CAPACITY_FACTOR = 1.25
        BATCH, SEQ = (4, 256)

        def _moe_forward(x, Wg, w1, w2):
            B, T, d = x.shape
            S = B * T
            E, K = (NUM_EXPERTS, TOP_K)
            C = math.ceil(CAPACITY_FACTOR * S * K / E)
            xr = x.reshape(S, d)
            probs = jax.nn.softmax(xr @ Wg, axis=-1)
            gate_vals, expert_idx = jax.lax.top_k(probs, K)
            flat_e = expert_idx.reshape(-1)
            oh = jax.nn.one_hot(flat_e, E, dtype=jnp.int32)
            pos = jnp.sum((jnp.cumsum(oh, axis=0) - 1) * oh, axis=1)
            kept = pos < C
            i = jnp.arange(S * K)
            slot = i % K * S + i // K
            sentinel = S * K
            pos_w = jnp.where(kept, pos, C)
            dispatch_mask = jnp.full((E, C), sentinel, dtype=jnp.int32)
            dispatch_mask = dispatch_mask.at[flat_e, pos_w].set(slot.astype(jnp.int32), mode='drop')
            combine_weights = (gate_vals * kept.reshape(S, K)).T
            dispatched = xr[dispatch_mask.reshape(-1) % S].reshape(E, C, d)
            h = jax.nn.relu(jnp.einsum('ecd,edf->ecf', dispatched, w1))
            expert_out = jnp.einsum('ecf,efd->ecd', h, w2)
            rerouted = jnp.zeros((S * K + 1, d), dtype=expert_out.dtype)
            rerouted = rerouted.at[dispatch_mask.reshape(-1)].set(expert_out.reshape(-1, d))
            rerouted = rerouted[:-1].reshape(K, S, d)
            out = jnp.einsum('ks,ksm->sm', combine_weights, rerouted)
            return out.reshape(B, T, d)
        return _moe_forward(x, Wg, w1, w2)
    x = L0_attn_hidden_states
    x = x + 0.5 * _L0_ffn_ref(_layernorm(x, axis=-1), L0_ffn_Wg, L0_ffn_w1, L0_ffn_w2)
    x = x + _L0_attn_ref(_layernorm(x, axis=-1), L0_attn_w_qkv, L0_attn_w_o)
    x = x + 0.5 * _L0_ffn_ref(_layernorm(x, axis=-1), L0_ffn_Wg, L0_ffn_w1, L0_ffn_w2)
    return x

_drawn_inputs = setup_inputs


def setup_inputs(seed=0):
    import zlib

    import numpy as np

    out = dict(_drawn_inputs(seed))
    spreads = {}
    factors = {'L0_attn_w_qkv': 3.402, 'L0_attn_w_o': 3.265}
    for name, (base, spread) in spreads.items():
        noise = np.random.default_rng([zlib.crc32(name.encode()), seed]).standard_normal(out[name].shape)
        drawn = base * np.exp(spread * noise) if base else spread * noise
        out[name] = jnp.asarray(drawn.astype(out[name].dtype))
    for name, factor in factors.items():
        out[name] = (out[name] * factor).astype(out[name].dtype)
    return out
```

```python
from contextlib import ExitStack

import concourse.bass as bass
from concourse import mybir

F32 = mybir.dt.float32
F32R = mybir.dt.float32r
BF16 = mybir.dt.bfloat16
I32 = mybir.dt.int32
ALU = mybir.AluOpType
ACT = mybir.ActivationFunctionType
AX_X = mybir.AxisListType.X

P = 128
BATCH, SEQ, D = 4, 512, 256
TOK = BATCH * SEQ
T = TOK // P
DK = D // P
FF = 1024
FT = FF // P
E, K = 8, 2
CAP = -(-5 * TOK * K // (4 * E))
ST = CAP // P
LC = E * ST
HALF = CAP // 2
EPS = 1e-5
FAR = 4096
NEG = -3.0e38
"""Every float32 product over a long dimension is made of three float32r ones: an operand a is
cut into hi = float32r(a), its upper 12 bits, and lo = a - hi, the rest, and a*b = hi*hi + hi*lo +
lo*hi up to 2**-24."""


class Chain:

    def __init__(self, engine, semaphore):
        self.engine, self.semaphore, self.count = engine, semaphore, 0

    def __call__(self, instruction):
        self.count += 1
        instruction.then_inc(self.semaphore, 1)
        self.engine.wait_ge(self.semaphore, self.count)


class Constants:

    def __init__(self, nc, enter):
        def sb(name, shape, dtype=F32):
            return enter(nc.sbuf_tensor(name, shape, dtype))

        self.identity = sb("identity", [P, P])
        self.identity_bf = sb("identity_bf", [P, P], BF16)
        self.earlier = sb("earlier", [P, P], BF16)
        self.ones = sb("ones", [P, P], BF16)
        self.lane = sb("lane", [P, P])
        self.slot_tile = sb("slot_tile", [P, LC])
        self.rank = sb("rank", [P, E])
        self.first_tile = sb("first_tile", [P, E])
        self.token1 = sb("token1", [P, K, T])
        self.not_first = sb("not_first", [P, E, T])
        self.hide_later = sb("hide_later", [P, P], BF16)
        self.hide_later_t = sb("hide_later_t", [P, P], BF16)

    def build(self, nc):
        with ExitStack() as stack:
            enter = stack.enter_context
            filled = enter(nc.semaphore("filled"))
            block = enter(nc.Block())

            @block.gpsimd
            def _(pool):
                for table, value in ((self.identity, 0.0), (self.identity_bf, 0.0), (self.earlier, 1.0),
                                     (self.ones, 1.0), (self.not_first, 1.0), (self.hide_later, 0.0),
                                     (self.hide_later_t, 0.0)):
                    pool.memset(table[:], value).then_inc(filled, 1)
                small = dict(allow_small_or_imprecise_dtypes=True)
                pool.iota(self.lane[:], [[1, P]], base=0, channel_multiplier=0, **small)
                pool.iota(self.slot_tile[:], [[1, LC]], base=0, channel_multiplier=0, **small)
                pool.iota(self.rank[:], [[-1, E]], base=E, channel_multiplier=0, **small)
                pool.iota(self.first_tile[:], [[ST, E]], base=0, channel_multiplier=0, **small)
                pool.iota(self.token1[:], [[0, K], [P, T]], base=1, channel_multiplier=1, **small)
                pool.wait_ge(filled, 7)
                for table in (self.identity, self.identity_bf):
                    pool.affine_select(table[:], table[:], [[-1, P]], ALU.not_equal, 1.0, base=0, channel_multiplier=1)
                pool.affine_select(self.earlier[:], self.earlier[:], [[1, P]], ALU.is_gt, 0.0, base=0, channel_multiplier=-1)
                pool.affine_select(self.not_first[:], self.not_first[:], [[0, E], [1, T]], ALU.is_gt, 0.0, base=0,
                                   channel_multiplier=0)
                pool.affine_select(self.hide_later[:], self.hide_later[:], [[-1, P]], ALU.is_ge, NEG, base=0,
                                   channel_multiplier=1)
                pool.affine_select(self.hide_later_t[:], self.hide_later_t[:], [[1, P]], ALU.is_ge, NEG, base=0,
                                   channel_multiplier=-1)


class Norm:

    def __init__(self, nc, enter, enter_semaphore, tag, x, xn):
        self.x, self.xn = x, xn
        self.stats = enter(nc.sbuf_tensor(f"{tag}_stats", [P, T, 6], F32))
        self.moments = enter(nc.sbuf_tensor(f"{tag}_moments", [P, T, 2], F32))
        self.variance = enter(nc.sbuf_tensor(f"{tag}_variance", [P, T], F32))
        self.root = enter(nc.sbuf_tensor(f"{tag}_root", [P, T], F32))
        self.inverse = enter(nc.sbuf_tensor(f"{tag}_inverse", [P, T], F32))
        self.scratch = enter(nc.sbuf_tensor(f"{tag}_scratch", [P, T], F32))
        self.has_variance = enter_semaphore(nc.semaphore(f"{tag}_has_variance"))
        self.has_root = enter_semaphore(nc.semaphore(f"{tag}_has_root"))

    def vector(self, v, chain, x_loaded, chunk, normed):
        for t in range(T):
            if t % chunk == 0:
                v.wait_ge(x_loaded[t // chunk], 16)
            last = v.bn_stats(self.stats[:, t, :], self.x[:, t, :])
        chain(last)
        for t in range(T):
            last = v.bn_aggr(self.moments[:, t, :], self.stats[:, t, :])
        chain(last)
        chain(v.tensor_scalar_add(self.variance[:], self.moments[:, :, 1], EPS))
        v.sem_inc(self.has_variance, 1)
        v.wait_ge(self.has_root, 1)
        chain(v.reciprocal(self.inverse[:], self.root[:]))
        chain(v.tensor_tensor(self.scratch[:], self.inverse[:], self.inverse[:], ALU.mult))
        chain(v.tensor_tensor(self.scratch[:], self.scratch[:], self.variance[:], ALU.mult))
        chain(v.tensor_scalar(self.scratch[:], self.scratch[:], -0.5, 1.5, ALU.mult, ALU.add))
        chain(v.tensor_tensor(self.inverse[:], self.inverse[:], self.scratch[:], ALU.mult))
        for t in range(T):
            v.tensor_scalar(self.xn[:, t, :], self.x[:, t, :], self.moments[:, t, 0:1], self.inverse[:, t:t + 1],
                            ALU.subtract, ALU.mult).then_inc(normed, 1)

    def scalar(self, s):
        s.wait_ge(self.has_variance, 1)
        s.activation(self.root[:], self.variance[:], ACT.Sqrt).then_inc(self.has_root, 1)


def row_tiles(rows, first, count):
    return rows[first * P:(first + count) * P, :].rearrange("(t p) c -> p t c", p=P)


def feed_forward(nc, const, tag, x_rows, sum_rows, xn_rows, Wg, w1, w2, copy_x):
    with ExitStack() as stack:
        enter = stack.enter_context

        def sb(name, shape, dtype=F32, enter=enter):
            return enter(nc.sbuf_tensor(f"{tag}_{name}", shape, dtype))

        def sem(name):
            return enter(nc.semaphore(f"{tag}_{name}"))

        gather_index = sb("gather_index", [P, LC], I32)
        add_index = sb("add_index", [P, LC], I32)
        gate = sb("gate", [P, LC])
        gather_now = [sb(f"gather_now{i}", [P, ST], I32) for i in range(2)]
        add_now = [sb(f"add_now{i}", [P, ST], I32) for i in range(2)]
        gate_now = [sb(f"gate_now{i}", [P, ST]) for i in range(2)]
        w1_raw = sb("w1_raw", [P, DK, FF])
        w2_raw = sb("w2_raw", [P, FT, D])
        w1_hi = [sb("w1_hi0", [P, DK, FF], F32R)]
        w1_lo = [sb("w1_lo0", [P, DK, FF], F32R)]
        w2_hi = [sb("w2_hi0", [P, FT, D], F32R)]
        w2_lo = [sb("w2_lo0", [P, FT, D], F32R)]
        xg = [sb(f"xg{i}", [P, ST, D]) for i in range(2)]
        xt_hi = sb("xt_hi", [P, DK, CAP], F32R)
        xt_lo = sb("xt_lo", [P, DK, CAP], F32R)
        scaled = [sb(f"scaled{i}", [P, ST, D]) for i in range(2)]

        with ExitStack() as early:
            def eb(name, shape, dtype=F32):
                return sb(name, shape, dtype, early.enter_context)

            x = eb("x", [P, T, D])
            xn = eb("xn", [P, T, D])
            xn_t = eb("xn_t", [P, DK, TOK])
            norm = Norm(nc, early.enter_context, enter, tag, x, xn)
            wg = eb("wg", [P, DK, 32])
            logits_t = eb("logits_t", [P, SEQ])
            logits = eb("logits", [P, T, E])
            others = eb("others", [P, T, E])
            top = eb("top", [P, K, T])
            equal = eb("equal", [P, T, E])
            best = eb("best", [P, T])
            chosen = eb("chosen", [P, K, T, E])
            exp_in = eb("exp_in", [P, (E + 1) * T])
            exp_out = eb("exp_out", [P, (E + 1) * T])
            gates = eb("gates", [P, K, T])
            taken = eb("taken", [P, E, T])
            taken_bf = eb("taken_bf", [P, E, T], BF16)
            running = eb("running", [P, E * T])
            before_bf = eb("before_bf", [P, E, T], BF16)
            product = eb("product", [P, K, T, E])
            position = eb("position", [P, K * T])
            column = eb("column", [P, K * T])
            tile_no = eb("tile_no", [P, K * T])
            in_tile = eb("in_tile", [P, K * T])
            of_tile = eb("of_tile", [P, K * T, LC])
            values = eb("values", [P, K * T * 2 * LC + P])
            of_lane = eb("of_lane", [P, K * T, P])
        h_hi = sb("h_hi", [P, FT, CAP], F32R)
        h_lo = sb("h_lo", [P, FT, CAP], F32R)
        w1_hi.append(sb("w1_hi1", [P, DK, FF], F32R))
        w1_lo.append(sb("w1_lo1", [P, DK, FF], F32R))
        w2_hi.append(sb("w2_hi1", [P, FT, D], F32R))
        w2_lo.append(sb("w2_lo1", [P, FT, D], F32R))

        ps_h = enter(nc.psum_tensor(f"{tag}_ps_h", [P, 2, 2, 512], F32))
        ps_o = enter(nc.psum_tensor(f"{tag}_ps_o", [P, 2, 512], F32))
        ps_x = enter(nc.psum_tensor(f"{tag}_ps_x", [P, 2, 512], F32))

        XB = [(0, 2), (2, 2), (4, 1)]
        CHUNK = 4
        x_loaded = [sem(f"x_loaded{c}") for c in range(T // CHUNK)]
        wg_loaded, x_copied = sem("wg_loaded"), sem("x_copied")
        normed, stored = sem("normed"), sem("stored")
        xn_turned, xn_t_ready = sem("xn_turned"), sem("xn_t_ready")
        wg_clear = sem("wg_clear")
        logits_t_made, logits_t_kept, logits_made = sem("logits_t_made"), sem("logits_t_kept"), sem("logits_made")
        exp_asked, exp_done = sem("exp_asked"), sem("exp_done")
        taken_ready, positions_made = sem("taken_ready"), sem("positions_made")
        lane_ready, list_made, list_kept = sem("lane_ready"), sem("list_made"), sem("list_kept")
        chained = sem("chained")

        raw_loaded, w_hi_done, w_split = sem("raw_loaded"), sem("w_hi_done"), sem("w_split")
        staged, gathered, x_turned = sem("staged"), [sem("gathered0"), sem("gathered1")], sem("x_turned")
        x_hi_done, x_split = sem("x_hi_done"), sem("x_split")
        h_made, h_hi_done, h_split = sem("h_made"), sem("h_hi_done"), sem("h_split")
        o_made, o_scaled = sem("o_made"), sem("o_scaled")
        added, listed, turn = sem("added"), sem("listed"), sem("turn")

        block = enter(nc.Block())

        def expert_loop(engine, pair):
            with engine.Fori(0, E // 2 - 1) as i:
                pair(i, False)
            pair(E // 2 - 1, True)

        @block.sync
        def _(sp):
            for c in range(T // CHUNK):
                sp.dma_start(x[:, c * CHUNK:(c + 1) * CHUNK, :], row_tiles(x_rows, c * CHUNK, CHUNK)).then_inc(x_loaded[c], 16)
            sp.wait_ge(wg_clear, 1)
            sp.dma_start(wg[:, :, 0:E], Wg.rearrange("(k p) e -> p k e", p=P)).then_inc(wg_loaded, 16)

            def load_expert(e):
                sp.dma_start(w1_raw[:], w1[e].rearrange("(k p) f -> p k f", p=P)).then_inc(raw_loaded, 16)
                sp.dma_start(w2_raw[:], w2[e].rearrange("(f p) c -> p f c", p=P)).then_inc(raw_loaded, 16)

            load_expert(0)
            if copy_x:
                sp.dma_start(sum_rows, x_rows).then_inc(x_copied, 16)
            for c in range(T // CHUNK):
                sp.wait_ge(normed, (c + 1) * CHUNK)
                sp.dma_start(row_tiles(xn_rows, c * CHUNK, CHUNK), xn[:, c * CHUNK:(c + 1) * CHUNK, :]).then_inc(stored, 16)
            with sp.Fori(1, E) as e:
                sp.wait_ge(w_split, e)
                sp.dma_start(w1_raw[:], w1[bass.ds(e, 1)].rearrange("o (k p) f -> p (o k) f", p=P)).then_inc(raw_loaded, 16)
                sp.dma_start(w2_raw[:], w2[bass.ds(e, 1)].rearrange("o (f p) c -> p (o f) c", p=P)).then_inc(raw_loaded, 16)

        @block.gpsimd
        def _(pool):
            pool.memset(wg[:], 0.0).then_inc(wg_clear, 1)
            pool.wait_ge(list_kept, 1)
            pool.wait_ge(stored, 16 * (T // CHUNK))
            if copy_x:
                pool.wait_ge(x_copied, 16)
            last_row = pool.to_reg(TOK - 1)

            def gather(e, par):
                pool.tensor_copy(gather_now[par][:], gather_index[:, bass.ds(e * ST, ST)]).then_inc(staged, 1)
                pool.wait_ge(staged, e + 1)
                pool.sem_inc(turn, 1)
                for s in range(ST):
                    pool.indirect_dma_start(xg[par][:, s, :], None, xn_rows,
                                            bass.IndirectOffsetOnAxis(ap=gather_now[par][:, s:s + 1], axis=0)
                                            ).then_inc(gathered[par], 16)

            def add_out(e, par):
                for s in range(ST):
                    if s > 0:
                        pool.wait_ge(added, 16 * (ST * e + s))
                        pool.sem_inc(turn, 1)
                    pool.wait_ge(o_scaled, ST * e + s + 3)
                    pool.sem_inc(turn, 1)
                    pool.indirect_dma_start(sum_rows, bass.IndirectOffsetOnAxis(ap=add_now[par][:, s:s + 1], axis=0),
                                            scaled[par][:, s, :], None, bounds_check=last_row, oob_is_err=False,
                                            compute_op=ALU.add).then_inc(added, 16)

            def expert(e, par, last, first=False):
                if not last:
                    pool.wait_ge(x_turned, len(XB) * (e + 1))
                    pool.sem_inc(turn, 1)
                    gather(e + 2, par)
                if not first:
                    pool.wait_ge(added, 16 * ST * e)
                    pool.sem_inc(turn, 1)
                pool.tensor_copy(add_now[par][:], add_index[:, bass.ds(e * ST, ST)])
                pool.tensor_copy(gate_now[par][:], gate[:, bass.ds(e * ST, ST)]).then_inc(listed, 1)
                pool.wait_ge(listed, e + 1)
                pool.sem_inc(turn, 1)
                add_out(e, par)

            gather(0, 0)
            gather(1, 1)
            expert(0, 0, False, first=True)
            expert(1, 1, False)
            with pool.Fori(1, E // 2 - 1) as i:
                expert(2 * i, 0, False)
                expert(2 * i + 1, 1, False)
            expert(E - 2, 0, True)
            expert(E - 1, 1, True)
            pool.wait_ge(added, 16 * LC)

        @block.scalar
        def _(act):
            norm.scalar(act)
            for n in range(DK * BATCH):
                act.wait_ge(xn_turned, n + 1)
                g, k = n // DK, n % DK
                act.activation(xn_t[:, k, g * SEQ:(g + 1) * SEQ], ps_h[:, n // 2 % 2, n % 2, :], ACT.Copy).then_inc(xn_t_ready, 1)
            act.wait_ge(logits_t_made, 1)
            act.activation(logits_t[:], ps_o[:, 0, :], ACT.Copy).then_inc(logits_t_kept, 1)
            act.wait_ge(exp_asked, 1)
            act.activation(exp_out[:], exp_in[:], ACT.Exp).then_inc(exp_done, 1)

            def split_x(e, par, b):
                s, n = XB[b]
                act.wait_ge(x_turned, len(XB) * e + b + 1)
                act.activation(xt_hi[:, :, s * P:(s + n) * P],
                               ps_x[:, (par + b) % 2, :].rearrange("p (k c) -> p k c", k=DK)[:, :, 0:n * P],
                               ACT.Copy).then_inc(x_hi_done, 1)

            def split_w1(e, par):
                act.wait_ge(raw_loaded, 32 * (e + 1))
                act.activation(w1_hi[par][:], w1_raw[:], ACT.Copy).then_inc(w_hi_done, 1)

            def split_w2(e, par):
                act.activation(w2_hi[par][:], w2_raw[:], ACT.Copy).then_inc(w_hi_done, 1)

            def scale(e, par, s):
                act.wait_ge(o_made, ST * e + s + 1)
                act.activation(scaled[par][:, s, :], ps_o[:, (par + s) % 2, 0:D], ACT.Copy,
                               scale=gate_now[par][:, s:s + 1]).then_inc(o_scaled, 1)

            def expert(e, par, last):
                for f in range(FT):
                    act.wait_ge(h_made, FT * e + f + 1)
                    act.activation(h_hi[:, f, :].rearrange("p (a c) -> p a c", a=2), ps_h[:, f % 2, :, 0:HALF],
                                   ACT.Relu).then_inc(h_hi_done, 1)
                if not last:
                    split_x(e + 1, 1 - par, 0)
                    split_x(e + 1, 1 - par, 1)
                    split_w1(e + 1, 1 - par)
                act.wait_ge(listed, e + 1)
                scale(e, par, 0)
                if not last:
                    split_x(e + 1, 1 - par, 2)
                    split_w2(e + 1, 1 - par)
                for s in range(1, ST):
                    scale(e, par, s)

            act.wait_ge(staged, 1)
            act.sem_inc(o_scaled, 2)
            split_w1(0, 0)
            split_w2(0, 0)
            for b in range(len(XB)):
                split_x(0, 0, b)

            def pair(i, last):
                expert(2 * i, 0, False)
                expert(2 * i + 1, 1, last)

            expert_loop(act, pair)

        @block.vector
        def _(v):
            chain = Chain(v, chained)
            norm.vector(v, chain, x_loaded, CHUNK, normed)

            v.wait_ge(logits_made, 1)
            chain(v.tensor_copy(logits[:].rearrange("p (g j) e -> p g j e", g=BATCH),
                                ps_o[:, 1, :].rearrange("p (j g s) -> p g j s", j=SEQ // P, g=BATCH)[:, :, :, 0:E]))
            scores = logits
            for k in range(K):
                chain(v.reduce_max(top[:, k, :], scores[:], AX_X))
                chain(v.tensor_tensor(equal[:], scores[:], top[:, k, :].unsqueeze(2).broadcast_to([P, T, E]), ALU.is_equal))
                chain(v.tensor_tensor(equal[:], equal[:], const.rank[:].unsqueeze(1).broadcast_to([P, T, E]), ALU.mult))
                chain(v.reduce_max(best[:], equal[:], AX_X))
                chain(v.tensor_tensor(chosen[:, k], equal[:], best[:].unsqueeze(2).broadcast_to([P, T, E]), ALU.is_equal))
                if k == 0:
                    chain(v.scalar_tensor_tensor(others[:], chosen[:, 0], NEG, logits[:], ALU.mult, ALU.add))
                    scores = others
            v.tensor_tensor(exp_in[:, 0:T * E].rearrange("p (t e) -> p t e", e=E), logits[:],
                            top[:, 0, :].unsqueeze(2).broadcast_to([P, T, E]), ALU.subtract)
            v.tensor_tensor(exp_in[:, T * E:], top[:, 1, :], top[:, 0, :], ALU.subtract).then_inc(exp_asked, 1)
            chain(v.tensor_tensor(taken[:].rearrange("p e t -> p t e"), chosen[:, 0], chosen[:, 1], ALU.add))
            chain(v.tensor_copy(taken_bf[:], taken[:]))
            chain(v.tensor_tensor_scan(running[:], const.not_first[:].rearrange("p e t -> p (e t)"),
                                       taken[:].rearrange("p e t -> p (e t)"), 0.0, ALU.mult, ALU.add))
            v.tensor_tensor(before_bf[:].rearrange("p e t -> p (e t)"), running[:],
                            taken[:].rearrange("p e t -> p (e t)"), ALU.subtract).then_inc(taken_ready, 1)
            v.wait_ge(exp_done, 1)
            chain(v.reduce_sum(best[:], exp_out[:, 0:T * E].rearrange("p (t e) -> p t e", e=E), AX_X))
            chain(v.reciprocal(best[:], best[:]))
            chain(v.tensor_scalar_mul(gates[:, 0, :], best[:], 0.5))
            chain(v.tensor_tensor(gates[:, 1, :], gates[:, 0, :], exp_out[:, T * E:], ALU.mult))
            v.wait_ge(positions_made, 1)
            chain(v.tensor_copy(running[:], ps_x[:, 0, 0:E * T]))
            ranks = running[:].rearrange("p (e t) -> p t e", e=E)
            for k in range(K):
                chain(v.tensor_tensor(product[:, k], chosen[:, k], ranks, ALU.mult))
            chain(v.reduce_sum(position[:], product[:].rearrange("p k t e -> p (k t) e"), AX_X))
            for k in range(K):
                chain(v.tensor_tensor(product[:, k], chosen[:, k], const.first_tile[:].unsqueeze(1).broadcast_to([P, T, E]), ALU.mult))
            chain(v.reduce_sum(column[:], product[:].rearrange("p k t e -> p (k t) e"), AX_X))
            chain(v.tensor_scalar(tile_no[:], position[:], float(P), None, ALU.is_ge))
            for a in range(2, ST):
                chain(v.scalar_tensor_tensor(tile_no[:], position[:], float(a * P), tile_no[:], ALU.is_ge, ALU.add))
            chain(v.scalar_tensor_tensor(in_tile[:], tile_no[:], -float(P), position[:], ALU.mult, ALU.add))
            chain(v.tensor_tensor(column[:], column[:], tile_no[:], ALU.add))
            chain(v.tensor_scalar(position[:], position[:], float(CAP), float(2 * LC), ALU.is_ge, ALU.mult))
            chain(v.tensor_tensor(column[:], column[:], position[:], ALU.add))
            pairs = [P, K * T, LC]
            chain(v.tensor_tensor(of_tile[:], const.slot_tile[:].unsqueeze(1).broadcast_to(pairs),
                                  column[:].unsqueeze(2).broadcast_to(pairs), ALU.is_equal))
            by_pair = values[:, 0:K * T * 2 * LC].rearrange("p (n two c) -> p n two c", n=K * T, two=2)
            v.memset(values[:, K * T * 2 * LC:], 0.0)
            v.tensor_tensor(by_pair[:, :, 0, :], of_tile[:],
                            const.token1[:].rearrange("p k t -> p (k t)").unsqueeze(2).broadcast_to(pairs), ALU.mult)
            v.tensor_tensor(by_pair[:, :, 1, :], of_tile[:],
                            gates[:].rearrange("p k t -> p (k t)").unsqueeze(2).broadcast_to(pairs), ALU.mult)
            for n in range(K * T):
                v.tensor_scalar(of_lane[:, n, :], const.lane[:], in_tile[:, n:n + 1], None, ALU.is_equal).then_inc(lane_ready, 1)
            by_slot = of_tile[:, 0, :]
            v.wait_ge(list_made, 1)
            chain(v.tensor_scalar(by_slot, ps_x[:, 1, 0:LC], -1.0, 0.0, ALU.add, ALU.max))
            chain(v.tensor_copy(gather_index[:], by_slot))
            chain(v.tensor_scalar(by_slot, ps_x[:, 1, 0:LC], 0.5, float(FAR), ALU.is_lt, ALU.mult))
            chain(v.tensor_tensor(by_slot, by_slot, ps_x[:, 1, 0:LC], ALU.add))
            chain(v.tensor_scalar_add(by_slot, by_slot, -1.0))
            chain(v.tensor_copy(add_index[:], by_slot))
            v.tensor_copy(gate[:], ps_x[:, 1, LC:2 * LC]).then_inc(list_kept, 1)

            def split_x(e, par, b):
                s, n = XB[b]
                v.wait_ge(x_hi_done, len(XB) * e + b + 1)
                v.tensor_tensor(xt_lo[:, :, s * P:(s + n) * P],
                                ps_x[:, (par + b) % 2, :].rearrange("p (k c) -> p k c", k=DK)[:, :, 0:n * P],
                                xt_hi[:, :, s * P:(s + n) * P].bitcast(F32), ALU.subtract).then_inc(x_split, 1)

            def split_w1(e, par):
                v.wait_ge(w_hi_done, 2 * e + 1)
                v.tensor_tensor(w1_lo[par][:], w1_raw[:], w1_hi[par][:].bitcast(F32), ALU.subtract)

            def split_w2(e, par):
                v.wait_ge(w_hi_done, 2 * e + 2)
                v.tensor_tensor(w2_lo[par][:], w2_raw[:], w2_hi[par][:].bitcast(F32), ALU.subtract).then_inc(w_split, 1)

            v.sem_inc(h_split, 2)
            v.sem_inc(x_split, 2)
            split_w1(0, 0)
            split_w2(0, 0)
            for b in range(len(XB)):
                split_x(0, 0, b)

            def expert(e, par, last):
                for f in range(FT):
                    v.wait_ge(h_hi_done, FT * e + f + 1)
                    v.scalar_tensor_tensor(h_lo[:, f, :].rearrange("p (a c) -> p a c", a=2), ps_h[:, f % 2, :, 0:HALF], 0.0,
                                           h_hi[:, f, :].rearrange("p (a c) -> p a c", a=2).bitcast(F32),
                                           ALU.max, ALU.subtract).then_inc(h_split, 1)
                if not last:
                    split_x(e + 1, 1 - par, 0)
                    split_x(e + 1, 1 - par, 1)
                    split_w1(e + 1, 1 - par)
                    split_x(e + 1, 1 - par, 2)
                    split_w2(e + 1, 1 - par)

            def pair(i, last):
                expert(2 * i, 0, False)
                expert(2 * i + 1, 1, last)

            expert_loop(v, pair)

        @block.tensor
        def _(pe):
            for n in range(DK * BATCH):
                g, k = n // DK, n % DK
                pe.wait_ge(normed, (SEQ // P) * (g + 1))
                if n >= 4:
                    pe.wait_ge(xn_t_ready, n - 3)
                for j in range(SEQ // P):
                    last = pe.transpose(ps_h[:, n // 2 % 2, n % 2, j * P:(j + 1) * P],
                                        xn[:, g * (SEQ // P) + j, k * P:(k + 1) * P], const.identity[:])
                last.then_inc(xn_turned, 1)
            pe.wait_ge(wg_loaded, 16)
            pe.wait_ge(xn_t_ready, DK * BATCH)
            for k in range(DK):
                for g in range(BATCH):
                    last = pe.matmul(ps_o[32 * g:32 * g + 32, 0, :], wg[:, k, :], xn_t[:, k, g * SEQ:(g + 1) * SEQ],
                                     start=(k == 0), stop=(k == DK - 1), skip_group_check=True)
            last.then_inc(logits_t_made, 1)
            pe.wait_ge(logits_t_kept, 1)
            for j in range(SEQ // P):
                last = pe.transpose(ps_o[:, 1, j * P:(j + 1) * P], logits_t[:, j * P:(j + 1) * P], const.identity[:])
            last.then_inc(logits_made, 1)
            pe.wait_ge(taken_ready, 1)
            pe.matmul(ps_x[:, 0, 0:E * T], const.earlier[:], taken_bf[:].rearrange("p e t -> p (e t)"), start=True, stop=False)
            pe.matmul(ps_x[:, 0, 0:E * T], const.ones[:], before_bf[:].rearrange("p e t -> p (e t)"),
                      start=False, stop=True).then_inc(positions_made, 1)
            for n in range(K * T):
                pe.wait_ge(lane_ready, n + 1)
                last = pe.matmul(ps_x[:, 1, 0:P], of_lane[:, n, :], values[:, n * 2 * LC:n * 2 * LC + P],
                                 start=(n == 0), stop=(n == K * T - 1))
            last.then_inc(list_made, 1)

            def turn_x(i, par, batches):
                e = 2 * i + par
                pe.wait_ge(gathered[par], 16 * ST * (i + 1))
                for b in batches:
                    s0, n = XB[b]
                    pe.wait_ge(x_split, len(XB) * e + b + 1)
                    for k in range(DK):
                        for s in range(n):
                            at = k * 2 * P + s * P
                            last = pe.transpose(ps_x[:, (par + b) % 2, at:at + P],
                                                xg[par][:, s0 + s, k * P:(k + 1) * P], const.identity[:])
                    last.then_inc(x_turned, 1)

            def expert(i, par, last_one):
                e = 2 * i + par
                pe.wait_ge(w_split, e + 1)
                pe.wait_ge(x_split, len(XB) * (e + 1) + 2)
                for f in range(FT):
                    pe.wait_ge(h_split, FT * e + f + 1)
                    fs = slice(f * P, (f + 1) * P)
                    for a in range(2):
                        cs = slice(a * HALF, (a + 1) * HALF)
                        parts = [(w1_hi[par][:, k, fs], xt_hi[:, k, cs]) for k in range(DK)]
                        parts += [(w1_hi[par][:, k, fs], xt_lo[:, k, cs]) for k in range(DK)]
                        parts += [(w1_lo[par][:, k, fs], xt_hi[:, k, cs]) for k in range(DK)]
                        for n, (w, m) in enumerate(parts):
                            last = pe.matmul(ps_h[:, f % 2, a, 0:HALF], w, m, start=(n == 0), stop=(n == len(parts) - 1))
                    last.then_inc(h_made, 1)
                if not last_one:
                    turn_x(i + par, 1 - par, (0, 1))
                for s in range(ST):
                    pe.wait_ge(o_scaled, ST * e + s + 1)
                    cs = slice(s * P, (s + 1) * P)
                    for f in range(FT):
                        if s == 0:
                            pe.wait_ge(h_split, FT * e + f + 3)
                        for n, (h, w) in enumerate(((h_hi, w2_hi), (h_hi, w2_lo), (h_lo, w2_hi))):
                            last = pe.matmul(ps_o[:, (par + s) % 2, 0:D], h[:, f, cs], w[par][:, f, :],
                                             start=(f == 0 and n == 0), stop=(f == FT - 1 and n == 2))
                    last.then_inc(o_made, 1)
                    if s == 0 and not last_one:
                        turn_x(i + par, 1 - par, (2,))

            turn_x(0, 0, range(len(XB)))

            def pair(i, last):
                expert(i, 0, False)
                expert(i, 1, last)

            expert_loop(pe, pair)


def attention(nc, const, x_rows, out_rows, xt_rows, w_qkv, w_o):
    HEADS, HD, STACK = 16, 16, 64
    UNIT_HEADS = HEADS // 2
    PAIRS = UNIT_HEADS // 2
    QT = SEQ // P
    GROUP = 4
    CHUNK = 4
    MAX_ROW = 3 * HD
    KEY_TILES = [(kt, min(kt * P, SEQ - 2 * P)) for kt in range(QT)]
    WIDTH = sum(SEQ - q0 for _, q0 in KEY_TILES)
    WIDE = (SEQ - KEY_TILES[0][1]) + (SEQ - KEY_TILES[1][1])
    QKV = [0, 1, 4, 7]
    TURN = [2, 5, 8, 10]
    MAXIMA = 12
    SCORES = [(qt, (h, h + 1)) for qt in (0, 1) for h in range(0, UNIT_HEADS, 2)]
    SCORES += [(qt, (h,)) for qt in (2, 3) for h in range(UNIT_HEADS)]
    TURN_MAX = MAXIMA + len(SCORES)
    USES = TURN_MAX + 1
    assert USES % 2 == 1
    SLICES = [((0, 1), (), 0, 0), ((2,), (0,), 0, 0), ((3,), (1,), 0, 0), ((), (2, 3), 0, 3), ((), (), 3, 8),
              ((), (), 8, 13), ((), (), 13, 18), ((), (), 18, len(SCORES))]
    TAIL_USES = 8
    PV_AFTER = (5, UNIT_HEADS - 1)

    with ExitStack() as stack:
        enter = stack.enter_context

        def sb(name, shape, dtype=F32, enter=enter):
            return enter(nc.sbuf_tensor(f"at_{name}", shape, dtype))

        def sem(name):
            return enter(nc.semaphore(f"at_{name}"))

        w_hi = sb("w_hi", [P, 16, P], F32R)
        w_lo = sb("w_lo", [P, 16, P], F32R)
        xt = sb("xt", [P, 2, DK, SEQ], F32R)
        with ExitStack() as early:
            def eb(name, shape, dtype=F32):
                return sb(name, shape, dtype, early.enter_context)

            x = eb("x", [P, T, D])
            xn = eb("xn", [P, T, D])
            norm = Norm(nc, early.enter_context, enter, "at", x, xn)
            w_raw = eb("w_raw", [P, 8, D])
            xt_all = [eb("xt_hi_all", [P, DK, TOK], F32R), eb("xt_lo_all", [P, DK, TOK], F32R)]
        row_stack = [sb(f"row_stack{i}", [P, 2, UNIT_HEADS, STACK]) for i in range(2)]
        q_stack = [sb(f"q_stack{i}", [P, PAIRS, SEQ], F32R) for i in range(2)]
        k_stack = [sb(f"k_stack{i}", [P, 2, PAIRS, SEQ], F32R) for i in range(2)]
        v_ones = [sb(f"v_ones{i}", [P, QT, UNIT_HEADS, 32]) for i in range(2)]
        maxima = sb("maxima", [P, QT, 2, PAIRS])
        minus_max = sb("minus_max", [P, QT, 2, 2, PAIRS])
        max_t = sb("max_t", [4 * PAIRS, SEQ])
        probs = [sb(f"probs{i}", [P, GROUP, WIDTH]) for i in range(2)]
        o_t = [sb(f"o_t{i}", [P, SEQ]) for i in range(2)]
        inverse = sb("inverse_sum", [P, QT, GROUP])
        heads_out = sb("heads_out", [P, QT, D])
        heads_t_hi = sb("heads_t_hi", [P, DK, SEQ], F32R)
        heads_t_lo = sb("heads_t_lo", [P, DK, SEQ], F32R)
        x_now = sb("x_now", [P, QT, D])
        x_out = sb("x_out", [P, QT, D])
        hide_256 = sb("hide_256", [P, 2 * P], BF16)

        ps_keys = enter(nc.psum_tensor("at_ps_keys", [P, 3 * 512], F32))
        ps_pv = enter(nc.psum_tensor("at_ps_pv", [P, 512], F32))
        ps_4 = enter(nc.psum_tensor("at_ps_4", [P, 4, 512], F32))

        def front_bank(hh, use):
            return ps_4[:, (hh + use) % 2, :]

        def tail_bank(use):
            return ps_4[:, 2 + use % 2, :]

        def early_part(n, part):
            if n < 4:
                return (w_hi, w_lo)[part][:, 4 * n:4 * n + 4, :].rearrange("p a c -> p (a c)")
            g, k = (n - 4) // DK, n % DK
            return xt_all[part][:, k, g * SEQ:(g + 1) * SEQ]

        def keys_columns(half):
            return ps_keys[:, 0:WIDE] if half == 0 else ps_keys[:, 1024:1024 + WIDTH - WIDE]

        x_loaded = [sem(f"x_loaded{c}") for c in range(T // CHUNK)]
        w_loaded, normed, early_made, early_hi, early_kept, xt_stored = (
            sem("w_loaded"), sem("normed"), sem("early_made"), sem("early_hi"), sem("early_kept"), sem("xt_stored"))
        set_up, filled = sem("set_up"), sem("filled")
        chained = sem("chained")
        xt_loaded, x_now_loaded, x_stored = sem("xt_loaded"), sem("x_now_loaded"), sem("x_stored")
        front_made, front_kept = sem("front_made"), sem("front_kept")
        hi_done, stacked, evac_done = sem("hi_done"), sem("stacked"), sem("evac_done")
        minus_hi, minus_ready, max_t_ready, max_in = sem("minus_hi"), sem("minus_ready"), sem("max_t_ready"), sem("max_in")
        keys_made, exped, pv_made, o_t_kept = sem("keys_made"), sem("exped"), sem("pv_made"), sem("o_t_kept")
        tail_made, tail_kept, inverse_done, heads_hi, out_ready = (
            sem("tail_made"), sem("tail_kept"), sem("inverse_done"), sem("heads_hi"), sem("out_ready"))
        turn_taken = sem("turn_taken")
        block = enter(nc.Block())

        def unit_loop(engine, front, step):
            front(0, 0)
            with engine.Fori(0, BATCH - 1) as b:
                step(b, 0, b, 1)
                step(b, 1, b + 1, 0)
            step(BATCH - 1, 0, BATCH - 1, 1)
            step(BATCH - 1, 1, None, None)

        @block.sync
        def _(sp):
            for c in range(T // CHUNK):
                sp.dma_start(x[:, c * CHUNK:(c + 1) * CHUNK, :], row_tiles(x_rows, c * CHUNK, CHUNK)).then_inc(x_loaded[c], 16)
            sp.dma_start(w_raw[:, 0:6, :], w_qkv.rearrange("(i p) c -> p i c", p=P)).then_inc(w_loaded, 16)
            sp.dma_start(w_raw[:, 6:8, :], w_o.rearrange("(i p) c -> p i c", p=P)).then_inc(w_loaded, 16)
            sp.wait_ge(early_kept, 12)
            for part in range(2):
                sp.dma_start(xt_rows[part], xt_all[part][:].bitcast(F32)).then_inc(xt_stored, 16)
            sp.wait_ge(xt_stored, 32)

            def load_xt(b):
                sp.dma_start(xt[:, 0].bitcast(F32), xt_rows[0, :, :, bass.ds(b * SEQ, SEQ)]).then_inc(xt_loaded, 16)
                sp.dma_start(xt[:, 1].bitcast(F32), xt_rows[1, :, :, bass.ds(b * SEQ, SEQ)]).then_inc(xt_loaded, 16)

            def rows_of(table, b):
                return table[bass.ds(b * SEQ, SEQ), :].rearrange("(t p) c -> p t c", p=P)

            def insert_max(b, hh):
                sp.wait_ge(max_t_ready, 2 * b + hh + 1)
                for odd in range(2):
                    for c in range(2):
                        row = odd * STACK + MAX_ROW + c
                        sp.dma_start(q_stack[hh][row:row + 1, :, :].bitcast(F32),
                                     max_t[(2 * odd + c) * PAIRS:(2 * odd + c + 1) * PAIRS, :]).then_inc(max_in, 16)

            def front(b, hh):
                if hh == 0:
                    load_xt(b)
                    sp.dma_start(x_now[:], rows_of(x_rows, b)).then_inc(x_now_loaded, 16)
                insert_max(b, hh)

            def step(b, hh, next_b, next_hh):
                if next_b is not None and hh == 0:
                    insert_max(next_b, next_hh)
                    if not isinstance(b, int):
                        load_xt(b + 1)
                if hh == 1:
                    if next_b is not None:
                        insert_max(next_b, next_hh)
                    sp.wait_ge(out_ready, b + 1)
                    sp.dma_start(rows_of(out_rows, b), x_out[:]).then_inc(x_stored, 16)
                    if next_b is not None:
                        sp.dma_start(x_now[:], rows_of(x_rows, b + 1)).then_inc(x_now_loaded, 16)

            sp.sem_inc(x_stored, 16)
            sp.sem_inc(max_in, 64)
            unit_loop(sp, front, step)
            sp.wait_ge(x_stored, 16 * (BATCH + 1))

        @block.gpsimd
        def _(pool):
            pool.wait_ge(xt_stored, 32)
            for i in range(2):
                pool.memset(row_stack[i][:], 0.0).then_inc(filled, 1)
                pool.memset(k_stack[i][:].rearrange("p a b c -> p (a b c)").bitcast(F32), 0.0)
                pool.memset(v_ones[i][:], 0.0).then_inc(filled, 1)
            pool.memset(hide_256[:], 0.0).then_inc(filled, 1)
            pool.wait_ge(filled, 5)
            for i in range(2):
                pool.memset(row_stack[i][:, 1, :, MAX_ROW:MAX_ROW + 2], 1.0)
                pool.memset(v_ones[i][:, :, :, HD:HD + 1], 1.0)
            pool.affine_select(hide_256[:], hide_256[:], [[1, 2 * P]], ALU.is_ge, NEG, base=-P,
                               channel_multiplier=-1).then_inc(set_up, 1)

            def front(b, hh):
                for t in range(QT):
                    stack_of = row_stack[t % 2]
                    pool.wait_ge(hi_done, QT * (2 * b + hh) + t + 1)
                    pool.sem_inc(turn_taken, 1)
                    pool.tensor_copy(stack_of[:, 0, :, HD:2 * HD], stack_of[:, 0, :, 0:HD])
                    pool.tensor_copy(stack_of[:, 1, :, 2 * HD:3 * HD], stack_of[:, 1, :, 0:HD]).then_inc(stacked, 1)

            def step(b, hh, next_b, next_hh):
                if next_b is not None:
                    front(next_b, next_hh)

            unit_loop(pool, front, step)

        @block.scalar
        def _(act):
            norm.scalar(act)
            for n in range(12):
                act.wait_ge(early_made, n + 1)
                act.activation(early_part(n, 0), ps_4[:, n % 4, :], ACT.Copy).then_inc(early_hi, 1)
            act.wait_ge(set_up, 1)

            def project(u, hh, t):
                act.wait_ge(front_made, USES * u + QKV[t] + 1)
                bank = front_bank(hh, QKV[t])
                act.activation(v_ones[hh][:, t, :, 0:HD], bank[:, 2 * P:3 * P].rearrange("p (h c) -> p h c", c=HD), ACT.Copy)
                act.activation(row_stack[t % 2][:, :, :, 0:HD].rearrange("p a h c -> p (a h) c").bitcast(F32R),
                               bank[:, 0:2 * P].rearrange("p (h c) -> p h c", c=HD), ACT.Copy).then_inc(hi_done, 1)

            def turn(u, hh, t):
                at = slice(t * P, (t + 1) * P)
                act.wait_ge(front_made, USES * u + TURN[t] + 1)
                act.activation(q_stack[hh][:, 0:2, at], front_bank(hh, TURN[t]).rearrange("p (a c) -> p a c", c=P)[:, 0:2, :],
                               ACT.Copy).then_inc(evac_done, 1)
                act.wait_ge(front_made, USES * u + TURN[t] + 2)
                act.activation(k_stack[hh][0:STACK, 0, :, at],
                               front_bank(hh, TURN[t] + 1)[0:STACK, :].rearrange("p (a c) -> p a c", c=P),
                               ACT.Copy).then_inc(evac_done, 1)

            def front_slice(b, hh, j):
                if b is not None:
                    projected, turned, _, _ = SLICES[j]
                    for t in turned:
                        turn(2 * b + hh, hh, t)
                    for t in projected:
                        project(2 * b + hh, hh, t)

            def exps(b, hh, h):
                into = probs[h // GROUP]
                for half, (lo, hi) in enumerate(((0, WIDE), (WIDE, WIDTH))):
                    act.wait_ge(keys_made, 2 * UNIT_HEADS * (2 * b + hh) + 2 * h + half + 1)
                    act.activation(into[:, h % GROUP, lo:hi], keys_columns(half), ACT.Exp, scale=float(HD) ** -0.5).then_inc(exped, 1)

            def keep_o_t(b, hh, g):
                act.wait_ge(pv_made, 2 * (2 * b + hh) + g + 1)
                act.activation(o_t[g][:], ps_pv[:], ACT.Copy).then_inc(o_t_kept, 1)

            def front(b, hh):
                for j in range(len(SLICES)):
                    front_slice(b, hh, j)

            def step(b, hh, next_b, next_hh):
                for h in range(UNIT_HEADS):
                    exps(b, hh, h)
                    front_slice(next_b, next_hh, h)
                    if h == PV_AFTER[0]:
                        keep_o_t(b, hh, 0)
                keep_o_t(b, hh, 1)
                if hh == 1:
                    for k in range(DK):
                        act.wait_ge(tail_made, TAIL_USES * b + 5 + k)
                        act.activation(heads_t_hi[:, k, :], tail_bank(4 + k), ACT.Copy).then_inc(heads_hi, 1)

            act.sem_inc(exped, 2)
            act.sem_inc(o_t_kept, 1)
            unit_loop(act, front, step)



        @block.vector
        def _(v):
            chain = Chain(v, chained)
            norm.vector(v, chain, x_loaded, CHUNK, normed)
            for n in range(12):
                v.wait_ge(early_hi, n + 1)
                v.tensor_tensor(early_part(n, 1), ps_4[:, n % 4, :], early_part(n, 0).bitcast(F32), ALU.subtract).then_inc(early_kept, 1)
            v.sem_inc(front_kept, 2)
            v.sem_inc(tail_kept, 2)
            v.wait_ge(set_up, 1)

            def project(u, hh, t):
                bank = front_bank(hh, QKV[t])
                stack_of = row_stack[t % 2]
                v.wait_ge(hi_done, QT * u + t + 1)
                v.tensor_tensor(stack_of[:, 0, :, 2 * HD:3 * HD], bank[:, 0:P].rearrange("p (h c) -> p h c", c=HD),
                                stack_of[:, 0, :, 0:HD], ALU.subtract)
                v.tensor_tensor(stack_of[:, 1, :, HD:2 * HD], bank[:, P:2 * P].rearrange("p (h c) -> p h c", c=HD),
                                stack_of[:, 1, :, 0:HD], ALU.subtract).then_inc(front_kept, 1)

            def turn(u, hh, t):
                at = slice(t * P, (t + 1) * P)
                v.wait_ge(evac_done, 2 * (QT * u + t) + 1)
                v.tensor_copy(q_stack[hh][:, 2:4, at],
                              front_bank(hh, TURN[t]).rearrange("p (a c) -> p a c", c=P)[:, 2:4, :]).then_inc(front_kept, 1)
                v.wait_ge(evac_done, 2 * (QT * u + t) + 2)
                v.tensor_copy(k_stack[hh][STACK:P, 1, :, at],
                              front_bank(hh, TURN[t] + 1)[STACK:P, :].rearrange("p (a c) -> p a c", c=P)).then_inc(front_kept, 1)

            def maximum(u, hh, n):
                qt, heads = SCORES[n]
                bank = front_bank(hh, MAXIMA + n)
                v.wait_ge(front_made, USES * u + MAXIMA + n + 1)
                if len(heads) == 2:
                    v.reduce_max(maxima[:, qt, :, heads[0] // 2],
                                 bank.rearrange("p (a c) -> p a c", a=2)[:, :, 0:(qt + 1) * P], AX_X).then_inc(front_kept, 1)
                else:
                    h = heads[0]
                    v.reduce_max(maxima[:, qt, h % 2, h // 2:h // 2 + 1], bank[:, 0:(qt + 1) * P], AX_X).then_inc(front_kept, 1)

            def negate(u, hh):
                most = maxima[:].rearrange("p q o a -> p (q o) a")
                hi = minus_max[:, :, :, 0, :].rearrange("p q o a -> p (q o) a")
                lo = minus_max[:, :, :, 1, :].rearrange("p q o a -> p (q o) a")
                v.wait_ge(front_kept, USES * u + TURN_MAX + 2)
                v.tensor_scalar_mul(hi.bitcast(F32R), most, -1.0).then_inc(minus_hi, 1)
                v.wait_ge(minus_hi, u + 1)
                v.scalar_tensor_tensor(lo, most, -1.0, hi, ALU.mult, ALU.subtract).then_inc(minus_ready, 1)
                v.wait_ge(max_in, 64 * (u + 1))
                v.wait_ge(front_made, USES * u + TURN_MAX + 1)
                v.tensor_copy(max_t[:], front_bank(hh, TURN_MAX)[0:4 * PAIRS, :]).then_inc(front_kept, 1)
                v.wait_ge(front_kept, USES * u + TURN_MAX + 3)
                v.sem_inc(max_t_ready, 1)

            def front_slice(b, hh, j):
                if b is not None:
                    u = 2 * b + hh
                    projected, turned, first, end = SLICES[j]
                    for t in turned:
                        turn(u, hh, t)
                    for t in projected:
                        project(u, hh, t)
                    for n in range(first, end):
                        maximum(u, hh, n)
                    if j == len(SLICES) - 1:
                        negate(u, hh)

            def divide(b, hh, g):
                use = 2 * hh + g
                v.wait_ge(tail_made, TAIL_USES * b + use + 1)
                v.wait_ge(tail_kept, TAIL_USES * b + use + 2)
                by_head = tail_bank(use).rearrange("p (q h c) -> p q h c", q=QT, h=GROUP)
                v.reciprocal(inverse[:], by_head[:, :, :, HD]).then_inc(inverse_done, 1)
                v.wait_ge(inverse_done, 2 * (2 * b + hh) + g + 1)
                columns = heads_out[:, :, (2 * hh + g) * GROUP * HD:(2 * hh + g + 1) * GROUP * HD]
                v.tensor_tensor(columns.rearrange("p q (h c) -> p q h c", h=GROUP), by_head[:, :, :, 0:HD],
                                inverse[:].unsqueeze(3).broadcast_to([P, QT, GROUP, HD]), ALU.mult).then_inc(tail_kept, 1)

            def front(b, hh):
                for j in range(len(SLICES)):
                    front_slice(b, hh, j)

            def step(b, hh, next_b, next_hh):
                for h in range(UNIT_HEADS):
                    front_slice(next_b, next_hh, h)
                    if h == PV_AFTER[0]:
                        divide(b, hh, 0)
                divide(b, hh, 1)
                if hh == 1:
                    for k in range(DK):
                        v.wait_ge(heads_hi, DK * b + k + 1)
                        v.tensor_tensor(heads_t_lo[:, k, :], tail_bank(4 + k), heads_t_hi[:, k, :].bitcast(F32),
                                        ALU.subtract).then_inc(tail_kept, 1)
                    v.wait_ge(x_now_loaded, 16 * (b + 1))
                    v.wait_ge(x_stored, 16 * (b + 1))
                    for n in range(2):
                        v.wait_ge(tail_made, TAIL_USES * b + 7 + n)
                        v.tensor_tensor(x_out[:, 2 * n:2 * n + 2, :].rearrange("p q c -> p (q c)"), tail_bank(6 + n),
                                        x_now[:, 2 * n:2 * n + 2, :].rearrange("p q c -> p (q c)"), ALU.add).then_inc(tail_kept, 1)
                    v.wait_ge(tail_kept, TAIL_USES * (b + 1) + 2)
                    v.sem_inc(out_ready, 1)

            unit_loop(v, front, step)

        @block.tensor
        def _(pe):
            pe.wait_ge(w_loaded, 32)
            for n in range(12):
                if n >= 4:
                    pe.wait_ge(early_kept, n - 3)
                    g, k = (n - 4) // DK, n % DK
                    pe.wait_ge(normed, QT * (g + 1))
                for j in range(4):
                    if n < 3:
                        k, half, which = (4 * n + j) // 6, (4 * n + j) // 3 % 2, (4 * n + j) % 3
                        block_in = w_raw[:, 2 * which + half, k * P:(k + 1) * P]
                    elif n == 3:
                        block_in = w_raw[:, 6 + j % 2, j // 2 * P:(j // 2 + 1) * P]
                    else:
                        block_in = xn[:, g * QT + j, k * P:(k + 1) * P]
                    last = pe.transpose(ps_4[:, n % 4, j * P:(j + 1) * P], block_in, const.identity[:])
                last.then_inc(early_made, 1)
            pe.wait_ge(set_up, 1)

            def three(out, hi_hi, hi_lo, lo_hi, first=True, end=True):
                for n, (w, m) in enumerate((hi_hi, hi_lo, lo_hi)):
                    last = pe.matmul(out, w, m, start=(first and n == 0), stop=(end and n == 2))
                return last

            def use(u, k):
                pe.wait_ge(front_kept, USES * u + k + 1)

            def project(u, hh, t):
                use(u, QKV[t])
                out = front_bank(hh, QKV[t])[:, 0:3 * P]
                at = slice(t * P, (t + 1) * P)
                for k in range(DK):
                    tiles = slice((2 * k + hh) * 3, (2 * k + hh + 1) * 3)
                    hi, lo = (w[:, tiles, :].rearrange("p a c -> p (a c)") for w in (w_hi, w_lo))
                    last = three(out, (xt[:, 0, k, at], hi), (xt[:, 0, k, at], lo), (xt[:, 1, k, at], hi),
                                 first=(k == 0), end=(k == DK - 1))
                last.then_inc(front_made, 1)

            def turn(u, hh, t):
                pe.wait_ge(stacked, QT * u + t + 1)
                pe.wait_ge(front_kept, USES * u + QKV[t] + 3)
                for part in range(2):
                    use(u, TURN[t] + part)
                    for a in range(PAIRS):
                        last = pe.transpose(front_bank(hh, TURN[t] + part)[:, a * P:(a + 1) * P],
                                            row_stack[t % 2][:, part, 2 * a:2 * a + 2, :].rearrange("p h c -> p (h c)"),
                                            const.identity[:])
                    last.then_inc(front_made, 1)

            def scores(u, hh, n):
                qt, heads = SCORES[n]
                if n == 0:
                    pe.wait_ge(front_kept, USES * u + MAXIMA + 2)
                use(u, MAXIMA + n)
                keys = max(2 * P, (qt + 1) * P)
                for i, h in enumerate(heads):
                    out = front_bank(hh, MAXIMA + n)[:, i * keys:(i + 1) * keys]
                    pe.matmul(out, q_stack[hh][:, h // 2, qt * P:(qt + 1) * P], k_stack[hh][:, h % 2, h // 2, 0:keys],
                              start=True, stop=False)
                    last = pe.matmul(out[:, qt * P:(qt + 1) * P], const.identity_bf[:], const.hide_later[:], start=False, stop=True)
                last.then_inc(front_made, 1)

            def turn_max(u, hh):
                use(u, TURN_MAX)
                pe.wait_ge(minus_ready, u + 1)
                for qt in range(QT):
                    last = pe.transpose(front_bank(hh, TURN_MAX)[0:4 * PAIRS, qt * P:(qt + 1) * P],
                                        minus_max[:, qt].rearrange("p o c a -> p (o c a)"), const.identity[:])
                last.then_inc(front_made, 1)

            def front_slice(b, hh, j):
                if b is not None:
                    u = 2 * b + hh
                    projected, turned, first, end = SLICES[j]
                    if j == 0 and hh == 0:
                        pe.wait_ge(xt_loaded, 32 * (b + 1))
                    for t in turned:
                        turn(u, hh, t)
                    for t in projected:
                        project(u, hh, t)
                    for n in range(first, end):
                        scores(u, hh, n)
                    if j == len(SLICES) - 1:
                        turn_max(u, hh)

            def key_scores(b, hh, h):
                u = 2 * b + hh
                q, k = q_stack[hh][:, h // 2, :], k_stack[hh][:, h % 2, h // 2, :]
                for half in range(2):
                    pe.wait_ge(exped, 2 * UNIT_HEADS * u + 2 * h + half + 1)
                    for i, (kt, q0) in enumerate(KEY_TILES[2 * half:2 * half + 2]):
                        at = 512 * i if half == 0 else 1024 + 256 * i
                        hidden = const.hide_later_t if q0 == kt * P else hide_256
                        out = ps_keys[:, at:at + SEQ - q0]
                        pe.matmul(out, k[:, kt * P:(kt + 1) * P], q[:, q0:SEQ], start=True, stop=False)
                        last = pe.matmul(out[:, 0:hidden.shape[1]], const.identity_bf[:], hidden[:], start=False, stop=True)
                    last.then_inc(keys_made, 1)

            def values(b, hh, g):
                u = 2 * b + hh
                pe.wait_ge(exped, 2 * UNIT_HEADS * u + 2 * GROUP * (g + 1) + 2)
                pe.wait_ge(o_t_kept, 2 * u + g + 1)
                at = 0
                for kt, q0 in KEY_TILES:
                    skip = kt * P - q0
                    for j in range(GROUP):
                        last = pe.matmul(ps_pv[32 * j:32 * j + 32, kt * P:SEQ], v_ones[hh][:, kt, g * GROUP + j, :],
                                         probs[g][:, j, at + skip:at + SEQ - q0], start=(kt == 0), stop=(kt == QT - 1),
                                         skip_group_check=True)
                    at += SEQ - q0
                last.then_inc(pv_made, 1)

            def turn_o(b, hh, g):
                k = 2 * hh + g
                pe.wait_ge(o_t_kept, 2 * (2 * b + hh) + g + 2)
                pe.wait_ge(tail_kept, TAIL_USES * b + k + 1)
                for qt in range(QT):
                    last = pe.transpose(tail_bank(k)[:, qt * P:(qt + 1) * P], o_t[g][:, qt * P:(qt + 1) * P], const.identity[:])
                last.then_inc(tail_made, 1)

            def project_out(b):
                pe.wait_ge(tail_kept, TAIL_USES * b + 6)
                for k in range(DK):
                    for qt in range(QT):
                        last = pe.transpose(tail_bank(4 + k)[:, qt * P:(qt + 1) * P], heads_out[:, qt, k * P:(k + 1) * P],
                                            const.identity[:])
                    last.then_inc(tail_made, 1)
                for n in range(2):
                    pe.wait_ge(tail_kept, TAIL_USES * b + 8)
                    for i in range(2):
                        at = slice((2 * n + i) * P, (2 * n + i + 1) * P)
                        for k in range(DK):
                            hi, lo = (w[:, 12 + 2 * k:14 + 2 * k, :].rearrange("p a c -> p (a c)") for w in (w_hi, w_lo))
                            last = three(tail_bank(6 + n)[:, i * D:(i + 1) * D], (heads_t_hi[:, k, at], hi),
                                         (heads_t_hi[:, k, at], lo), (heads_t_lo[:, k, at], hi), first=(k == 0), end=(k == DK - 1))
                    last.then_inc(tail_made, 1)

            def front(b, hh):
                for j in range(len(SLICES)):
                    front_slice(b, hh, j)

            def step(b, hh, next_b, next_hh):
                pe.wait_ge(max_in, 64 * (2 * b + hh + 2))
                for h in range(UNIT_HEADS):
                    key_scores(b, hh, h)
                    front_slice(next_b, next_hh, h)
                    if h == PV_AFTER[0]:
                        values(b, hh, 0)
                        turn_o(b, hh, 0)
                values(b, hh, 1)
                turn_o(b, hh, 1)
                if hh == 1:
                    project_out(b)

            unit_loop(pe, front, step)



def macaron_kernel(nc, hidden, w_qkv, w_o, Wg, w1, w2, out):
    x_rows = hidden.rearrange("b s c -> (b s) c")
    out_rows = out.rearrange("b s c -> (b s) c")
    after_first = nc.dram_tensor("after_first", (TOK, D), F32, kind="Internal").ap()
    normed_rows = nc.dram_tensor("normed_rows", (TOK, D), F32, kind="Internal").ap()
    transposed_rows = nc.dram_tensor("transposed_rows", (2, P, DK, TOK), F32, kind="Internal").ap()
    with ExitStack() as stack:
        const = Constants(nc, stack.enter_context)
        const.build(nc)
        feed_forward(nc, const, "first", x_rows, after_first, normed_rows, Wg, w1, w2, True)
        attention(nc, const, after_first, out_rows, transposed_rows, w_qkv, w_o)
        feed_forward(nc, const, "second", out_rows, out_rows, normed_rows, Wg, w1, w2, False)


_INS = ["L0_attn_hidden_states", "L0_attn_w_qkv", "L0_attn_w_o", "L0_ffn_Wg", "L0_ffn_w1", "L0_ffn_w2"]
_OUT = ((BATCH, SEQ, D), "float32")


def kernel(**inputs):
    import numpy as _np
    import concourse.bacc as _bacc
    from concourse import mybir as _mybir
    from concourse.bass_utils import run_bass_kernel_spmd as _run

    nc = _bacc.Bacc("TRN2", target_bir_lowering=False, num_devices=1)
    arrays, args = {}, []
    for name in _INS:
        a = _np.ascontiguousarray(inputs[name])
        arrays[f"in_{name}_dram"] = a
        args.append(nc.dram_tensor(f"in_{name}_dram", a.shape, _mybir.dt.from_np(a.dtype), kind="ExternalInput").ap())
    shape, dtype = _OUT
    args.append(nc.dram_tensor("out_0_dram", shape, _mybir.dt.from_np(_np.dtype(dtype)), kind="ExternalOutput").ap())
    macaron_kernel(nc, *args)
    r = _run(nc, [arrays], core_ids=[0])
    return r.results[0]["out_0_dram"]
```

```python
from contextlib import ExitStack

import concourse.bass as bass
from concourse import mybir

F32 = mybir.dt.float32
F32R = mybir.dt.float32r
BF16 = mybir.dt.bfloat16
I32 = mybir.dt.int32
ALU = mybir.AluOpType
ACT = mybir.ActivationFunctionType
AX_X = mybir.AxisListType.X

P = 128
BATCH, SEQ, D = 4, 512, 256
TOK = BATCH * SEQ
T = TOK // P
DK = D // P
FF = 1024
FT = FF // P
E, K = 8, 2
CAP = -(-5 * TOK * K // (4 * E))
ST = CAP // P
LC = E * ST
HALF = CAP // 2
EPS = 1e-5
FAR = 4096
NEG = -3.0e38
"""Every float32 product over a long dimension is made of three float32r ones: an operand a is
cut into hi = float32r(a), its upper 12 bits, and lo = a - hi, the rest, and a*b = hi*hi + hi*lo +
lo*hi up to 2**-24."""


class Chain:

    def __init__(self, engine, semaphore):
        self.engine, self.semaphore, self.count = engine, semaphore, 0

    def __call__(self, instruction):
        self.count += 1
        instruction.then_inc(self.semaphore, 1)
        self.engine.wait_ge(self.semaphore, self.count)


class Constants:

    def __init__(self, nc, enter):
        def sb(name, shape, dtype=F32):
            return enter(nc.sbuf_tensor(name, shape, dtype))

        self.identity = sb("identity", [P, P])
        self.identity_bf = sb("identity_bf", [P, P], BF16)
        self.earlier = sb("earlier", [P, P], BF16)
        self.ones = sb("ones", [P, P], BF16)
        self.lane = sb("lane", [P, P])
        self.slot_tile = sb("slot_tile", [P, LC])
        self.rank = sb("rank", [P, E])
        self.first_tile = sb("first_tile", [P, E])
        self.token1 = sb("token1", [P, K, T])
        self.not_first = sb("not_first", [P, E, T])
        self.hide_later = sb("hide_later", [P, P], BF16)
        self.hide_later_t = sb("hide_later_t", [P, P], BF16)

    def build(self, nc):
        with ExitStack() as stack:
            enter = stack.enter_context
            filled = enter(nc.semaphore("filled"))
            block = enter(nc.Block())

            @block.gpsimd
            def _(pool):
                for table, value in ((self.identity, 0.0), (self.identity_bf, 0.0), (self.earlier, 1.0),
                                     (self.ones, 1.0), (self.not_first, 1.0), (self.hide_later, 0.0),
                                     (self.hide_later_t, 0.0)):
                    pool.memset(table[:], value).then_inc(filled, 1)
                small = dict(allow_small_or_imprecise_dtypes=True)
                pool.iota(self.lane[:], [[1, P]], base=0, channel_multiplier=0, **small)
                pool.iota(self.slot_tile[:], [[1, LC]], base=0, channel_multiplier=0, **small)
                pool.iota(self.rank[:], [[-1, E]], base=E, channel_multiplier=0, **small)
                pool.iota(self.first_tile[:], [[ST, E]], base=0, channel_multiplier=0, **small)
                pool.iota(self.token1[:], [[0, K], [P, T]], base=1, channel_multiplier=1, **small)
                pool.wait_ge(filled, 7)
                for table in (self.identity, self.identity_bf):
                    pool.affine_select(table[:], table[:], [[-1, P]], ALU.not_equal, 1.0, base=0, channel_multiplier=1)
                pool.affine_select(self.earlier[:], self.earlier[:], [[1, P]], ALU.is_gt, 0.0, base=0, channel_multiplier=-1)
                pool.affine_select(self.not_first[:], self.not_first[:], [[0, E], [1, T]], ALU.is_gt, 0.0, base=0,
                                   channel_multiplier=0)
                pool.affine_select(self.hide_later[:], self.hide_later[:], [[-1, P]], ALU.is_ge, NEG, base=0,
                                   channel_multiplier=1)
                pool.affine_select(self.hide_later_t[:], self.hide_later_t[:], [[1, P]], ALU.is_ge, NEG, base=0,
                                   channel_multiplier=-1)


class Norm:

    def __init__(self, nc, enter, enter_semaphore, tag, x, xn):
        self.x, self.xn = x, xn
        self.rounds, self.roots = 0, 0
        self.stats = enter(nc.sbuf_tensor(f"{tag}_stats", [P, T, 6], F32))
        self.moments = enter(nc.sbuf_tensor(f"{tag}_moments", [P, T, 2], F32))
        self.variance = enter(nc.sbuf_tensor(f"{tag}_variance", [P, T], F32))
        self.root = enter(nc.sbuf_tensor(f"{tag}_root", [P, T], F32))
        self.inverse = enter(nc.sbuf_tensor(f"{tag}_inverse", [P, T], F32))
        self.scratch = enter(nc.sbuf_tensor(f"{tag}_scratch", [P, T], F32))
        self.has_variance = enter_semaphore(nc.semaphore(f"{tag}_has_variance"))
        self.has_root = enter_semaphore(nc.semaphore(f"{tag}_has_root"))

    def statistics(self, v, chain, loaded, first, count):
        tiles = slice(first, first + count)
        v.wait_ge(loaded, 16)
        for t in range(first, first + count):
            last = v.bn_stats(self.stats[:, t, :], self.x[:, t, :])
        chain(last)
        for t in range(first, first + count):
            last = v.bn_aggr(self.moments[:, t, :], self.stats[:, t, :])
        chain(last)
        v.tensor_scalar_add(self.variance[:, tiles], self.moments[:, tiles, 1], EPS).then_inc(self.has_variance, 1)

    def inverses(self, v, chain, first, count):
        tiles = slice(first, first + count)
        self.rounds += 1
        v.wait_ge(self.has_root, self.rounds)
        inverse, scratch = self.inverse[:, tiles], self.scratch[:, tiles]
        chain(v.reciprocal(inverse, self.root[:, tiles]))
        chain(v.tensor_tensor(scratch, inverse, inverse, ALU.mult))
        chain(v.tensor_tensor(scratch, scratch, self.variance[:, tiles], ALU.mult))
        chain(v.tensor_scalar(scratch, scratch, -0.5, 1.5, ALU.mult, ALU.add))
        chain(v.tensor_tensor(inverse, inverse, scratch, ALU.mult))

    def rows(self, v, first, count, normed):
        for t in range(first, first + count):
            v.tensor_scalar(self.xn[:, t, :], self.x[:, t, :], self.moments[:, t, 0:1], self.inverse[:, t:t + 1],
                            ALU.subtract, ALU.mult).then_inc(normed, 1)

    def scalar(self, s, first, count):
        self.roots += 1
        s.wait_ge(self.has_variance, self.roots)
        s.activation(self.root[:, first:first + count], self.variance[:, first:first + count], ACT.Sqrt).then_inc(self.has_root, 1)


def row_tiles(rows, first, count):
    return rows[first * P:(first + count) * P, :].rearrange("(t p) c -> p t c", p=P)


def feed_forward(nc, const, tag, x_rows, sum_rows, xn_rows, Wg, w1, w2, copy_x):
    with ExitStack() as stack:
        enter = stack.enter_context

        def sb(name, shape, dtype=F32, enter=enter):
            return enter(nc.sbuf_tensor(f"{tag}_{name}", shape, dtype))

        def sem(name):
            return enter(nc.semaphore(f"{tag}_{name}"))

        gather_index = sb("gather_index", [P, LC], I32)
        add_index = sb("add_index", [P, LC], I32)
        gate = sb("gate", [P, LC])
        gather_now = [sb(f"gather_now{i}", [P, ST], I32) for i in range(2)]
        add_now = [sb(f"add_now{i}", [P, ST], I32) for i in range(2)]
        gate_now = [sb(f"gate_now{i}", [P, ST]) for i in range(2)]
        w1_raw = sb("w1_raw", [P, DK, FF])
        w2_raw = sb("w2_raw", [P, FT, D])
        w1_hi = [sb("w1_hi0", [P, DK, FF], F32R)]
        w1_lo = [sb("w1_lo0", [P, DK, FF], F32R)]
        w2_hi = [sb("w2_hi0", [P, FT, D], F32R)]
        w2_lo = [sb("w2_lo0", [P, FT, D], F32R)]
        xg = [sb(f"xg{i}", [P, ST, D]) for i in range(2)]
        xt_hi = sb("xt_hi", [P, DK, CAP], F32R)
        xt_lo = sb("xt_lo", [P, DK, CAP], F32R)
        scaled = [sb(f"scaled{i}", [P, ST, D]) for i in range(2)]

        PARTS = 4
        PART = K * T // PARTS
        with ExitStack() as early:
            def eb(name, shape, dtype=F32):
                return sb(name, shape, dtype, early.enter_context)

            x = eb("x", [P, T, D])
            xn = eb("xn", [P, T, D])
            xn_t = eb("xn_t", [P, DK, TOK])
            norm = Norm(nc, early.enter_context, enter, tag, x, xn)
            wg = eb("wg", [P, DK, 32])
            logits_t = eb("logits_t", [P, SEQ])
            logits = eb("logits", [P, T, E])
            others = eb("others", [P, T, E])
            top = eb("top", [P, K, T])
            equal = eb("equal", [P, T, E])
            best = eb("best", [P, T])
            chosen = eb("chosen", [P, K, T, E])
            exp_in = eb("exp_in", [P, (E + 1) * T])
            exp_out = eb("exp_out", [P, (E + 1) * T])
            gates = eb("gates", [P, K, T])
            taken = eb("taken", [P, E, T])
            taken_bf = eb("taken_bf", [P, E, T], BF16)
            running = eb("running", [P, E * T])
            before_bf = eb("before_bf", [P, E, T], BF16)
            product = eb("product", [P, K, T, E])
            position = eb("position", [P, K * T])
            column = eb("column", [P, K * T])
            tile_no = eb("tile_no", [P, K * T])
            in_tile = eb("in_tile", [P, K * T])
            of_tile = eb("of_tile", [P, K * T, LC])
            values = eb("values", [P, PARTS, PART * 2 * LC + P - 2 * LC])
            of_lane = eb("of_lane", [P, K * T, P])
        h_hi = sb("h_hi", [P, FT, CAP], F32R)
        h_lo = sb("h_lo", [P, FT, CAP], F32R)
        w1_hi.append(sb("w1_hi1", [P, DK, FF], F32R))
        w1_lo.append(sb("w1_lo1", [P, DK, FF], F32R))
        w2_hi.append(sb("w2_hi1", [P, FT, D], F32R))
        w2_lo.append(sb("w2_lo1", [P, FT, D], F32R))

        ps_h = enter(nc.psum_tensor(f"{tag}_ps_h", [P, 2, 2, 512], F32))
        ps_o = enter(nc.psum_tensor(f"{tag}_ps_o", [P, 2, 512], F32))
        ps_x = enter(nc.psum_tensor(f"{tag}_ps_x", [P, 2, 512], F32))

        XB = [(0, 2), (2, 2), (4, 1)]
        CHUNK = SEQ // P
        x_loaded = [sem(f"x_loaded{c}") for c in range(T // CHUNK)]
        wg_loaded, x_copied = sem("wg_loaded"), sem("x_copied")
        normed, stored = [sem(f"normed{c}") for c in range(T // CHUNK)], sem("stored")
        xn_turned, xn_t_ready = sem("xn_turned"), sem("xn_t_ready")
        wg_clear, pads_clear = sem("wg_clear"), sem("pads_clear")
        logits_t_made, logits_t_kept, logits_made = sem("logits_t_made"), sem("logits_t_kept"), sem("logits_made")
        exp_asked, exp_done = sem("exp_asked"), sem("exp_done")
        taken_ready, positions_made = sem("taken_ready"), sem("positions_made")
        lane_ready, list_made, list_kept = sem("lane_ready"), sem("list_made"), sem("list_kept")
        chained = sem("chained")

        raw_loaded, w_hi_done, w_split = sem("raw_loaded"), sem("w_hi_done"), sem("w_split")
        staged, gathered, x_turned = sem("staged"), [[sem(f"gathered{i}_{b}") for b in range(3)] for i in range(2)], sem("x_turned")
        x_hi_done, x_split = sem("x_hi_done"), sem("x_split")
        h_made, h_hi_done, h_split = sem("h_made"), sem("h_hi_done"), sem("h_split")
        o_made, o_scaled = sem("o_made"), sem("o_scaled")
        added, listed, turn = sem("added"), sem("listed"), sem("turn")

        block = enter(nc.Block())

        def expert_loop(engine, pair):
            with engine.Fori(0, E // 2 - 1) as i:
                pair(i, False)
            pair(E // 2 - 1, True)

        @block.sync
        def _(sp):
            for c in range(T // CHUNK):
                sp.dma_start(x[:, c * CHUNK:(c + 1) * CHUNK, :], row_tiles(x_rows, c * CHUNK, CHUNK)).then_inc(x_loaded[c], 16)
            sp.wait_ge(wg_clear, 1)
            sp.dma_start(wg[:, :, 0:E], Wg.rearrange("(k p) e -> p k e", p=P)).then_inc(wg_loaded, 16)

            def load_expert(e):
                sp.dma_start(w1_raw[:], w1[e].rearrange("(k p) f -> p k f", p=P)).then_inc(raw_loaded, 16)
                sp.dma_start(w2_raw[:], w2[e].rearrange("(f p) c -> p f c", p=P)).then_inc(raw_loaded, 16)

            load_expert(0)
            if copy_x:
                sp.dma_start(sum_rows, x_rows).then_inc(x_copied, 16)
            for c in range(T // CHUNK):
                sp.wait_ge(normed[c], CHUNK)
                sp.dma_start(row_tiles(xn_rows, c * CHUNK, CHUNK), xn[:, c * CHUNK:(c + 1) * CHUNK, :]).then_inc(stored, 16)
            sp.wait_ge(x_turned, len(XB))
            with sp.Fori(1, E) as e:
                sp.wait_ge(w_split, e)
                sp.dma_start(w1_raw[:], w1[bass.ds(e, 1)].rearrange("o (k p) f -> p (o k) f", p=P)).then_inc(raw_loaded, 16)
                sp.dma_start(w2_raw[:], w2[bass.ds(e, 1)].rearrange("o (f p) c -> p (o f) c", p=P)).then_inc(raw_loaded, 16)

        @block.gpsimd
        def _(pool):
            pool.memset(wg[:], 0.0).then_inc(wg_clear, 1)
            pool.memset(values[:, :, PART * 2 * LC:], 0.0).then_inc(pads_clear, 1)
            pool.wait_ge(list_kept, 1)
            pool.wait_ge(stored, 16 * (T // CHUNK))
            if copy_x:
                pool.wait_ge(x_copied, 16)
            last_row = pool.to_reg(TOK - 1)

            def gather(e, par):
                pool.tensor_copy(gather_now[par][:], gather_index[:, bass.ds(e * ST, ST)]).then_inc(staged, 1)
                pool.wait_ge(staged, e + 1)
                pool.sem_inc(turn, 1)
                for b, (s0, n) in enumerate(XB):
                    for s in range(s0, s0 + n):
                        pool.indirect_dma_start(xg[par][:, s, :], None, xn_rows,
                                                bass.IndirectOffsetOnAxis(ap=gather_now[par][:, s:s + 1], axis=0)
                                                ).then_inc(gathered[par][b], 16)

            def add_out(e, par):
                for s in range(ST):
                    if s > 0:
                        pool.wait_ge(added, 16 * (ST * e + s))
                        pool.sem_inc(turn, 1)
                    pool.wait_ge(o_scaled, ST * e + s + 3)
                    pool.sem_inc(turn, 1)
                    pool.indirect_dma_start(sum_rows, bass.IndirectOffsetOnAxis(ap=add_now[par][:, s:s + 1], axis=0),
                                            scaled[par][:, s, :], None, bounds_check=last_row, oob_is_err=False,
                                            compute_op=ALU.add).then_inc(added, 16)

            def expert(e, par, last, first=False):
                if not last:
                    pool.wait_ge(x_turned, len(XB) * (e + 1))
                    pool.sem_inc(turn, 1)
                    gather(e + 2, par)
                if not first:
                    pool.wait_ge(added, 16 * ST * e)
                    pool.sem_inc(turn, 1)
                pool.tensor_copy(add_now[par][:], add_index[:, bass.ds(e * ST, ST)])
                pool.tensor_copy(gate_now[par][:], gate[:, bass.ds(e * ST, ST)]).then_inc(listed, 1)
                pool.wait_ge(listed, e + 1)
                pool.sem_inc(turn, 1)
                add_out(e, par)

            gather(0, 0)
            gather(1, 1)
            expert(0, 0, False, first=True)
            expert(1, 1, False)
            with pool.Fori(1, E // 2 - 1) as i:
                expert(2 * i, 0, False)
                expert(2 * i + 1, 1, False)
            expert(E - 2, 0, True)
            expert(E - 1, 1, True)
            pool.wait_ge(added, 16 * LC)

        @block.scalar
        def _(act):
            def split_w1(e, par):
                act.wait_ge(raw_loaded, 32 * (e + 1))
                act.activation(w1_hi[par][:], w1_raw[:], ACT.Copy).then_inc(w_hi_done, 1)

            def split_w2(e, par):
                act.activation(w2_hi[par][:], w2_raw[:], ACT.Copy).then_inc(w_hi_done, 1)

            norm.scalar(act, 0, CHUNK)
            for n in range(DK * BATCH):
                g, k = n // DK, n % DK
                if k == 0 and g + 1 < BATCH:
                    norm.scalar(act, (g + 1) * CHUNK, CHUNK)
                if n == DK:
                    split_w1(0, 0)
                if n == 2 * DK:
                    split_w2(0, 0)
                act.wait_ge(xn_turned, n + 1)
                act.activation(xn_t[:, k, g * SEQ:(g + 1) * SEQ], ps_h[:, n // 2 % 2, n % 2, :], ACT.Copy).then_inc(xn_t_ready, 1)
            act.wait_ge(logits_t_made, 1)
            act.activation(logits_t[:], ps_o[:, 0, :], ACT.Copy).then_inc(logits_t_kept, 1)
            act.wait_ge(exp_asked, 1)
            act.activation(exp_out[:], exp_in[:], ACT.Exp).then_inc(exp_done, 1)

            def split_x(e, par, b):
                s, n = XB[b]
                act.wait_ge(x_turned, len(XB) * e + b + 1)
                act.activation(xt_hi[:, :, s * P:(s + n) * P],
                               ps_x[:, (par + b) % 2, :].rearrange("p (k c) -> p k c", k=DK)[:, :, 0:n * P],
                               ACT.Copy).then_inc(x_hi_done, 1)

            def scale(e, par, s):
                act.wait_ge(o_made, ST * e + s + 1)
                act.activation(scaled[par][:, s, :], ps_o[:, (par + s) % 2, 0:D], ACT.Copy,
                               scale=gate_now[par][:, s:s + 1]).then_inc(o_scaled, 1)

            def expert(e, par, last):
                for n in range(2 * FT):
                    f, a = n // 2, n % 2
                    act.wait_ge(h_made, 2 * FT * e + n + 1)
                    act.activation(h_hi[:, f, a * HALF:(a + 1) * HALF], ps_h[:, f % 2, a, 0:HALF], ACT.Relu).then_inc(h_hi_done, 1)
                if not last:
                    split_x(e + 1, 1 - par, 0)
                    split_x(e + 1, 1 - par, 1)
                    split_w1(e + 1, 1 - par)
                act.wait_ge(listed, e + 1)
                scale(e, par, 0)
                if not last:
                    split_x(e + 1, 1 - par, 2)
                    split_w2(e + 1, 1 - par)
                for s in range(1, ST):
                    scale(e, par, s)

            act.wait_ge(staged, 1)
            act.sem_inc(o_scaled, 2)
            for b in range(len(XB)):
                split_x(0, 0, b)

            def pair(i, last):
                expert(2 * i, 0, False)
                expert(2 * i + 1, 1, last)

            expert_loop(act, pair)

        @block.vector
        def _(v):
            chain = Chain(v, chained)

            def split_w1(e, par):
                v.wait_ge(w_hi_done, 2 * e + 1)
                v.tensor_tensor(w1_lo[par][:], w1_raw[:], w1_hi[par][:].bitcast(F32), ALU.subtract)

            def split_w2(e, par):
                v.wait_ge(w_hi_done, 2 * e + 2)
                v.tensor_tensor(w2_lo[par][:], w2_raw[:], w2_hi[par][:].bitcast(F32), ALU.subtract).then_inc(w_split, 1)

            norm.statistics(v, chain, x_loaded[0], 0, CHUNK)
            for c in range(T // CHUNK):
                if c + 1 < T // CHUNK:
                    norm.statistics(v, chain, x_loaded[c + 1], (c + 1) * CHUNK, CHUNK)
                norm.inverses(v, chain, c * CHUNK, CHUNK)
                norm.rows(v, c * CHUNK, CHUNK, normed[c])
            split_w1(0, 0)

            v.wait_ge(logits_made, 1)
            chain(v.tensor_copy(logits[:].rearrange("p (g j) e -> p g j e", g=BATCH),
                                ps_o[:, 1, :].rearrange("p (j g s) -> p g j s", j=SEQ // P, g=BATCH)[:, :, :, 0:E]))
            scores = logits
            for k in range(K):
                chain(v.reduce_max(top[:, k, :], scores[:], AX_X))
                chain(v.tensor_tensor(equal[:], scores[:], top[:, k, :].unsqueeze(2).broadcast_to([P, T, E]), ALU.is_equal))
                chain(v.tensor_tensor(equal[:], equal[:], const.rank[:].unsqueeze(1).broadcast_to([P, T, E]), ALU.mult))
                chain(v.reduce_max(best[:], equal[:], AX_X))
                chain(v.tensor_tensor(chosen[:, k], equal[:], best[:].unsqueeze(2).broadcast_to([P, T, E]), ALU.is_equal))
                if k == 0:
                    chain(v.scalar_tensor_tensor(others[:], chosen[:, 0], NEG, logits[:], ALU.mult, ALU.add))
                    scores = others
            v.tensor_tensor(exp_in[:, 0:T * E].rearrange("p (t e) -> p t e", e=E), logits[:],
                            top[:, 0, :].unsqueeze(2).broadcast_to([P, T, E]), ALU.subtract)
            v.tensor_tensor(exp_in[:, T * E:], top[:, 1, :], top[:, 0, :], ALU.subtract).then_inc(exp_asked, 1)
            chain(v.tensor_tensor(taken[:].rearrange("p e t -> p t e"), chosen[:, 0], chosen[:, 1], ALU.add))
            chain(v.tensor_copy(taken_bf[:], taken[:]))
            chain(v.tensor_tensor_scan(running[:], const.not_first[:].rearrange("p e t -> p (e t)"),
                                       taken[:].rearrange("p e t -> p (e t)"), 0.0, ALU.mult, ALU.add))
            v.tensor_tensor(before_bf[:].rearrange("p e t -> p (e t)"), running[:],
                            taken[:].rearrange("p e t -> p (e t)"), ALU.subtract).then_inc(taken_ready, 1)
            v.wait_ge(exp_done, 1)
            chain(v.reduce_sum(best[:], exp_out[:, 0:T * E].rearrange("p (t e) -> p t e", e=E), AX_X))
            chain(v.reciprocal(best[:], best[:]))
            chain(v.tensor_scalar_mul(gates[:, 0, :], best[:], 0.5))
            chain(v.tensor_tensor(gates[:, 1, :], gates[:, 0, :], exp_out[:, T * E:], ALU.mult))
            v.wait_ge(positions_made, 1)
            chain(v.tensor_copy(running[:], ps_x[:, 0, 0:E * T]))
            ranks = running[:].rearrange("p (e t) -> p t e", e=E)
            for k in range(K):
                chain(v.tensor_tensor(product[:, k], chosen[:, k], ranks, ALU.mult))
            chain(v.reduce_sum(position[:], product[:].rearrange("p k t e -> p (k t) e"), AX_X))
            for k in range(K):
                chain(v.tensor_tensor(product[:, k], chosen[:, k], const.first_tile[:].unsqueeze(1).broadcast_to([P, T, E]), ALU.mult))
            chain(v.reduce_sum(column[:], product[:].rearrange("p k t e -> p (k t) e"), AX_X))
            chain(v.tensor_scalar(tile_no[:], position[:], float(P), None, ALU.is_ge))
            for a in range(2, ST):
                chain(v.scalar_tensor_tensor(tile_no[:], position[:], float(a * P), tile_no[:], ALU.is_ge, ALU.add))
            chain(v.scalar_tensor_tensor(in_tile[:], tile_no[:], -float(P), position[:], ALU.mult, ALU.add))
            chain(v.tensor_tensor(column[:], column[:], tile_no[:], ALU.add))
            chain(v.tensor_scalar(position[:], position[:], float(CAP), float(2 * LC), ALU.is_ge, ALU.mult))
            chain(v.tensor_tensor(column[:], column[:], position[:], ALU.add))
            pairs = [P, PART, LC]
            for h in range(PARTS):
                first = PART * h
                part = slice(first, first + PART)
                by_pair = values[:, h, 0:PART * 2 * LC].rearrange("p (n two c) -> p n two c", n=PART, two=2)
                chain(v.tensor_tensor(of_tile[:, part], const.slot_tile[:].unsqueeze(1).broadcast_to(pairs),
                                      column[:, part].unsqueeze(2).broadcast_to(pairs), ALU.is_equal))
                v.tensor_tensor(by_pair[:, :, 0, :], of_tile[:, part],
                                const.token1[:].rearrange("p k t -> p (k t)")[:, part].unsqueeze(2).broadcast_to(pairs), ALU.mult)
                v.tensor_tensor(by_pair[:, :, 1, :], of_tile[:, part],
                                gates[:].rearrange("p k t -> p (k t)")[:, part].unsqueeze(2).broadcast_to(pairs), ALU.mult)
                for n in range(first, first + PART):
                    v.tensor_scalar(of_lane[:, n, :], const.lane[:], in_tile[:, n:n + 1], None, ALU.is_equal).then_inc(lane_ready, 1)
            by_slot = of_tile[:, 0, :]
            v.wait_ge(list_made, 1)
            chain(v.tensor_scalar(by_slot, ps_x[:, 1, 0:LC], -1.0, 0.0, ALU.add, ALU.max))
            chain(v.tensor_copy(gather_index[:], by_slot))
            chain(v.tensor_scalar(by_slot, ps_x[:, 1, 0:LC], 0.5, float(FAR), ALU.is_lt, ALU.mult))
            chain(v.tensor_tensor(by_slot, by_slot, ps_x[:, 1, 0:LC], ALU.add))
            chain(v.tensor_scalar_add(by_slot, by_slot, -1.0))
            chain(v.tensor_copy(add_index[:], by_slot))
            v.tensor_copy(gate[:], ps_x[:, 1, LC:2 * LC]).then_inc(list_kept, 1)

            def split_x(e, par, b):
                s, n = XB[b]
                v.wait_ge(x_hi_done, len(XB) * e + b + 1)
                v.tensor_tensor(xt_lo[:, :, s * P:(s + n) * P],
                                ps_x[:, (par + b) % 2, :].rearrange("p (k c) -> p k c", k=DK)[:, :, 0:n * P],
                                xt_hi[:, :, s * P:(s + n) * P].bitcast(F32), ALU.subtract).then_inc(x_split, 1)

            v.sem_inc(h_split, 4)
            v.sem_inc(x_split, 2)
            split_w2(0, 0)
            for b in range(len(XB)):
                split_x(0, 0, b)

            def expert(e, par, last):
                for n in range(2 * FT):
                    f, a = n // 2, n % 2
                    v.wait_ge(h_hi_done, 2 * FT * e + n + 1)
                    v.scalar_tensor_tensor(h_lo[:, f, a * HALF:(a + 1) * HALF], ps_h[:, f % 2, a, 0:HALF], 0.0,
                                           h_hi[:, f, a * HALF:(a + 1) * HALF].bitcast(F32),
                                           ALU.max, ALU.subtract).then_inc(h_split, 1)
                if not last:
                    split_x(e + 1, 1 - par, 0)
                    split_x(e + 1, 1 - par, 1)
                    split_w1(e + 1, 1 - par)
                    split_x(e + 1, 1 - par, 2)
                    split_w2(e + 1, 1 - par)

            def pair(i, last):
                expert(2 * i, 0, False)
                expert(2 * i + 1, 1, last)

            expert_loop(v, pair)

        @block.tensor
        def _(pe):
            def group_logits(g):
                if g == 0:
                    pe.wait_ge(wg_loaded, 16)
                pe.wait_ge(xn_t_ready, DK * (g + 1))
                for k in range(DK):
                    last = pe.matmul(ps_o[32 * g:32 * g + 32, 0, :], wg[:, k, :], xn_t[:, k, g * SEQ:(g + 1) * SEQ],
                                     start=(k == 0), stop=(k == DK - 1), skip_group_check=True)
                return last

            for g in range(BATCH):
                pe.wait_ge(normed[g], CHUNK)
                for k in range(DK):
                    n = DK * g + k
                    if n >= 4:
                        pe.wait_ge(xn_t_ready, n - 3)
                    for j in range(SEQ // P):
                        last = pe.transpose(ps_h[:, n // 2 % 2, n % 2, j * P:(j + 1) * P],
                                            xn[:, g * (SEQ // P) + j, k * P:(k + 1) * P], const.identity[:])
                    last.then_inc(xn_turned, 1)
                if g > 0:
                    group_logits(g - 1)
            group_logits(BATCH - 1).then_inc(logits_t_made, 1)
            pe.wait_ge(logits_t_kept, 1)
            for j in range(SEQ // P):
                last = pe.transpose(ps_o[:, 1, j * P:(j + 1) * P], logits_t[:, j * P:(j + 1) * P], const.identity[:])
            last.then_inc(logits_made, 1)
            pe.wait_ge(taken_ready, 1)
            pe.matmul(ps_x[:, 0, 0:E * T], const.earlier[:], taken_bf[:].rearrange("p e t -> p (e t)"), start=True, stop=False)
            pe.matmul(ps_x[:, 0, 0:E * T], const.ones[:], before_bf[:].rearrange("p e t -> p (e t)"),
                      start=False, stop=True).then_inc(positions_made, 1)
            pe.wait_ge(pads_clear, 1)
            for n in range(K * T):
                pe.wait_ge(lane_ready, n + 1)
                last = pe.matmul(ps_x[:, 1, 0:P], of_lane[:, n, :], values[:, n // PART, n % PART * 2 * LC:n % PART * 2 * LC + P],
                                 start=(n == 0), stop=(n == K * T - 1))
            last.then_inc(list_made, 1)

            def turn_x(i, par, batches):
                e = 2 * i + par
                for b in batches:
                    s0, n = XB[b]
                    pe.wait_ge(gathered[par][b], 16 * n * (i + 1))
                    pe.wait_ge(x_split, len(XB) * e + b + 1)
                    for k in range(DK):
                        for s in range(n):
                            at = k * 2 * P + s * P
                            last = pe.transpose(ps_x[:, (par + b) % 2, at:at + P],
                                                xg[par][:, s0 + s, k * P:(k + 1) * P], const.identity[:])
                    last.then_inc(x_turned, 1)

            def expert(i, par, last_one):
                e = 2 * i + par
                pe.wait_ge(w_split, e + 1)
                pe.wait_ge(x_split, len(XB) * (e + 1) + 2)
                for f in range(FT):
                    pe.wait_ge(h_split, 2 * (FT * e + f + 1))
                    fs = slice(f * P, (f + 1) * P)
                    for a in range(2):
                        cs = slice(a * HALF, (a + 1) * HALF)
                        parts = [(w1_hi[par][:, k, fs], xt_hi[:, k, cs]) for k in range(DK)]
                        parts += [(w1_hi[par][:, k, fs], xt_lo[:, k, cs]) for k in range(DK)]
                        parts += [(w1_lo[par][:, k, fs], xt_hi[:, k, cs]) for k in range(DK)]
                        for n, (w, m) in enumerate(parts):
                            last = pe.matmul(ps_h[:, f % 2, a, 0:HALF], w, m, start=(n == 0), stop=(n == len(parts) - 1))
                        last.then_inc(h_made, 1)
                if not last_one:
                    turn_x(i + par, 1 - par, (0, 1))
                for s in range(ST):
                    pe.wait_ge(o_scaled, ST * e + s + 1)
                    cs = slice(s * P, (s + 1) * P)
                    for f in range(FT):
                        if s == 0:
                            pe.wait_ge(h_split, 2 * (FT * e + f + 3))
                        for n, (h, w) in enumerate(((h_hi, w2_hi), (h_hi, w2_lo), (h_lo, w2_hi))):
                            last = pe.matmul(ps_o[:, (par + s) % 2, 0:D], h[:, f, cs], w[par][:, f, :],
                                             start=(f == 0 and n == 0), stop=(f == FT - 1 and n == 2))
                    last.then_inc(o_made, 1)
                    if s == 0 and not last_one:
                        turn_x(i + par, 1 - par, (2,))

            turn_x(0, 0, range(len(XB)))

            def pair(i, last):
                expert(i, 0, False)
                expert(i, 1, last)

            expert_loop(pe, pair)


def attention(nc, const, x_rows, out_rows, w_qkv, w_o):
    HEADS, HD, STACK = 16, 16, 64
    UNIT_HEADS = HEADS // 2
    PAIRS = UNIT_HEADS // 2
    QT = SEQ // P
    GROUP = 4
    MAX_ROW = 3 * HD
    KEY_TILES = [(kt, min(kt * P, SEQ - 2 * P)) for kt in range(QT)]
    WIDTH = sum(SEQ - q0 for _, q0 in KEY_TILES)
    WIDE = (SEQ - KEY_TILES[0][1]) + (SEQ - KEY_TILES[1][1])
    SCORES = [(qt, (h, h + 1)) for qt in (0, 1) for h in range(0, UNIT_HEADS, 2)]
    SCORES += [(qt, (h,)) for qt in (2, 3) for h in range(UNIT_HEADS)]
    LEAD = [("project", 0), ("project", 1)]
    BESIDE = [[("turn", 0)], [("project", 2)], [("turn", 1)], [("project", 3), 0, 1], [("turn", 2), 2, 3], [4, 5],
              [("turn", 3), 6, 7], [8, 9], [10, 11, 12], [13, 14], [15, 16, 17], [18, 19], [20, 21], [22, 23], [], []]
    BESIDE = [[("scores", w) if isinstance(w, int) else w for w in beside] for beside in BESIDE]
    assert len(BESIDE) == 2 * UNIT_HEADS
    VALUES_AFTER = [8, 9, 10, 11]
    OUTPUTS_AFTER, MAXIMA_AFTER = 13, 15
    PROJECT_AFTER = [0, 2, 4, 6]
    QKV, TURN, SCORED = {}, {}, {}
    USES = 0
    for what, n in LEAD + sum(BESIDE, []):
        {"project": QKV, "turn": TURN, "scores": SCORED}[what][n] = USES
        USES += 2 if what == "turn" else 1
    BANKS = 3
    assert USES % BANKS == 0
    K_TURNS = [k + 1 for k in TURN.values()]
    BY_VECTOR = [k for k in range(USES) if k not in K_TURNS]
    KEPT = len(BY_VECTOR)
    NORM_AFTER = {2: 1, 7: 2, 15: 3}
    TURN_ROWS_AFTER = {5: 1, 12: 2, 21: 3}

    def kept_after(u, k):
        return KEPT * u + sum(j <= k for j in BY_VECTOR) + BANKS

    TAIL = ["outputs00", "maxima1", "outputs01", "outputs10", "maxima0", "outputs11", "heads0", "heads1", "out0", "out1"]

    def tail_number(b, use):
        at = TAIL.index(use)
        if b is LAST and at > TAIL.index("maxima0"):
            at -= 1
        return len(TAIL) * b + at + 1

    def maxima_number(b, hh):
        if hh == 1:
            return tail_number(b, "maxima1")
        return 0 if b is FIRST else tail_number(b - 1, "maxima0")

    FIRST, LAST = 0, BATCH - 1

    with ExitStack() as stack:
        enter = stack.enter_context

        def sb(name, shape, dtype=F32, enter=enter):
            return enter(nc.sbuf_tensor(f"at_{name}", shape, dtype))

        def sem(name):
            return enter(nc.semaphore(f"at_{name}"))

        w_hi = sb("w_hi", [P, 16, P], F32R)
        w_lo = sb("w_lo", [P, 16, P], F32R)
        xt = sb("xt", [P, 2, DK, SEQ], F32R)
        row_stack = [sb(f"row_stack{i}", [P, 2, UNIT_HEADS, STACK]) for i in range(2)]
        q_stack = [sb(f"q_stack{i}", [P, PAIRS, SEQ], F32R) for i in range(2)]
        k_stack = [sb(f"k_stack{i}", [P, 2, PAIRS, SEQ], F32R) for i in range(2)]
        v_ones = [sb(f"v_ones{i}", [P, QT, UNIT_HEADS, 32]) for i in range(2)]
        maxima = sb("maxima", [P, QT, 2, PAIRS])
        minus_max = sb("minus_max", [P, QT, 2, 2, PAIRS])
        max_t = sb("max_t", [4 * PAIRS, SEQ])
        hide_256 = sb("hide_256", [P, 2 * P], BF16)
        x = sb("x", [P, T, D])
        xt_all = sb("xt_all", [P, 2, DK, TOK - SEQ], F32R)
        norm = Norm(nc, enter, enter, "at", x, x)
        probs = [sb(f"probs{i}", [P, GROUP, WIDTH]) for i in range(2)]
        w_raw = probs[0][:].rearrange("p g c -> p (g c)")[:, 0:8 * D].rearrange("p (i c) -> p i c", c=D)
        o_t = [sb(f"o_t{i}", [P, SEQ]) for i in range(2)]
        inverse = sb("inverse_sum", [P, QT, GROUP])
        heads_out = sb("heads_out", [P, QT, D])
        heads_t_hi = sb("heads_t_hi", [P, DK, SEQ], F32R)
        heads_t_lo = sb("heads_t_lo", [P, DK, SEQ], F32R)
        x_now = sb("x_now", [P, QT, D])
        x_out = sb("x_out", [P, QT, D])

        ps_keys = enter(nc.psum_tensor("at_ps_keys", [P, 3 * 512], F32))
        ps_pv = enter(nc.psum_tensor("at_ps_pv", [P, 512], F32))
        ps_4 = enter(nc.psum_tensor("at_ps_4", [P, 4, 512], F32))

        def front_bank(use):
            return ps_4[:, use % BANKS, :]

        tail_bank = ps_4[:, BANKS, :]

        def early_part(n, part):
            if n < 4:
                return (w_hi, w_lo)[part][:, 4 * n:4 * n + 4, :].rearrange("p a c -> p (a c)")
            g, k = (n - 4) // DK, n % DK
            return xt[:, part, k, :] if g == 0 else xt_all[:, part, k, (g - 1) * SEQ:g * SEQ]

        def early_bank(n):
            return ps_4[:, n, :] if n < 4 else ps_keys[:, (n - 4) % 3 * 512:((n - 4) % 3 + 1) * 512]

        def rows_turns(g):
            return range(4 + DK * g, 4 + DK * (g + 1))

        def keys_columns(half):
            return ps_keys[:, 0:WIDE] if half == 0 else ps_keys[:, 1024:1024 + WIDTH - WIDE]

        x_loaded = [sem(f"x_loaded{c}") for c in range(BATCH)]
        normed = [sem(f"normed{g}") for g in range(BATCH)]
        w_loaded, early_made, early_hi, early_kept = (
            sem("w_loaded"), sem("early_made"), sem("early_hi"), sem("early_kept"))
        filled, stacks_ready, v_ready, k_ready = sem("filled"), sem("stacks_ready"), sem("v_ready"), sem("k_ready")
        chained = sem("chained")
        xt_loaded, x_now_loaded, x_stored = sem("xt_loaded"), sem("x_now_loaded"), sem("x_stored")
        front_made, front_kept = sem("front_made"), sem("front_kept")
        v_kept, hi_done, stacked, k_turned = sem("v_kept"), sem("hi_done"), sem("stacked"), sem("k_turned")
        minus_hi, minus_ready, max_t_ready, max_in = sem("minus_hi"), sem("minus_ready"), sem("max_t_ready"), sem("max_in")
        keys_made, exped, pv_made, o_t_kept = sem("keys_made"), sem("exped"), sem("pv_made"), sem("o_t_kept")
        tail_made, tail_kept, inverse_done, heads_hi, out_ready = (
            sem("tail_made"), sem("tail_kept"), sem("inverse_done"), sem("heads_hi"), sem("out_ready"))
        turn_taken = sem("turn_taken")
        block = enter(nc.Block())

        def unit_loop(engine, front, step, finish):
            front(FIRST, 0)
            step(FIRST, 0, FIRST, 1, None)
            with engine.Fori(0, BATCH - 1) as b:
                step(b, 1, b + 1, 0, b)
                step(b + 1, 0, b + 1, 1, b)
            step(LAST, 1, None, None, LAST)
            finish(LAST)

        def front_alone(do, norm_rows, turn_rows):
            for i, (what, n) in enumerate(LEAD + sum(BESIDE, [])):
                do(what, n)
                if i in NORM_AFTER:
                    norm_rows(NORM_AFTER[i])
                if i in TURN_ROWS_AFTER:
                    turn_rows(TURN_ROWS_AFTER[i])

        @block.sync
        def _(sp):
            def load_rows(g):
                sp.dma_start(x[:, QT * g:QT * (g + 1), :], row_tiles(x_rows, QT * g, QT)).then_inc(x_loaded[g], 16)

            load_rows(0)
            sp.dma_start(w_raw[:, 0:6, :], w_qkv.rearrange("(i p) c -> p i c", p=P)).then_inc(w_loaded, 16)
            sp.dma_start(w_raw[:, 6:8, :], w_o.rearrange("(i p) c -> p i c", p=P)).then_inc(w_loaded, 16)
            for g in range(1, BATCH):
                load_rows(g)

            def rows_of(table, b):
                return table[bass.ds(b * SEQ, SEQ), :].rearrange("(t p) c -> p t c", p=P)

            def load_xt(b):
                sp.wait_ge(front_made, USES * (2 * b - 1) + QKV[QT - 1] + 1)
                sp.dma_start(xt[:].rearrange("p a k c -> p (a k) c").bitcast(F32),
                             xt_all[:, :, :, bass.ds((b - 1) * SEQ, SEQ)].rearrange("p a k c -> p (a k) c").bitcast(F32)
                             ).then_inc(xt_loaded, 16)

            def insert_max(b, hh):
                sp.wait_ge(max_t_ready, 2 * b + hh + 1)
                for odd in range(2):
                    for c in range(2):
                        row = odd * STACK + MAX_ROW + c
                        sp.dma_start(q_stack[hh][row:row + 1, :, :].bitcast(F32),
                                     max_t[(2 * odd + c) * PAIRS:(2 * odd + c + 1) * PAIRS, :]).then_inc(max_in, 16)

            def store(b):
                sp.wait_ge(out_ready, b + 1)
                sp.dma_start(rows_of(out_rows, b), x_out[:]).then_inc(x_stored, 16)

            def load_x(b):
                sp.dma_start(x_now[:], rows_of(x_rows, b)).then_inc(x_now_loaded, 16)

            def batch(b, next_xt):
                insert_max(b, 0)
                if next_xt:
                    load_xt(b + 1)
                store(b - 1)
                load_x(b)
                insert_max(b, 1)

            sp.sem_inc(x_stored, 16)
            sp.sem_inc(max_in, 64)
            load_x(FIRST)
            insert_max(FIRST, 0)
            sp.wait_ge(early_kept, 12)
            load_xt(1)
            insert_max(FIRST, 1)
            with sp.Fori(1, LAST) as b:
                batch(b, True)
            batch(LAST, False)
            store(LAST)
            sp.wait_ge(x_stored, 16 * (BATCH + 1))

        @block.gpsimd
        def _(pool):
            for i in range(2):
                pool.memset(row_stack[i][:], 0.0).then_inc(filled, 1)
            for i in range(2):
                pool.memset(v_ones[i][:], 0.0).then_inc(filled, 1)
            pool.memset(hide_256[:], 0.0).then_inc(filled, 1)
            pool.wait_ge(filled, 2)
            for i in range(2):
                pool.memset(row_stack[i][:, 1, :, MAX_ROW:MAX_ROW + 2], 1.0).then_inc(stacks_ready, 1)
            pool.wait_ge(filled, 5)
            for i in range(2):
                pool.memset(v_ones[i][:, :, :, HD:HD + 1], 1.0).then_inc(v_ready, 1)
            for i in range(2):
                pool.memset(k_stack[i][:].rearrange("p a b c -> p (a b c)").bitcast(F32), 0.0).then_inc(k_ready, 1)
            pool.affine_select(hide_256[:], hide_256[:], [[1, 2 * P]], ALU.is_ge, NEG, base=-P,
                               channel_multiplier=-1).then_inc(k_ready, 1)

            def front(b, hh):
                for t in range(QT):
                    stack_of = row_stack[t % 2]
                    pool.wait_ge(hi_done, QT * (2 * b + hh) + t + 1)
                    pool.sem_inc(turn_taken, 1)
                    pool.tensor_copy(stack_of[:, 0, :, HD:2 * HD], stack_of[:, 0, :, 0:HD])
                    pool.tensor_copy(stack_of[:, 1, :, 2 * HD:3 * HD], stack_of[:, 1, :, 0:HD]).then_inc(stacked, 1)

            def step(b, hh, next_b, next_hh, last_b):
                if next_b is not None:
                    front(next_b, next_hh)

            unit_loop(pool, front, step, lambda b: None)

        @block.scalar
        def _(act):
            def early(n):
                act.wait_ge(early_made, n + 1)
                act.activation(early_part(n, 0), early_bank(n), ACT.Copy).then_inc(early_hi, 1)

            norm.scalar(act, 0, QT)
            for n in range(4):
                early(n)
            norm.scalar(act, QT, QT)
            for n in rows_turns(0):
                early(n)
            act.wait_ge(stacks_ready, 2)
            act.wait_ge(v_ready, 2)
            act.wait_ge(k_ready, 3)

            def project(u, hh, t):
                act.wait_ge(front_made, USES * u + QKV[t] + 1)
                bank = front_bank(QKV[t])
                act.activation(row_stack[t % 2][:, :, :, 0:HD].rearrange("p a h c -> p (a h) c").bitcast(F32R),
                               bank[:, 0:2 * P].rearrange("p (h c) -> p h c", c=HD), ACT.Copy).then_inc(hi_done, 1)
                act.activation(v_ones[hh][:, t, :, 0:HD], bank[:, 2 * P:3 * P].rearrange("p (h c) -> p h c", c=HD),
                               ACT.Copy).then_inc(v_kept, 1)

            def turn(u, hh, t):
                at = slice(t * P, (t + 1) * P)
                act.wait_ge(front_made, USES * u + TURN[t] + 2)
                for odd in range(2):
                    rows = slice(odd * STACK, (odd + 1) * STACK)
                    last = act.activation(k_stack[hh][rows, odd, :, at],
                                          front_bank(TURN[t] + 1)[rows, :].rearrange("p (a c) -> p a c", c=P), ACT.Copy)
                last.then_inc(k_turned, 1)

            def do(u, hh, what, n):
                if what == "project":
                    project(u, hh, n)
                if what == "turn":
                    turn(u, hh, n)

            def exps(b, hh, i):
                h, half = i // 2, i % 2
                columns = slice(0, WIDE) if half == 0 else slice(WIDE, WIDTH)
                act.wait_ge(keys_made, 2 * UNIT_HEADS * (2 * b + hh) + i + 1)
                act.activation(probs[h // GROUP][:, h % GROUP, columns], keys_columns(half), ACT.Exp,
                               scale=float(HD) ** -0.5).then_inc(exped, 1)

            def keep_o_t(b, hh, g):
                act.wait_ge(pv_made, 2 * (2 * b + hh) + g + 1)
                act.activation(o_t[g][:], ps_pv[:], ACT.Copy).then_inc(o_t_kept, 1)

            def norm_rows(g):
                if g + 1 < BATCH:
                    norm.scalar(act, QT * (g + 1), QT)

            def front(b, hh):
                front_alone(lambda what, n: do(2 * b + hh, hh, what, n), norm_rows,
                            lambda g: [early(n) for n in rows_turns(g)])

            def keep_heads(b, k):
                act.wait_ge(tail_made, tail_number(b, f"heads{k}") + 1)
                act.activation(heads_t_hi[:, k, :], tail_bank, ACT.Copy).then_inc(heads_hi, 1)

            def step(b, hh, next_b, next_hh, last_b):
                def beside(work):
                    if next_b is not None:
                        for what, n in work:
                            do(2 * next_b + next_hh, next_hh, what, n)

                if last_b is not None:
                    keep_o_t(last_b, 1 - hh, 1)
                beside(LEAD)
                for i in range(2 * UNIT_HEADS):
                    exps(b, hh, i)
                    beside(BESIDE[i])
                    if i == OUTPUTS_AFTER - 1:
                        keep_o_t(b, hh, 0)
                    if hh == 0 and last_b is not None and i in PROJECT_AFTER[0:DK]:
                        keep_heads(last_b, PROJECT_AFTER.index(i))

            def finish(b):
                keep_o_t(b, 1, 1)
                for k in range(DK):
                    keep_heads(b, k)

            act.sem_inc(exped, 2)
            act.sem_inc(o_t_kept, 1)
            unit_loop(act, front, step, finish)



        @block.vector
        def _(v):
            chain = Chain(v, chained)

            def norm_rows(g):
                norm.inverses(v, chain, QT * g, QT)
                norm.rows(v, QT * g, QT, normed[g])
                if g + 1 < BATCH:
                    norm.statistics(v, chain, x_loaded[g + 1], QT * (g + 1), QT)

            def early(n):
                v.wait_ge(early_hi, n + 1)
                v.tensor_tensor(early_part(n, 1), early_bank(n), early_part(n, 0).bitcast(F32), ALU.subtract).then_inc(early_kept, 1)

            norm.statistics(v, chain, x_loaded[0], 0, QT)
            norm.inverses(v, chain, 0, QT)
            norm.rows(v, 0, QT, normed[0])
            norm.statistics(v, chain, x_loaded[1], QT, QT)
            for n in (*range(4), *rows_turns(0)):
                early(n)
            v.sem_inc(front_kept, BANKS)
            v.wait_ge(stacks_ready, 2)

            def project(u, hh, t):
                bank = front_bank(QKV[t])
                stack_of = row_stack[t % 2]
                v.wait_ge(v_kept, QT * u + t + 1)
                v.tensor_tensor(stack_of[:, 0, :, 2 * HD:3 * HD], bank[:, 0:P].rearrange("p (h c) -> p h c", c=HD),
                                stack_of[:, 0, :, 0:HD], ALU.subtract)
                v.tensor_tensor(stack_of[:, 1, :, HD:2 * HD], bank[:, P:2 * P].rearrange("p (h c) -> p h c", c=HD),
                                stack_of[:, 1, :, 0:HD], ALU.subtract).then_inc(front_kept, 1)

            def turn(u, hh, t):
                v.wait_ge(front_made, USES * u + TURN[t] + 1)
                v.tensor_copy(q_stack[hh][:, :, t * P:(t + 1) * P],
                              front_bank(TURN[t]).rearrange("p (a c) -> p a c", c=P)).then_inc(front_kept, 1)

            def maximum(u, hh, n):
                qt, heads = SCORES[n]
                bank = front_bank(SCORED[n])
                v.wait_ge(front_made, USES * u + SCORED[n] + 1)
                if len(heads) == 2:
                    v.reduce_max(maxima[:, qt, :, heads[0] // 2],
                                 bank.rearrange("p (a c) -> p a c", a=2)[:, :, 0:(qt + 1) * P], AX_X).then_inc(front_kept, 1)
                else:
                    h = heads[0]
                    v.reduce_max(maxima[:, qt, h % 2, h // 2:h // 2 + 1], bank[:, 0:(qt + 1) * P], AX_X).then_inc(front_kept, 1)

            def negate(b, hh):
                u = 2 * b + hh
                most = maxima[:].rearrange("p q o a -> p (q o) a")
                hi = minus_max[:, :, :, 0, :].rearrange("p q o a -> p (q o) a")
                lo = minus_max[:, :, :, 1, :].rearrange("p q o a -> p (q o) a")
                v.wait_ge(front_kept, kept_after(u, USES - 1))
                v.tensor_scalar_mul(hi.bitcast(F32R), most, -1.0).then_inc(minus_hi, 1)
                v.wait_ge(minus_hi, u + 1)
                v.scalar_tensor_tensor(lo, most, -1.0, hi, ALU.mult, ALU.subtract).then_inc(minus_ready, 1)
                v.wait_ge(max_in, 64 * (u + 1))
                v.wait_ge(tail_made, maxima_number(b, hh) + 1)
                v.tensor_copy(max_t[:], tail_bank[0:4 * PAIRS, :]).then_inc(tail_kept, 1)
                v.wait_ge(tail_kept, maxima_number(b, hh) + 1)
                v.sem_inc(max_t_ready, 1)

            def do(u, hh, what, n):
                {"project": project, "turn": turn, "scores": maximum}[what](u, hh, n)

            def divide(b, hh, g):
                number = tail_number(b, f"outputs{hh}{g}")
                v.wait_ge(tail_made, number + 1)
                v.wait_ge(tail_kept, number)
                by_head = tail_bank.rearrange("p (q h c) -> p q h c", q=QT, h=GROUP)
                v.reciprocal(inverse[:], by_head[:, :, :, HD]).then_inc(inverse_done, 1)
                v.wait_ge(inverse_done, 2 * (2 * b + hh) + g + 1)
                columns = heads_out[:, :, (2 * hh + g) * GROUP * HD:(2 * hh + g + 1) * GROUP * HD]
                v.tensor_tensor(columns.rearrange("p q (h c) -> p q h c", h=GROUP), by_head[:, :, :, 0:HD],
                                inverse[:].unsqueeze(3).broadcast_to([P, QT, GROUP, HD]), ALU.mult).then_inc(tail_kept, 1)

            def front(b, hh):
                front_alone(lambda what, n: do(2 * b + hh, hh, what, n),
                            norm_rows,
                            lambda g: [early(n) for n in rows_turns(g)])
                negate(b, hh)

            def split_heads(b, k):
                v.wait_ge(heads_hi, DK * b + k + 1)
                v.tensor_tensor(heads_t_lo[:, k, :], tail_bank, heads_t_hi[:, k, :].bitcast(F32), ALU.subtract).then_inc(tail_kept, 1)

            def add_out(b, n):
                if n == 0:
                    v.wait_ge(x_now_loaded, 16 * (b + 1))
                    v.wait_ge(x_stored, 16 * (b + 1))
                v.wait_ge(tail_made, tail_number(b, f"out{n}") + 1)
                v.tensor_tensor(x_out[:, 2 * n:2 * n + 2, :].rearrange("p q c -> p (q c)"), tail_bank,
                                x_now[:, 2 * n:2 * n + 2, :].rearrange("p q c -> p (q c)"), ALU.add).then_inc(tail_kept, 1)
                if n == 1:
                    v.wait_ge(tail_kept, tail_number(b, "out1") + 1)
                    v.sem_inc(out_ready, 1)

            PROJECTION = [(split_heads, 0), (split_heads, 1), (add_out, 0), (add_out, 1)]

            def step(b, hh, next_b, next_hh, last_b):
                def beside(work):
                    if next_b is not None:
                        for what, n in work:
                            do(2 * next_b + next_hh, next_hh, what, n)

                beside(LEAD)
                if last_b is not None:
                    divide(last_b, 1 - hh, 1)
                for i in range(2 * UNIT_HEADS):
                    beside(BESIDE[i])
                    if i == OUTPUTS_AFTER:
                        divide(b, hh, 0)
                    if i == MAXIMA_AFTER and next_b is not None:
                        negate(next_b, next_hh)
                    if hh == 0 and last_b is not None and i in PROJECT_AFTER:
                        part, n = PROJECTION[PROJECT_AFTER.index(i)]
                        part(last_b, n)

            def finish(b):
                divide(b, 1, 1)
                for part, n in PROJECTION:
                    part(b, n)

            unit_loop(v, front, step, finish)

        @block.tensor
        def _(pe):
            def early(n):
                g, k = (n - 4) // DK, n % DK
                if n >= 4:
                    pe.wait_ge(normed[g], QT)
                if n >= 7:
                    pe.wait_ge(early_kept, n - 2)
                for j in range(4):
                    if n < 3:
                        k, half, which = (4 * n + j) // 6, (4 * n + j) // 3 % 2, (4 * n + j) % 3
                        block_in = w_raw[:, 2 * which + half, k * P:(k + 1) * P]
                    elif n == 3:
                        block_in = w_raw[:, 6 + j % 2, j // 2 * P:(j // 2 + 1) * P]
                    else:
                        block_in = x[:, g * QT + j, k * P:(k + 1) * P]
                    last = pe.transpose(early_bank(n)[:, j * P:(j + 1) * P], block_in, const.identity[:])
                last.then_inc(early_made, 1)

            pe.wait_ge(w_loaded, 32)
            for n in (*range(4), *rows_turns(0)):
                early(n)
            pe.wait_ge(early_kept, 6)

            def three(out, hi_hi, hi_lo, lo_hi, first=True, end=True):
                for n, (w, m) in enumerate((hi_hi, hi_lo, lo_hi)):
                    last = pe.matmul(out, w, m, start=(first and n == 0), stop=(end and n == 2))
                return last

            def use(u, k, kept=-1):
                before = k - BANKS
                if before in K_TURNS:
                    pe.wait_ge(k_turned, QT * u + K_TURNS.index(before) + 1)
                elif before >= 0:
                    kept = max(kept, before)
                elif kept < 0:
                    pe.wait_ge(front_kept, KEPT * u + k + 1)
                if kept >= 0:
                    pe.wait_ge(front_kept, kept_after(u, kept))

            def project(u, hh, t):
                use(u, QKV[t])
                out = front_bank(QKV[t])[:, 0:3 * P]
                at = slice(t * P, (t + 1) * P)
                for k in range(DK):
                    tiles = slice((2 * k + hh) * 3, (2 * k + hh + 1) * 3)
                    hi, lo = (w[:, tiles, :].rearrange("p a c -> p (a c)") for w in (w_hi, w_lo))
                    last = three(out, (xt[:, 0, k, at], hi), (xt[:, 0, k, at], lo), (xt[:, 1, k, at], hi),
                                 first=(k == 0), end=(k == DK - 1))
                last.then_inc(front_made, 1)

            def turn(u, hh, t):
                pe.wait_ge(stacked, QT * u + t + 1)
                for part in range(2):
                    use(u, TURN[t] + part, QKV[t] if part == 0 else -1)
                    for a in range(PAIRS):
                        last = pe.transpose(front_bank(TURN[t] + part)[:, a * P:(a + 1) * P],
                                            row_stack[t % 2][:, part, 2 * a:2 * a + 2, :].rearrange("p h c -> p (h c)"),
                                            const.identity[:])
                    last.then_inc(front_made, 1)

            def scores(u, hh, n):
                qt, heads = SCORES[n]
                tiles = max(2, qt + 1)
                if n == 0 or SCORES[n - 1][0] != qt:
                    pe.wait_ge(k_turned, QT * u + tiles)
                    use(u, SCORED[n], TURN[tiles - 1])
                else:
                    use(u, SCORED[n])
                keys = max(2 * P, (qt + 1) * P)
                for i, h in enumerate(heads):
                    out = front_bank(SCORED[n])[:, i * keys:(i + 1) * keys]
                    pe.matmul(out, q_stack[hh][:, h // 2, qt * P:(qt + 1) * P], k_stack[hh][:, h % 2, h // 2, 0:keys],
                              start=True, stop=False)
                    last = pe.matmul(out[:, qt * P:(qt + 1) * P], const.identity_bf[:], const.hide_later[:], start=False, stop=True)
                last.then_inc(front_made, 1)

            def turn_max(b, hh):
                pe.wait_ge(minus_ready, 2 * b + hh + 1)
                if b is not FIRST or hh > 0:
                    pe.wait_ge(tail_kept, maxima_number(b, hh))
                for qt in range(QT):
                    last = pe.transpose(tail_bank[0:4 * PAIRS, qt * P:(qt + 1) * P],
                                        minus_max[:, qt].rearrange("p o c a -> p (o c a)"), const.identity[:])
                last.then_inc(tail_made, 1)

            def do(u, hh, what, n):
                if what == "project" and n == 0 and hh == 0 and u is not FIRST:
                    pe.wait_ge(xt_loaded, 8 * u)
                {"project": project, "turn": turn, "scores": scores}[what](u, hh, n)

            def key_scores(b, hh, i):
                h, half = i // 2, i % 2
                q, k = q_stack[hh][:, h // 2, :], k_stack[hh][:, h % 2, h // 2, :]
                pe.wait_ge(exped, 2 * UNIT_HEADS * (2 * b + hh) + i + 1)
                for j, (kt, q0) in enumerate(KEY_TILES[2 * half:2 * half + 2]):
                    at = 512 * j if half == 0 else 1024 + 256 * j
                    hidden = const.hide_later_t if q0 == kt * P else hide_256
                    out = ps_keys[:, at:at + SEQ - q0]
                    pe.matmul(out, k[:, kt * P:(kt + 1) * P], q[:, q0:SEQ], start=True, stop=False)
                    last = pe.matmul(out[:, 0:hidden.shape[1]], const.identity_bf[:], hidden[:], start=False, stop=True)
                last.then_inc(keys_made, 1)

            def values(b, hh, g, kt):
                u = 2 * b + hh
                if kt == 0:
                    pe.wait_ge(exped, 2 * UNIT_HEADS * u + 2 * GROUP * (g + 1) + 2)
                    pe.wait_ge(o_t_kept, 2 * u + g + 1)
                at = sum(SEQ - q0 for _, q0 in KEY_TILES[:kt])
                q0 = KEY_TILES[kt][1]
                for j in range(GROUP):
                    last = pe.matmul(ps_pv[32 * j:32 * j + 32, kt * P:SEQ], v_ones[hh][:, kt, g * GROUP + j, :],
                                     probs[g][:, j, at + kt * P - q0:at + SEQ - q0], start=(kt == 0), stop=(kt == QT - 1),
                                     skip_group_check=True)
                if kt == QT - 1:
                    last.then_inc(pv_made, 1)

            def turn_o(b, hh, g):
                pe.wait_ge(o_t_kept, 2 * (2 * b + hh) + g + 2)
                pe.wait_ge(tail_kept, tail_number(b, f"outputs{hh}{g}"))
                for qt in range(QT):
                    last = pe.transpose(tail_bank[:, qt * P:(qt + 1) * P], o_t[g][:, qt * P:(qt + 1) * P], const.identity[:])
                last.then_inc(tail_made, 1)

            def turn_heads(b, k):
                pe.wait_ge(tail_kept, tail_number(b, f"heads{k}"))
                for qt in range(QT):
                    last = pe.transpose(tail_bank[:, qt * P:(qt + 1) * P], heads_out[:, qt, k * P:(k + 1) * P],
                                        const.identity[:])
                last.then_inc(tail_made, 1)

            def project_out(b, n):
                pe.wait_ge(tail_kept, tail_number(b, f"out{n}"))
                for i in range(2):
                    at = slice((2 * n + i) * P, (2 * n + i + 1) * P)
                    for k in range(DK):
                        hi, lo = (w[:, 12 + 2 * k:14 + 2 * k, :].rearrange("p a c -> p (a c)") for w in (w_hi, w_lo))
                        last = three(tail_bank[:, i * D:(i + 1) * D], (heads_t_hi[:, k, at], hi),
                                     (heads_t_hi[:, k, at], lo), (heads_t_lo[:, k, at], hi), first=(k == 0), end=(k == DK - 1))
                last.then_inc(tail_made, 1)

            PROJECTION = [(turn_heads, 0), (turn_heads, 1), (project_out, 0), (project_out, 1)]

            def front(b, hh):
                front_alone(lambda what, n: do(2 * b + hh, hh, what, n), lambda g: None,
                            lambda g: [early(n) for n in rows_turns(g)])
                turn_max(b, hh)
                pe.wait_ge(early_kept, 12)

            def step(b, hh, next_b, next_hh, last_b):
                def beside(work):
                    if next_b is not None:
                        for what, n in work:
                            do(2 * next_b + next_hh, next_hh, what, n)

                beside(LEAD)
                if last_b is not None:
                    turn_o(last_b, 1 - hh, 1)
                pe.wait_ge(max_in, 64 * (2 * b + hh + 2))
                for i in range(2 * UNIT_HEADS):
                    key_scores(b, hh, i)
                    beside(BESIDE[i])
                    if i in VALUES_AFTER:
                        values(b, hh, 0, VALUES_AFTER.index(i))
                    if i == OUTPUTS_AFTER:
                        turn_o(b, hh, 0)
                    if i == MAXIMA_AFTER and next_b is not None:
                        turn_max(next_b, next_hh)
                    if hh == 0 and last_b is not None and i in PROJECT_AFTER:
                        part, n = PROJECTION[PROJECT_AFTER.index(i)]
                        part(last_b, n)
                for kt in range(QT):
                    values(b, hh, 1, kt)

            def finish(b):
                turn_o(b, 1, 1)
                for part, n in PROJECTION:
                    part(b, n)

            unit_loop(pe, front, step, finish)



def macaron_kernel(nc, hidden, w_qkv, w_o, Wg, w1, w2, out):
    x_rows = hidden.rearrange("b s c -> (b s) c")
    out_rows = out.rearrange("b s c -> (b s) c")
    after_first = nc.dram_tensor("after_first", (TOK, D), F32, kind="Internal").ap()
    normed_rows = nc.dram_tensor("normed_rows", (TOK, D), F32, kind="Internal").ap()
    with ExitStack() as stack:
        const = Constants(nc, stack.enter_context)
        const.build(nc)
        feed_forward(nc, const, "first", x_rows, after_first, normed_rows, Wg, w1, w2, True)
        attention(nc, const, after_first, out_rows, w_qkv, w_o)
        feed_forward(nc, const, "second", out_rows, out_rows, normed_rows, Wg, w1, w2, False)


_INS = ["L0_attn_hidden_states", "L0_attn_w_qkv", "L0_attn_w_o", "L0_ffn_Wg", "L0_ffn_w1", "L0_ffn_w2"]
_OUT = ((BATCH, SEQ, D), "float32")


def kernel(**inputs):
    import numpy as _np
    import concourse.bacc as _bacc
    from concourse import mybir as _mybir
    from concourse.bass_utils import run_bass_kernel_spmd as _run

    nc = _bacc.Bacc("TRN2", target_bir_lowering=False, num_devices=1)
    arrays, args = {}, []
    for name in _INS:
        a = _np.ascontiguousarray(inputs[name])
        arrays[f"in_{name}_dram"] = a
        args.append(nc.dram_tensor(f"in_{name}_dram", a.shape, _mybir.dt.from_np(a.dtype), kind="ExternalInput").ap())
    shape, dtype = _OUT
    args.append(nc.dram_tensor("out_0_dram", shape, _mybir.dt.from_np(_np.dtype(dtype)), kind="ExternalOutput").ap())
    macaron_kernel(nc, *args)
    r = _run(nc, [arrays], core_ids=[0])
    return r.results[0]["out_0_dram"]
```

```python
from contextlib import ExitStack

import concourse.bass as bass
from concourse import mybir

F32 = mybir.dt.float32
F32R = mybir.dt.float32r
BF16 = mybir.dt.bfloat16
I32 = mybir.dt.int32
ALU = mybir.AluOpType
ACT = mybir.ActivationFunctionType
AX_X = mybir.AxisListType.X

P = 128
BATCH, SEQ, D = 4, 512, 256
TOK = BATCH * SEQ
T = TOK // P
DK = D // P
FF = 1024
FT = FF // P
E, K = 8, 2
CAP = -(-5 * TOK * K // (4 * E))
ST = CAP // P
LC = E * ST
HALF = CAP // 2
EPS = 1e-5
FAR = 4096
NEG = -3.0e38
"""Every float32 product over a long dimension is made of three float32r ones: an operand a is
cut into hi = float32r(a), its upper 12 bits, and lo = a - hi, the rest, and a*b = hi*hi + hi*lo +
lo*hi up to 2**-24."""


class Chain:

    def __init__(self, engine, semaphore):
        self.engine, self.semaphore, self.count = engine, semaphore, 0

    def __call__(self, *instructions):
        for instruction in instructions:
            self.count += 1
            instruction.then_inc(self.semaphore, 1)
        self.engine.wait_ge(self.semaphore, self.count)


class Constants:

    def __init__(self, nc, enter):
        def sb(name, shape, dtype=F32):
            return enter(nc.sbuf_tensor(name, shape, dtype))

        self.identity = sb("identity", [P, P])
        self.identity_bf = sb("identity_bf", [P, P], BF16)
        self.earlier = sb("earlier", [P, P], BF16)
        self.ones = sb("ones", [P, P], BF16)
        self.lane = sb("lane", [P, P])
        self.slot_tile = sb("slot_tile", [P, LC])
        self.rank = sb("rank", [P, E])
        self.first_tile = sb("first_tile", [P, E])
        self.token1 = sb("token1", [P, K, T])
        self.not_first = sb("not_first", [P, E, T])
        self.hide_later = sb("hide_later", [P, P], BF16)
        self.hide_later_t = sb("hide_later_t", [P, P], BF16)

        self.filled = enter(nc.semaphore("filled"))
        self.ready = enter(nc.semaphore("tables_ready"))

    def fill(self, pool):
        for table, value in ((self.identity, 0.0), (self.identity_bf, 0.0), (self.earlier, 1.0), (self.ones, 1.0),
                             (self.not_first, 1.0), (self.hide_later, 0.0), (self.hide_later_t, 0.0)):
            pool.memset(table[:], value).then_inc(self.filled, 1)
        small = dict(allow_small_or_imprecise_dtypes=True)
        pool.iota(self.lane[:], [[1, P]], base=0, channel_multiplier=0, **small).then_inc(self.filled, 1)
        pool.iota(self.slot_tile[:], [[1, LC]], base=0, channel_multiplier=0, **small).then_inc(self.filled, 1)
        pool.iota(self.rank[:], [[-1, E]], base=E, channel_multiplier=0, **small).then_inc(self.filled, 1)
        pool.iota(self.first_tile[:], [[ST, E]], base=0, channel_multiplier=0, **small).then_inc(self.filled, 1)
        pool.iota(self.token1[:], [[0, K], [P, T]], base=1, channel_multiplier=1, **small).then_inc(self.filled, 1)
        pool.wait_ge(self.filled, 12)
        for table in (self.identity, self.identity_bf):
            pool.affine_select(table[:], table[:], [[-1, P]], ALU.not_equal, 1.0, base=0,
                               channel_multiplier=1).then_inc(self.filled, 1)
        pool.affine_select(self.earlier[:], self.earlier[:], [[1, P]], ALU.is_gt, 0.0, base=0,
                           channel_multiplier=-1).then_inc(self.filled, 1)
        pool.affine_select(self.not_first[:], self.not_first[:], [[0, E], [1, T]], ALU.is_gt, 0.0, base=0,
                           channel_multiplier=0).then_inc(self.filled, 1)
        pool.affine_select(self.hide_later[:], self.hide_later[:], [[-1, P]], ALU.is_ge, NEG, base=0,
                           channel_multiplier=1).then_inc(self.filled, 1)
        pool.affine_select(self.hide_later_t[:], self.hide_later_t[:], [[1, P]], ALU.is_ge, NEG, base=0,
                           channel_multiplier=-1).then_inc(self.filled, 1)
        pool.wait_ge(self.filled, 18)
        pool.sem_inc(self.ready, 1)


class Norm:

    def __init__(self, nc, enter, enter_semaphore, tag, x, xn, stats):
        self.x, self.xn = x, xn
        self.rounds, self.roots = 0, 0
        self.stats = stats
        self.moments = enter(nc.sbuf_tensor(f"{tag}_moments", [P, T, 2], F32))
        self.variance = enter(nc.sbuf_tensor(f"{tag}_variance", [P, T], F32))
        self.root = enter(nc.sbuf_tensor(f"{tag}_root", [P, T], F32))
        self.inverse = enter(nc.sbuf_tensor(f"{tag}_inverse", [P, T], F32))
        self.scratch = enter(nc.sbuf_tensor(f"{tag}_scratch", [P, T], F32))
        self.has_variance = enter_semaphore(nc.semaphore(f"{tag}_has_variance"))
        self.has_root = enter_semaphore(nc.semaphore(f"{tag}_has_root"))

    def statistics(self, v, chain, loaded, first, count):
        v.wait_ge(loaded, 16)
        for t in range(first, first + count):
            last = v.bn_stats(self.stats[:, t, :], self.x[:, t, :])
        chain(last)
        self.variances(v, chain, first, count)

    def variances(self, v, chain, first, count):
        tiles = slice(first, first + count)
        for t in range(first, first + count):
            last = v.bn_aggr(self.moments[:, t, :], self.stats[:, t, :])
        chain(last)
        v.tensor_scalar_add(self.variance[:, tiles], self.moments[:, tiles, 1], EPS).then_inc(self.has_variance, 1)

    def inverses(self, v, chain, first, count):
        tiles = slice(first, first + count)
        self.rounds += 1
        v.wait_ge(self.has_root, self.rounds)
        inverse, scratch = self.inverse[:, tiles], self.scratch[:, tiles]
        chain(v.reciprocal(inverse, self.root[:, tiles]))
        chain(v.tensor_tensor(scratch, inverse, inverse, ALU.mult))
        chain(v.tensor_tensor(scratch, scratch, self.variance[:, tiles], ALU.mult))
        chain(v.tensor_scalar(scratch, scratch, -0.5, 1.5, ALU.mult, ALU.add))
        chain(v.tensor_tensor(inverse, inverse, scratch, ALU.mult))

    def rows(self, v, first, count, normed):
        for t in range(first, first + count):
            v.tensor_scalar(self.xn[:, t, :], self.x[:, t, :], self.moments[:, t, 0:1], self.inverse[:, t:t + 1],
                            ALU.subtract, ALU.mult).then_inc(normed, 1)

    def scalar(self, s, first, count):
        self.roots += 1
        s.wait_ge(self.has_variance, self.roots)
        s.activation(self.root[:, first:first + count], self.variance[:, first:first + count], ACT.Sqrt).then_inc(self.has_root, 1)


def row_tiles(rows, first, count):
    return rows[first * P:(first + count) * P, :].rearrange("(t p) c -> p t c", p=P)


def feed_forward(nc, const, tag, x, stats, x_rows, sum_rows, xn_rows, Wg, w1, w2, first_phase, rows_stored):
    with ExitStack() as stack:
        enter = stack.enter_context

        def sb(name, shape, dtype=F32, enter=enter):
            return enter(nc.sbuf_tensor(f"{tag}_{name}", shape, dtype))

        def sem(name):
            return enter(nc.semaphore(f"{tag}_{name}"))

        gather_index = sb("gather_index", [P, LC], I32)
        add_index = sb("add_index", [P, LC], I32)
        gate = sb("gate", [P, LC])
        gather_now = [sb(f"gather_now{i}", [P, ST], I32) for i in range(2)]
        add_now = [sb(f"add_now{i}", [P, ST], I32) for i in range(2)]
        gate_now = [sb(f"gate_now{i}", [P, ST]) for i in range(2)]
        w1_raw = sb("w1_raw", [P, DK, FF])
        w2_raw = sb("w2_raw", [P, FT, D])
        w1_hi = [sb("w1_hi0", [P, DK, FF], F32R)]
        w1_lo = [sb("w1_lo0", [P, DK, FF], F32R)]
        w2_hi = [sb("w2_hi0", [P, FT, D], F32R)]
        w2_lo = [sb("w2_lo0", [P, FT, D], F32R)]
        xg = [sb(f"xg{i}", [P, ST, D]) for i in range(2)]
        xt_hi = sb("xt_hi", [P, DK, CAP], F32R)
        xt_lo = sb("xt_lo", [P, DK, CAP], F32R)
        scaled = [sb(f"scaled{i}", [P, ST, D]) for i in range(2)]

        PARTS = 8
        PART = K * T // PARTS
        with ExitStack() as early:
            def eb(name, shape, dtype=F32):
                return sb(name, shape, dtype, early.enter_context)

            xn = eb("xn", [P, T, D])
            xn_t = eb("xn_t", [P, DK, TOK])
            norm = Norm(nc, early.enter_context, enter, tag, x, xn, stats)
            wg = eb("wg", [P, DK, 32])
            logits_t = eb("logits_t", [P, SEQ])
            logits = eb("logits", [P, T, E])
            others = eb("others", [P, T, E])
            top = eb("top", [P, K, T])
            equal = eb("equal", [P, T, E])
            best = eb("best", [P, T])
            chosen = eb("chosen", [P, K, T, E])
            exp_in = eb("exp_in", [P, (E + 1) * T])
            exp_out = eb("exp_out", [P, (E + 1) * T])
            gates = eb("gates", [P, K, T])
            taken = eb("taken", [P, E, T])
            taken_bf = eb("taken_bf", [P, E, T], BF16)
            running = eb("running", [P, E * T])
            before_bf = eb("before_bf", [P, E, T], BF16)
            product = eb("product", [P, K, T, E])
            start = eb("start", [P, K, T, E])
            over = eb("over", [P, K * T])
            position = eb("position", [P, K * T])
            column = eb("column", [P, K * T])
            tile_no = eb("tile_no", [P, K * T])
            in_tile = eb("in_tile", [P, K * T])
            of_tile = eb("of_tile", [P, K * T, LC])
            values = eb("values", [P, PARTS, PART * 2 * LC + P - 2 * LC])
            of_lane = eb("of_lane", [P, K * T, P])
        h_hi = sb("h_hi", [P, FT, CAP], F32R)
        h_lo = sb("h_lo", [P, FT, CAP], F32R)
        w1_hi.append(sb("w1_hi1", [P, DK, FF], F32R))
        w1_lo.append(sb("w1_lo1", [P, DK, FF], F32R))
        w2_hi.append(sb("w2_hi1", [P, FT, D], F32R))
        w2_lo.append(sb("w2_lo1", [P, FT, D], F32R))

        ps_h = enter(nc.psum_tensor(f"{tag}_ps_h", [P, 2, 2, 512], F32))
        ps_o = enter(nc.psum_tensor(f"{tag}_ps_o", [P, 2, 512], F32))
        ps_x = enter(nc.psum_tensor(f"{tag}_ps_x", [P, 2, 512], F32))

        XB = [(0, 2), (2, 2), (4, 1)]
        CHUNK = SEQ // P
        x_loaded = [sem(f"x_loaded{c}") for c in range(T // CHUNK)]
        wg_loaded, x_copied = sem("wg_loaded"), sem("x_copied")
        normed, stored = [sem(f"normed{c}") for c in range(T // CHUNK)], sem("stored")
        xn_turned, xn_t_ready = sem("xn_turned"), sem("xn_t_ready")
        wg_clear, pads_clear = sem("wg_clear"), sem("pads_clear")
        tiles_ready, tokens_ready = sem("tiles_ready"), sem("tokens_ready")
        logits_t_made, logits_t_kept, logits_made = sem("logits_t_made"), sem("logits_t_kept"), sem("logits_made")
        exp_asked, exp_done = sem("exp_asked"), sem("exp_done")
        taken_ready, positions_made = sem("taken_ready"), sem("positions_made")
        lane_ready, list_made, list_kept = sem("lane_ready"), sem("list_made"), sem("list_kept")
        rows_listed = sem("rows_listed")
        chained = sem("chained")

        raw_loaded, w_hi_done, w_split = sem("raw_loaded"), sem("w_hi_done"), sem("w_split")
        staged, gathered, x_turned = sem("staged"), [[sem(f"gathered{i}_{b}") for b in range(3)] for i in range(2)], sem("x_turned")
        x_hi_done, x_split = sem("x_hi_done"), sem("x_split")
        h_made, h_hi_done, h_split = sem("h_made"), sem("h_hi_done"), sem("h_split")
        o_made, o_scaled = sem("o_made"), sem("o_scaled")
        added, listed, turn = sem("added"), sem("listed"), sem("turn")

        block = enter(nc.Block())

        def expert_loop(engine, pair):
            with engine.Fori(0, E // 2 - 1) as i:
                pair(i, False)
            pair(E // 2 - 1, True)

        @block.sync
        def _(sp):
            if first_phase:
                for c in range(T // CHUNK):
                    sp.dma_start(x[:, c * CHUNK:(c + 1) * CHUNK, :], row_tiles(x_rows, c * CHUNK, CHUNK)).then_inc(x_loaded[c], 16)
            sp.wait_ge(wg_clear, 1)
            sp.dma_start(wg[:, :, 0:E], Wg.rearrange("(k p) e -> p k e", p=P)).then_inc(wg_loaded, 16)

            def load_expert(e):
                sp.dma_start(w1_raw[:], w1[e].rearrange("(k p) f -> p k f", p=P)).then_inc(raw_loaded, 16)
                sp.dma_start(w2_raw[:], w2[e].rearrange("(f p) c -> p f c", p=P)).then_inc(raw_loaded, 16)

            load_expert(0)
            if first_phase:
                sp.dma_start(sum_rows, x_rows).then_inc(x_copied, 16)
            for c in range(T // CHUNK):
                sp.wait_ge(normed[c], CHUNK)
                sp.dma_start(row_tiles(xn_rows, c * CHUNK, CHUNK), xn[:, c * CHUNK:(c + 1) * CHUNK, :]).then_inc(stored, 16)
            sp.wait_ge(x_turned, len(XB))
            with sp.Fori(1, E) as e:
                sp.wait_ge(w_split, e)
                sp.dma_start(w1_raw[:], w1[bass.ds(e, 1)].rearrange("o (k p) f -> p (o k) f", p=P)).then_inc(raw_loaded, 16)
                sp.dma_start(w2_raw[:], w2[bass.ds(e, 1)].rearrange("o (f p) c -> p (o f) c", p=P)).then_inc(raw_loaded, 16)

        @block.gpsimd
        def _(pool):
            pool.memset(wg[:], 0.0).then_inc(wg_clear, 1)
            if first_phase:
                const.fill(pool)
            pool.memset(values[:, :, PART * 2 * LC:], 0.0).then_inc(pads_clear, 1)
            for h in range(PARTS):
                part = slice(PART * h, PART * (h + 1))
                by_pair = values[:, h, 0:PART * 2 * LC].rearrange("p (n two c) -> p n two c", n=PART, two=2)
                pool.wait_ge(tiles_ready, h + 1)
                pool.tensor_tensor(by_pair[:, :, 0, :], of_tile[:, part],
                                   const.token1[:].rearrange("p k t -> p (k t)")[:, part].unsqueeze(2).broadcast_to([P, PART, LC]),
                                   ALU.mult).then_inc(tokens_ready, 1)
            pool.wait_ge(rows_listed, 1)
            pool.wait_ge(stored, 16 * (T // CHUNK))
            if first_phase:
                pool.wait_ge(x_copied, 16)
            else:
                pool.wait_ge(rows_stored, 16 * BATCH)
            last_row = pool.to_reg(TOK - 1)

            def gather(e, par):
                pool.tensor_copy(gather_now[par][:], gather_index[:, bass.ds(e * ST, ST)]).then_inc(staged, 1)
                pool.wait_ge(staged, e + 1)
                pool.sem_inc(turn, 1)
                for b, (s0, n) in enumerate(XB):
                    for s in range(s0, s0 + n):
                        pool.indirect_dma_start(xg[par][:, s, :], None, xn_rows,
                                                bass.IndirectOffsetOnAxis(ap=gather_now[par][:, s:s + 1], axis=0)
                                                ).then_inc(gathered[par][b], 16)

            def add_out(e, par):
                for s in range(ST):
                    if s > 0:
                        pool.wait_ge(added, 16 * (ST * e + s))
                        pool.sem_inc(turn, 1)
                    pool.wait_ge(o_scaled, ST * e + s + 3)
                    pool.sem_inc(turn, 1)
                    pool.indirect_dma_start(sum_rows, bass.IndirectOffsetOnAxis(ap=add_now[par][:, s:s + 1], axis=0),
                                            scaled[par][:, s, :], None, bounds_check=last_row, oob_is_err=False,
                                            compute_op=ALU.add).then_inc(added, 16)

            def expert(e, par, last, first=False):
                if not last:
                    pool.wait_ge(x_turned, len(XB) * (e + 1))
                    pool.sem_inc(turn, 1)
                    gather(e + 2, par)
                if not first:
                    pool.wait_ge(added, 16 * ST * e)
                    pool.sem_inc(turn, 1)
                pool.tensor_copy(add_now[par][:], add_index[:, bass.ds(e * ST, ST)])
                pool.tensor_copy(gate_now[par][:], gate[:, bass.ds(e * ST, ST)]).then_inc(listed, 1)
                pool.wait_ge(listed, e + 1)
                pool.sem_inc(turn, 1)
                add_out(e, par)

            gather(0, 0)
            gather(1, 1)
            pool.wait_ge(list_kept, 1)
            expert(0, 0, False, first=True)
            expert(1, 1, False)
            with pool.Fori(1, E // 2 - 1) as i:
                expert(2 * i, 0, False)
                expert(2 * i + 1, 1, False)
            expert(E - 2, 0, True)
            expert(E - 1, 1, True)
            pool.wait_ge(added, 16 * LC)

        @block.scalar
        def _(act):
            def split_w1(e, par):
                act.wait_ge(raw_loaded, 32 * (e + 1))
                act.activation(w1_hi[par][:], w1_raw[:], ACT.Copy).then_inc(w_hi_done, 1)

            def split_w2(e, par):
                act.activation(w2_hi[par][:], w2_raw[:], ACT.Copy).then_inc(w_hi_done, 1)

            norm.scalar(act, 0, CHUNK if first_phase else T)
            for n in range(DK * BATCH):
                g, k = n // DK, n % DK
                if first_phase and k == 0 and g + 1 < BATCH:
                    norm.scalar(act, (g + 1) * CHUNK, CHUNK)
                if n == DK:
                    split_w1(0, 0)
                if n == 2 * DK:
                    split_w2(0, 0)
                act.wait_ge(xn_turned, n + 1)
                act.activation(xn_t[:, k, g * SEQ:(g + 1) * SEQ], ps_h[:, n // 2 % 2, n % 2, :], ACT.Copy).then_inc(xn_t_ready, 1)
            act.wait_ge(logits_t_made, 1)
            act.activation(logits_t[:], ps_o[:, 0, :], ACT.Copy).then_inc(logits_t_kept, 1)
            act.wait_ge(exp_asked, 1)
            act.activation(exp_out[:], exp_in[:], ACT.Exp).then_inc(exp_done, 1)

            def split_x(e, par, b):
                s, n = XB[b]
                act.wait_ge(x_turned, len(XB) * e + b + 1)
                act.activation(xt_hi[:, :, s * P:(s + n) * P],
                               ps_x[:, (par + b) % 2, :].rearrange("p (k c) -> p k c", k=DK)[:, :, 0:n * P],
                               ACT.Copy).then_inc(x_hi_done, 1)

            def scale(e, par, s):
                act.wait_ge(o_made, ST * e + s + 1)
                act.activation(scaled[par][:, s, :], ps_o[:, (par + s) % 2, 0:D], ACT.Copy,
                               scale=gate_now[par][:, s:s + 1]).then_inc(o_scaled, 1)

            def expert(e, par, last):
                for n in range(2 * FT):
                    f, a = n // 2, n % 2
                    act.wait_ge(h_made, 2 * FT * e + n + 1)
                    act.activation(h_hi[:, f, a * HALF:(a + 1) * HALF], ps_h[:, f % 2, a, 0:HALF], ACT.Relu).then_inc(h_hi_done, 1)
                if not last:
                    split_x(e + 1, 1 - par, 0)
                    split_x(e + 1, 1 - par, 1)
                    split_w1(e + 1, 1 - par)
                act.wait_ge(listed, e + 1)
                scale(e, par, 0)
                if not last:
                    split_x(e + 1, 1 - par, 2)
                    split_w2(e + 1, 1 - par)
                for s in range(1, ST):
                    scale(e, par, s)

            act.wait_ge(staged, 1)
            act.sem_inc(o_scaled, 2)
            for b in range(len(XB)):
                split_x(0, 0, b)

            def pair(i, last):
                expert(2 * i, 0, False)
                expert(2 * i + 1, 1, last)

            expert_loop(act, pair)

        @block.vector
        def _(v):
            chain = Chain(v, chained)

            def split_w1(e, par):
                v.wait_ge(w_hi_done, 2 * e + 1)
                v.tensor_tensor(w1_lo[par][:], w1_raw[:], w1_hi[par][:].bitcast(F32), ALU.subtract)

            def split_w2(e, par):
                v.wait_ge(w_hi_done, 2 * e + 2)
                v.tensor_tensor(w2_lo[par][:], w2_raw[:], w2_hi[par][:].bitcast(F32), ALU.subtract).then_inc(w_split, 1)

            def statistics(c):
                norm.statistics(v, chain, x_loaded[c], c * CHUNK, CHUNK)

            if first_phase:
                statistics(0)
            else:
                norm.variances(v, chain, 0, T)
                norm.inverses(v, chain, 0, T)
            for c in range(T // CHUNK):
                if first_phase:
                    if c + 1 < T // CHUNK:
                        statistics(c + 1)
                    norm.inverses(v, chain, c * CHUNK, CHUNK)
                norm.rows(v, c * CHUNK, CHUNK, normed[c])
            split_w1(0, 0)

            v.wait_ge(const.ready, 1)
            v.wait_ge(logits_made, 1)
            chain(v.tensor_copy(logits[:].rearrange("p (g j) e -> p g j e", g=BATCH),
                                ps_o[:, 1, :].rearrange("p (j g s) -> p g j s", j=SEQ // P, g=BATCH)[:, :, :, 0:E]))
            scores = logits
            for k in range(K):
                chain(v.reduce_max(top[:, k, :], scores[:], AX_X))
                chain(v.tensor_tensor(equal[:], scores[:], top[:, k, :].unsqueeze(2).broadcast_to([P, T, E]), ALU.is_equal))
                chain(v.tensor_tensor(equal[:], equal[:], const.rank[:].unsqueeze(1).broadcast_to([P, T, E]), ALU.mult))
                chain(v.reduce_max(best[:], equal[:], AX_X))
                chain(v.tensor_tensor(chosen[:, k], equal[:], best[:].unsqueeze(2).broadcast_to([P, T, E]), ALU.is_equal))
                if k == 0:
                    chain(v.scalar_tensor_tensor(others[:], chosen[:, 0], NEG, logits[:], ALU.mult, ALU.add))
                    scores = others
            v.tensor_tensor(exp_in[:, 0:T * E].rearrange("p (t e) -> p t e", e=E), logits[:],
                            top[:, 0, :].unsqueeze(2).broadcast_to([P, T, E]), ALU.subtract)
            v.tensor_tensor(exp_in[:, T * E:], top[:, 1, :], top[:, 0, :], ALU.subtract).then_inc(exp_asked, 1)
            chain(v.tensor_tensor(taken[:].rearrange("p e t -> p t e"), chosen[:, 0], chosen[:, 1], ALU.add))
            chain(v.tensor_copy(taken_bf[:], taken[:]))
            chain(v.tensor_tensor_scan(running[:], const.not_first[:].rearrange("p e t -> p (e t)"),
                                       taken[:].rearrange("p e t -> p (e t)"), 0.0, ALU.mult, ALU.add))
            v.tensor_tensor(before_bf[:].rearrange("p e t -> p (e t)"), running[:],
                            taken[:].rearrange("p e t -> p (e t)"), ALU.subtract).then_inc(taken_ready, 1)
            v.wait_ge(exp_done, 1)
            v.wait_ge(positions_made, 1)
            all_pairs = [P, K, T, E]
            ranks = ps_x[:, 0, 0:E * T].rearrange("p (e t) -> p t e", e=E)
            chain(v.tensor_tensor(product[:], chosen[:], ranks.unsqueeze(1).broadcast_to(all_pairs), ALU.mult),
                  v.tensor_tensor(start[:].rearrange("p k t e -> p (k t) e"), chosen[:].rearrange("p k t e -> p (k t) e"),
                                  const.first_tile[:].unsqueeze(1).broadcast_to([P, K * T, E]), ALU.mult),
                  v.reduce_sum(best[:], exp_out[:, 0:T * E].rearrange("p (t e) -> p t e", e=E), AX_X))
            chain(v.reduce_sum(position[:], product[:].rearrange("p k t e -> p (k t) e"), AX_X),
                  v.reduce_sum(column[:], start[:].rearrange("p k t e -> p (k t) e"), AX_X),
                  v.reciprocal(best[:], best[:]))
            chain(v.tensor_scalar(tile_no[:], position[:], float(P), None, ALU.is_ge),
                  v.tensor_scalar(over[:], position[:], float(CAP), float(2 * LC), ALU.is_ge, ALU.mult),
                  v.tensor_scalar_mul(gates[:, 0, :], best[:], 0.5))
            chain(v.scalar_tensor_tensor(tile_no[:], position[:], float(2 * P), tile_no[:], ALU.is_ge, ALU.add),
                  v.tensor_tensor(column[:], column[:], over[:], ALU.add),
                  v.tensor_tensor(gates[:, 1, :], gates[:, 0, :], exp_out[:, T * E:], ALU.mult))
            for a in range(3, ST):
                chain(v.scalar_tensor_tensor(tile_no[:], position[:], float(a * P), tile_no[:], ALU.is_ge, ALU.add))
            chain(v.scalar_tensor_tensor(in_tile[:], tile_no[:], -float(P), position[:], ALU.mult, ALU.add),
                  v.tensor_tensor(column[:], column[:], tile_no[:], ALU.add))
            pairs = [P, PART, LC]
            for h in range(PARTS):
                first = PART * h
                part = slice(first, first + PART)
                by_pair = values[:, h, 0:PART * 2 * LC].rearrange("p (n two c) -> p n two c", n=PART, two=2)
                v.tensor_tensor(of_tile[:, part], const.slot_tile[:].unsqueeze(1).broadcast_to(pairs),
                                column[:, part].unsqueeze(2).broadcast_to(pairs), ALU.is_equal).then_inc(tiles_ready, 1)
                v.wait_ge(tiles_ready, h + 1)
                v.tensor_tensor(by_pair[:, :, 1, :], of_tile[:, part],
                                gates[:].rearrange("p k t -> p (k t)")[:, part].unsqueeze(2).broadcast_to(pairs), ALU.mult)
                lanes = [P, PART, P]
                if h < PARTS - 1:
                    v.tensor_tensor(of_lane[:, part], const.lane[:].unsqueeze(1).broadcast_to(lanes),
                                    in_tile[:, part].unsqueeze(2).broadcast_to(lanes), ALU.is_equal).then_inc(lane_ready, PART)
                else:
                    for n in range(first, first + PART):
                        v.tensor_scalar(of_lane[:, n, :], const.lane[:], in_tile[:, n:n + 1], None, ALU.is_equal).then_inc(lane_ready, 1)
            by_slot = of_tile[:, 0, :]
            v.wait_ge(list_made, 1)
            v.tensor_scalar(gather_index[:], ps_x[:, 1, 0:LC], -1.0, 0.0, ALU.add, ALU.max).then_inc(rows_listed, 1)
            chain(v.tensor_scalar(by_slot, ps_x[:, 1, 0:LC], 0.5, float(FAR), ALU.is_lt, ALU.mult))
            chain(v.tensor_tensor(by_slot, by_slot, ps_x[:, 1, 0:LC], ALU.add))
            chain(v.tensor_scalar_add(add_index[:], by_slot, -1.0))
            v.tensor_copy(gate[:], ps_x[:, 1, LC:2 * LC]).then_inc(list_kept, 1)

            def split_x(e, par, b):
                s, n = XB[b]
                v.wait_ge(x_hi_done, len(XB) * e + b + 1)
                v.tensor_tensor(xt_lo[:, :, s * P:(s + n) * P],
                                ps_x[:, (par + b) % 2, :].rearrange("p (k c) -> p k c", k=DK)[:, :, 0:n * P],
                                xt_hi[:, :, s * P:(s + n) * P].bitcast(F32), ALU.subtract).then_inc(x_split, 1)

            v.sem_inc(h_split, 4)
            v.sem_inc(x_split, 2)
            split_w2(0, 0)
            for b in range(len(XB)):
                split_x(0, 0, b)

            def expert(e, par, last):
                for n in range(2 * FT):
                    f, a = n // 2, n % 2
                    v.wait_ge(h_hi_done, 2 * FT * e + n + 1)
                    v.scalar_tensor_tensor(h_lo[:, f, a * HALF:(a + 1) * HALF], ps_h[:, f % 2, a, 0:HALF], 0.0,
                                           h_hi[:, f, a * HALF:(a + 1) * HALF].bitcast(F32),
                                           ALU.max, ALU.subtract).then_inc(h_split, 1)
                if not last:
                    split_x(e + 1, 1 - par, 0)
                    split_x(e + 1, 1 - par, 1)
                    split_w1(e + 1, 1 - par)
                    split_x(e + 1, 1 - par, 2)
                    split_w2(e + 1, 1 - par)

            def pair(i, last):
                expert(2 * i, 0, False)
                expert(2 * i + 1, 1, last)

            expert_loop(v, pair)

        @block.tensor
        def _(pe):
            pe.wait_ge(const.ready, 1)

            def group_logits(g):
                if g == 0:
                    pe.wait_ge(wg_loaded, 16)
                pe.wait_ge(xn_t_ready, DK * (g + 1))
                for k in range(DK):
                    last = pe.matmul(ps_o[32 * g:32 * g + 32, 0, :], wg[:, k, :], xn_t[:, k, g * SEQ:(g + 1) * SEQ],
                                     start=(k == 0), stop=(k == DK - 1), skip_group_check=True)
                return last

            for g in range(BATCH):
                pe.wait_ge(normed[g], CHUNK)
                for k in range(DK):
                    n = DK * g + k
                    if n >= 4:
                        pe.wait_ge(xn_t_ready, n - 3)
                    for j in range(SEQ // P):
                        last = pe.transpose(ps_h[:, n // 2 % 2, n % 2, j * P:(j + 1) * P],
                                            xn[:, g * (SEQ // P) + j, k * P:(k + 1) * P], const.identity[:])
                    last.then_inc(xn_turned, 1)
                if g > 0:
                    group_logits(g - 1)
            group_logits(BATCH - 1).then_inc(logits_t_made, 1)
            pe.wait_ge(logits_t_kept, 1)
            for j in range(SEQ // P):
                last = pe.transpose(ps_o[:, 1, j * P:(j + 1) * P], logits_t[:, j * P:(j + 1) * P], const.identity[:])
            last.then_inc(logits_made, 1)
            pe.wait_ge(taken_ready, 1)
            pe.matmul(ps_x[:, 0, 0:E * T], const.earlier[:], taken_bf[:].rearrange("p e t -> p (e t)"), start=True, stop=False)
            pe.matmul(ps_x[:, 0, 0:E * T], const.ones[:], before_bf[:].rearrange("p e t -> p (e t)"),
                      start=False, stop=True).then_inc(positions_made, 1)
            pe.wait_ge(pads_clear, 1)
            for n in range(K * T):
                if n % PART == 0:
                    pe.wait_ge(tokens_ready, n // PART + 1)
                pe.wait_ge(lane_ready, n + 1)
                last = pe.matmul(ps_x[:, 1, 0:P], of_lane[:, n, :], values[:, n // PART, n % PART * 2 * LC:n % PART * 2 * LC + P],
                                 start=(n == 0), stop=(n == K * T - 1))
            last.then_inc(list_made, 1)

            def turn_x(i, par, batches):
                e = 2 * i + par
                for b in batches:
                    s0, n = XB[b]
                    pe.wait_ge(gathered[par][b], 16 * n * (i + 1))
                    pe.wait_ge(x_split, len(XB) * e + b + 1)
                    for k in range(DK):
                        for s in range(n):
                            at = k * 2 * P + s * P
                            last = pe.transpose(ps_x[:, (par + b) % 2, at:at + P],
                                                xg[par][:, s0 + s, k * P:(k + 1) * P], const.identity[:])
                    last.then_inc(x_turned, 1)

            def expert(i, par, last_one):
                e = 2 * i + par
                pe.wait_ge(w_split, e + 1)
                pe.wait_ge(x_split, len(XB) * (e + 1) + 2)
                for f in range(FT):
                    pe.wait_ge(h_split, 2 * (FT * e + f + 1))
                    fs = slice(f * P, (f + 1) * P)
                    for a in range(2):
                        cs = slice(a * HALF, (a + 1) * HALF)
                        parts = [(w1_hi[par][:, k, fs], xt_hi[:, k, cs]) for k in range(DK)]
                        parts += [(w1_hi[par][:, k, fs], xt_lo[:, k, cs]) for k in range(DK)]
                        parts += [(w1_lo[par][:, k, fs], xt_hi[:, k, cs]) for k in range(DK)]
                        for n, (w, m) in enumerate(parts):
                            last = pe.matmul(ps_h[:, f % 2, a, 0:HALF], w, m, start=(n == 0), stop=(n == len(parts) - 1))
                        last.then_inc(h_made, 1)
                if not last_one:
                    turn_x(i + par, 1 - par, (0, 1))
                for s in range(ST):
                    pe.wait_ge(o_scaled, ST * e + s + 1)
                    cs = slice(s * P, (s + 1) * P)
                    for f in range(FT):
                        if s == 0:
                            pe.wait_ge(h_split, 2 * (FT * e + f + 3))
                        for n, (h, w) in enumerate(((h_hi, w2_hi), (h_hi, w2_lo), (h_lo, w2_hi))):
                            last = pe.matmul(ps_o[:, (par + s) % 2, 0:D], h[:, f, cs], w[par][:, f, :],
                                             start=(f == 0 and n == 0), stop=(f == FT - 1 and n == 2))
                    last.then_inc(o_made, 1)
                    if s == 0 and not last_one:
                        turn_x(i + par, 1 - par, (2,))

            pe.wait_ge(list_kept, 1)
            turn_x(0, 0, range(len(XB)))

            def pair(i, last):
                expert(i, 0, False)
                expert(i, 1, last)

            expert_loop(pe, pair)


def attention(nc, const, x, stats, x_rows, out_rows, w_qkv, w_o, rows_stored):
    HEADS, HD, STACK = 16, 16, 64
    UNIT_HEADS = HEADS // 2
    PAIRS = UNIT_HEADS // 2
    QT = SEQ // P
    GROUP = 4
    MAX_ROW = 3 * HD
    KEY_TILES = [(kt, min(kt * P, SEQ - 2 * P)) for kt in range(QT)]
    WIDTH = sum(SEQ - q0 for _, q0 in KEY_TILES)
    WIDE = (SEQ - KEY_TILES[0][1]) + (SEQ - KEY_TILES[1][1])
    SCORES = [(qt, (h, h + 1)) for qt in (0, 1) for h in range(0, UNIT_HEADS, 2)]
    SCORES += [(qt, (h,)) for qt in (2, 3) for h in range(UNIT_HEADS)]
    LEAD = [("project", 0), ("project", 1)]
    BESIDE = [[("turn", 0)], [("project", 2)], [("turn", 1)], [("project", 3), 0, 1], [("turn", 2), 2, 3], [4, 5],
              [("turn", 3), 6, 7], [8, 9], [10, 11, 12], [13, 14], [15, 16, 17], [18, 19], [20, 21], [22, 23], [], []]
    BESIDE = [[("scores", w) if isinstance(w, int) else w for w in beside] for beside in BESIDE]
    assert len(BESIDE) == 2 * UNIT_HEADS
    VALUES_AFTER = [8, 9, 10, 11]
    OUTPUTS_AFTER = 13
    MAXIMA_AFTER = 15
    PROJECT_AFTER = [2, 1, 3, 5]
    STATISTICS_AFTER = 15
    QKV, TURN, SCORED = {}, {}, {}
    USES = 0
    for what, n in LEAD + sum(BESIDE, []):
        {"project": QKV, "turn": TURN, "scores": SCORED}[what][n] = USES
        USES += 2 if what == "turn" else 1
    BANKS = 3
    assert USES % BANKS == 0
    K_TURNS = [k + 1 for k in TURN.values()]
    BY_VECTOR = [k for k in range(USES) if k not in K_TURNS]
    KEPT = len(BY_VECTOR)
    NORM_AFTER = {1: 1, 4: 2, 9: 3}
    TURN_ROWS_AFTER = {5: 1, 10: 2, 16: 3}

    def kept_after(u, k):
        return KEPT * u + sum(j <= k for j in BY_VECTOR) + BANKS

    TAIL = ["outputs00", "maxima1", "outputs01", "heads0", "outputs10", "maxima0", "outputs11", "heads1", "out0", "out1"]

    def tail_number(b, use):
        at = TAIL.index(use)
        if b is LAST and at > TAIL.index("maxima0"):
            at -= 1
        return len(TAIL) * b + at + 1

    def maxima_number(b, hh):
        if hh == 1:
            return tail_number(b, "maxima1")
        return 0 if b is FIRST else tail_number(b - 1, "maxima0")

    FIRST, LAST = 0, BATCH - 1

    with ExitStack() as stack:
        enter = stack.enter_context

        def sb(name, shape, dtype=F32, enter=enter):
            return enter(nc.sbuf_tensor(f"at_{name}", shape, dtype))

        def sem(name):
            return enter(nc.semaphore(f"at_{name}"))

        w_hi = sb("w_hi", [P, 16, P], F32R)
        w_lo = sb("w_lo", [P, 16, P], F32R)
        xt = sb("xt", [P, 2, DK, SEQ], F32R)
        row_stack = [sb(f"row_stack{i}", [P, 2, UNIT_HEADS, STACK]) for i in range(2)]
        q_stack = [sb(f"q_stack{i}", [P, PAIRS, SEQ], F32R) for i in range(2)]
        k_stack = [sb(f"k_stack{i}", [P, 2, PAIRS, SEQ], F32R) for i in range(2)]
        v_ones = [sb(f"v_ones{i}", [P, QT, UNIT_HEADS, 32]) for i in range(2)]
        maxima = sb("maxima", [P, QT, 2, PAIRS])
        minus_max = sb("minus_max", [P, QT, 2, 2, PAIRS])
        max_t = sb("max_t", [4 * PAIRS, SEQ])
        xt_all = sb("xt_all", [P, 2, DK, TOK - SEQ], F32R)
        norm = Norm(nc, enter, enter, "at", x, x, stats)
        probs = [sb(f"probs{i}", [P, GROUP, WIDTH]) for i in range(2)]
        w_raw = probs[0][:].rearrange("p g c -> p (g c)")[:, 0:8 * D].rearrange("p (i c) -> p i c", c=D)
        o_t = [sb(f"o_t{i}", [P, SEQ]) for i in range(2)]
        inverse = sb("inverse_sum", [P, QT, GROUP])
        heads_out = sb("heads_out", [P, QT, D])
        heads_t_hi = sb("heads_t_hi", [P, DK, SEQ], F32R)
        heads_t_lo = sb("heads_t_lo", [P, DK, SEQ], F32R)
        x_now = sb("x_now", [P, QT, D])

        ps_keys = enter(nc.psum_tensor("at_ps_keys", [P, 3 * 512], F32))
        ps_pv = enter(nc.psum_tensor("at_ps_pv", [P, 512], F32))
        ps_4 = enter(nc.psum_tensor("at_ps_4", [P, 4, 512], F32))

        def front_bank(use):
            return ps_4[:, use % BANKS, :]

        tail_bank = ps_4[:, BANKS, :]

        def early_part(n, part):
            if n < 4:
                return (w_hi, w_lo)[part][:, 4 * n:4 * n + 4, :].rearrange("p a c -> p (a c)")
            g, k = (n - 4) // DK, n % DK
            return xt[:, part, k, :] if g == 0 else xt_all[:, part, k, (g - 1) * SEQ:g * SEQ]

        def early_bank(n):
            return ps_4[:, n, :] if n < 4 else ps_keys[:, (n - 4) % 3 * 512:((n - 4) % 3 + 1) * 512]

        def rows_turns(g):
            return range(4 + DK * g, 4 + DK * (g + 1))

        def keys_columns(half):
            return ps_keys[:, 0:WIDE] if half == 0 else ps_keys[:, 1024:1024 + WIDTH - WIDE]

        x_loaded = [sem(f"x_loaded{c}") for c in range(BATCH)]
        normed = [sem(f"normed{g}") for g in range(BATCH)]
        w_loaded, early_made, early_hi, early_kept = (
            sem("w_loaded"), sem("early_made"), sem("early_hi"), sem("early_kept"))
        filled, stacks_ready, v_ready, k_ready = sem("filled"), sem("stacks_ready"), sem("v_ready"), sem("k_ready")
        chained = sem("chained")
        xt_loaded, x_now_loaded = sem("xt_loaded"), sem("x_now_loaded")
        front_made, front_kept = sem("front_made"), sem("front_kept")
        v_kept, hi_done, stacked, k_turned = sem("v_kept"), sem("hi_done"), sem("stacked"), sem("k_turned")
        minus_hi, minus_ready, max_t_ready, max_in = sem("minus_hi"), sem("minus_ready"), sem("max_t_ready"), sem("max_in")
        keys_made, exped, cleared, pv_made, o_t_kept = (
            sem("keys_made"), sem("exped"), sem("cleared"), sem("pv_made"), sem("o_t_kept"))
        tail_made, tail_kept, inverse_done, heads_hi, out_ready = (
            sem("tail_made"), sem("tail_kept"), sem("inverse_done"), sem("heads_hi"), sem("out_ready"))
        turn_taken = sem("turn_taken")
        block = enter(nc.Block())

        def unit_loop(engine, front, step, finish):
            front(FIRST, 0)
            step(FIRST, 0, FIRST, 1, None)
            with engine.Fori(0, BATCH - 1) as b:
                step(b, 1, b + 1, 0, b)
                step(b + 1, 0, b + 1, 1, b)
            step(LAST, 1, None, None, LAST)
            finish(LAST)

        def front_alone(do, norm_rows, turn_rows):
            for i, (what, n) in enumerate(LEAD + sum(BESIDE, [])):
                do(what, n)
                if i in NORM_AFTER:
                    norm_rows(NORM_AFTER[i])
                if i in TURN_ROWS_AFTER:
                    turn_rows(TURN_ROWS_AFTER[i])

        @block.sync
        def _(sp):
            def load_rows(g):
                sp.dma_start(x[:, QT * g:QT * (g + 1), :], row_tiles(x_rows, QT * g, QT)).then_inc(x_loaded[g], 16)

            load_rows(0)
            sp.dma_start(w_raw[:, 0:6, :], w_qkv.rearrange("(i p) c -> p i c", p=P)).then_inc(w_loaded, 16)
            sp.dma_start(w_raw[:, 6:8, :], w_o.rearrange("(i p) c -> p i c", p=P)).then_inc(w_loaded, 16)
            for g in range(1, BATCH):
                load_rows(g)

            def rows_of(table, b):
                return table[bass.ds(b * SEQ, SEQ), :].rearrange("(t p) c -> p t c", p=P)

            def load_xt(b):
                sp.wait_ge(front_made, USES * (2 * b - 1) + QKV[QT - 1] + 1)
                sp.dma_start(xt[:].rearrange("p a k c -> p (a k) c").bitcast(F32),
                             xt_all[:, :, :, bass.ds((b - 1) * SEQ, SEQ)].rearrange("p a k c -> p (a k) c").bitcast(F32)
                             ).then_inc(xt_loaded, 16)

            def insert_max(b, hh):
                sp.wait_ge(max_t_ready, 2 * b + hh + 1)
                for odd in range(2):
                    for c in range(2):
                        row = odd * STACK + MAX_ROW + c
                        sp.dma_start(q_stack[hh][row:row + 1, :, :].bitcast(F32),
                                     max_t[(2 * odd + c) * PAIRS:(2 * odd + c + 1) * PAIRS, :]).then_inc(max_in, 16)

            def store(b):
                sp.wait_ge(out_ready, b + 1)
                sp.dma_start(rows_of(out_rows, b), x[:, bass.ds(QT * b, QT), :]).then_inc(rows_stored, 16)

            def load_x(b):
                sp.dma_start(x_now[:], rows_of(x_rows, b)).then_inc(x_now_loaded, 16)

            def batch(b, next_xt):
                insert_max(b, 0)
                if next_xt:
                    load_xt(b + 1)
                store(b - 1)
                load_x(b)
                insert_max(b, 1)

            sp.sem_inc(max_in, 64)
            load_x(FIRST)
            insert_max(FIRST, 0)
            sp.wait_ge(early_kept, 12)
            load_xt(1)
            insert_max(FIRST, 1)
            with sp.Fori(1, LAST) as b:
                batch(b, True)
            batch(LAST, False)
            store(LAST)

        @block.gpsimd
        def _(pool):
            for i in range(2):
                pool.memset(row_stack[i][:], 0.0).then_inc(filled, 1)
            for i in range(2):
                pool.memset(v_ones[i][:], 0.0).then_inc(filled, 1)
            pool.wait_ge(filled, 2)
            for i in range(2):
                pool.memset(row_stack[i][:, 1, :, MAX_ROW:MAX_ROW + 2], 1.0).then_inc(stacks_ready, 1)
            pool.wait_ge(filled, 4)
            for i in range(2):
                pool.memset(v_ones[i][:, :, :, HD:HD + 1], 1.0).then_inc(v_ready, 1)
            for i in range(2):
                pool.memset(k_stack[i][:].rearrange("p a b c -> p (a b c)").bitcast(F32), 0.0).then_inc(k_ready, 1)

            def front(b, hh):
                for t in range(QT):
                    stack_of = row_stack[t % 2]
                    pool.wait_ge(hi_done, QT * (2 * b + hh) + t + 1)
                    pool.sem_inc(turn_taken, 1)
                    pool.tensor_copy(stack_of[:, 0, :, HD:2 * HD], stack_of[:, 0, :, 0:HD])
                    pool.tensor_copy(stack_of[:, 1, :, 2 * HD:3 * HD], stack_of[:, 1, :, 0:HD]).then_inc(stacked, 1)

            def clear(b, hh, g, kt):
                heads = GROUP if g == 0 else GROUP - 1
                at = sum(SEQ - q0 for _, q0 in KEY_TILES[:kt]) + kt * P - KEY_TILES[kt][1]
                pool.wait_ge(exped, 2 * UNIT_HEADS * (2 * b + hh) + 2 * GROUP * g + 2 * (heads - 1) + kt // 2 + 3)
                pool.sem_inc(turn_taken, 1)
                pool.affine_select(probs[g][:, 0:heads, at:at + P], probs[g][:, 0:heads, at:at + P], [[0, heads], [1, P]],
                                   ALU.is_ge, 0.0, base=0, channel_multiplier=-1).then_inc(cleared, 1)

            def step(b, hh, next_b, next_hh, last_b):
                if next_b is not None:
                    front(next_b, next_hh)
                for g in range(2):
                    for kt in range(QT):
                        clear(b, hh, g, kt)

            unit_loop(pool, front, step, lambda b: None)

        @block.scalar
        def _(act):
            def early(n):
                act.wait_ge(early_made, n + 1)
                act.activation(early_part(n, 0), early_bank(n), ACT.Copy).then_inc(early_hi, 1)

            norm.scalar(act, 0, QT)
            for n in range(4):
                early(n)
            for n in rows_turns(0):
                early(n)
            norm.scalar(act, QT, QT)
            act.wait_ge(stacks_ready, 2)
            act.wait_ge(v_ready, 2)
            act.wait_ge(k_ready, 2)

            def project(u, hh, t):
                act.wait_ge(front_made, USES * u + QKV[t] + 1)
                bank = front_bank(QKV[t])
                act.activation(row_stack[t % 2][:, :, :, 0:HD].rearrange("p a h c -> p (a h) c").bitcast(F32R),
                               bank[:, 0:2 * P].rearrange("p (h c) -> p h c", c=HD), ACT.Copy).then_inc(hi_done, 1)
                act.activation(v_ones[hh][:, t, :, 0:HD], bank[:, 2 * P:3 * P].rearrange("p (h c) -> p h c", c=HD),
                               ACT.Copy).then_inc(v_kept, 1)

            def turn(u, hh, t):
                at = slice(t * P, (t + 1) * P)
                act.wait_ge(front_made, USES * u + TURN[t] + 2)
                for odd in range(2):
                    rows = slice(odd * STACK, (odd + 1) * STACK)
                    last = act.activation(k_stack[hh][rows, odd, :, at],
                                          front_bank(TURN[t] + 1)[rows, :].rearrange("p (a c) -> p a c", c=P), ACT.Copy)
                last.then_inc(k_turned, 1)

            def do(u, hh, what, n):
                if what == "project":
                    project(u, hh, n)
                if what == "turn":
                    turn(u, hh, n)

            def exps(b, hh, i):
                h, half = i // 2, i % 2
                columns = slice(0, WIDE) if half == 0 else slice(WIDE, WIDTH)
                act.wait_ge(keys_made, 2 * UNIT_HEADS * (2 * b + hh) + i + 1)
                act.activation(probs[h // GROUP][:, h % GROUP, columns], keys_columns(half), ACT.Exp,
                               scale=float(HD) ** -0.5).then_inc(exped, 1)

            def keep_o_t(b, hh, g):
                act.wait_ge(pv_made, 2 * (2 * b + hh) + g + 1)
                act.activation(o_t[g][:], ps_pv[:], ACT.Copy).then_inc(o_t_kept, 1)

            def norm_rows(g):
                if g + 1 < BATCH:
                    norm.scalar(act, QT * (g + 1), QT)

            def front(b, hh):
                front_alone(lambda what, n: do(2 * b + hh, hh, what, n), norm_rows,
                            lambda g: [early(n) for n in rows_turns(g)])

            def keep_heads(b, k):
                act.wait_ge(tail_made, tail_number(b, f"heads{k}") + 1)
                act.activation(heads_t_hi[:, k, :], tail_bank, ACT.Copy).then_inc(heads_hi, 1)

            def step(b, hh, next_b, next_hh, last_b):
                def beside(work):
                    if next_b is not None:
                        for what, n in work:
                            do(2 * next_b + next_hh, next_hh, what, n)

                if last_b is not None:
                    keep_o_t(last_b, 1 - hh, 1)
                beside(LEAD)
                for i in range(2 * UNIT_HEADS):
                    exps(b, hh, i)
                    beside(BESIDE[i])
                    if i == OUTPUTS_AFTER - 1:
                        keep_o_t(b, hh, 0)
                    if last_b is not None and i == PROJECT_AFTER[1 - hh]:
                        keep_heads(last_b, 1 - hh)

            def finish(b):
                keep_o_t(b, 1, 1)
                keep_heads(b, 1)

            act.sem_inc(exped, 2)
            act.sem_inc(o_t_kept, 1)
            unit_loop(act, front, step, finish)



        @block.vector
        def _(v):
            chain = Chain(v, chained)

            def norm_rows(g):
                norm.inverses(v, chain, QT * g, QT)
                norm.rows(v, QT * g, QT, normed[g])
                if g + 1 < BATCH:
                    norm.statistics(v, chain, x_loaded[g + 1], QT * (g + 1), QT)

            def early(n):
                v.wait_ge(early_hi, n + 1)
                v.tensor_tensor(early_part(n, 1), early_bank(n), early_part(n, 0).bitcast(F32), ALU.subtract).then_inc(early_kept, 1)

            norm.statistics(v, chain, x_loaded[0], 0, QT)
            norm.inverses(v, chain, 0, QT)
            norm.rows(v, 0, QT, normed[0])
            for n in (*range(4), *rows_turns(0)):
                early(n)
            v.sem_inc(front_kept, BANKS)
            norm.statistics(v, chain, x_loaded[1], QT, QT)
            v.wait_ge(stacks_ready, 2)

            def project(u, hh, t):
                bank = front_bank(QKV[t])
                stack_of = row_stack[t % 2]
                v.wait_ge(v_kept, QT * u + t + 1)
                v.tensor_tensor(stack_of[:, 0, :, 2 * HD:3 * HD], bank[:, 0:P].rearrange("p (h c) -> p h c", c=HD),
                                stack_of[:, 0, :, 0:HD], ALU.subtract)
                v.tensor_tensor(stack_of[:, 1, :, HD:2 * HD], bank[:, P:2 * P].rearrange("p (h c) -> p h c", c=HD),
                                stack_of[:, 1, :, 0:HD], ALU.subtract).then_inc(front_kept, 1)

            def turn(u, hh, t):
                v.wait_ge(front_made, USES * u + TURN[t] + 1)
                v.tensor_copy(q_stack[hh][:, :, t * P:(t + 1) * P],
                              front_bank(TURN[t]).rearrange("p (a c) -> p a c", c=P)).then_inc(front_kept, 1)

            def maximum(u, hh, n):
                qt, heads = SCORES[n]
                bank = front_bank(SCORED[n])
                v.wait_ge(front_made, USES * u + SCORED[n] + 1)
                if len(heads) == 2:
                    v.reduce_max(maxima[:, qt, :, heads[0] // 2],
                                 bank.rearrange("p (a c) -> p a c", a=2)[:, :, 0:(qt + 1) * P], AX_X).then_inc(front_kept, 1)
                else:
                    h = heads[0]
                    v.reduce_max(maxima[:, qt, h % 2, h // 2:h // 2 + 1], bank[:, 0:(qt + 1) * P], AX_X).then_inc(front_kept, 1)

            def negate(b, hh):
                u = 2 * b + hh
                most = maxima[:].rearrange("p q o a -> p (q o) a")
                hi = minus_max[:, :, :, 0, :].rearrange("p q o a -> p (q o) a")
                lo = minus_max[:, :, :, 1, :].rearrange("p q o a -> p (q o) a")
                v.wait_ge(front_kept, kept_after(u, USES - 1))
                v.tensor_scalar_mul(hi.bitcast(F32R), most, -1.0).then_inc(minus_hi, 1)
                v.wait_ge(minus_hi, u + 1)
                v.scalar_tensor_tensor(lo, most, -1.0, hi, ALU.mult, ALU.subtract).then_inc(minus_ready, 1)
                v.wait_ge(max_in, 64 * (u + 1))
                v.wait_ge(tail_made, maxima_number(b, hh) + 1)
                v.tensor_copy(max_t[:], tail_bank[0:4 * PAIRS, :]).then_inc(tail_kept, 1)
                v.wait_ge(tail_kept, maxima_number(b, hh) + 1)
                v.sem_inc(max_t_ready, 1)

            def do(u, hh, what, n):
                {"project": project, "turn": turn, "scores": maximum}[what](u, hh, n)

            def divide(b, hh, g):
                number = tail_number(b, f"outputs{hh}{g}")
                v.wait_ge(tail_made, number + 1)
                v.wait_ge(tail_kept, number)
                by_head = tail_bank.rearrange("p (q h c) -> p q h c", q=QT, h=GROUP)
                v.reciprocal(inverse[:], by_head[:, :, :, HD]).then_inc(inverse_done, 1)
                v.wait_ge(inverse_done, 2 * (2 * b + hh) + g + 1)
                columns = heads_out[:, :, (2 * hh + g) * GROUP * HD:(2 * hh + g + 1) * GROUP * HD]
                v.tensor_tensor(columns.rearrange("p q (h c) -> p q h c", h=GROUP), by_head[:, :, :, 0:HD],
                                inverse[:].unsqueeze(3).broadcast_to([P, QT, GROUP, HD]), ALU.mult).then_inc(tail_kept, 1)

            def front(b, hh):
                front_alone(lambda what, n: do(2 * b + hh, hh, what, n),
                            norm_rows,
                            lambda g: [early(n) for n in rows_turns(g)])
                negate(b, hh)

            def split_heads(b, k):
                v.wait_ge(heads_hi, DK * b + k + 1)
                v.tensor_tensor(heads_t_lo[:, k, :], tail_bank, heads_t_hi[:, k, :].bitcast(F32), ALU.subtract).then_inc(tail_kept, 1)

            def add_out(b, n):
                if n == 0:
                    v.wait_ge(x_now_loaded, 16 * (b + 1))
                v.wait_ge(tail_made, tail_number(b, f"out{n}") + 1)
                v.tensor_tensor(x[:, bass.ds(QT * b + 2 * n, 2), :].rearrange("p q c -> p (q c)"), tail_bank,
                                x_now[:, 2 * n:2 * n + 2, :].rearrange("p q c -> p (q c)"), ALU.add).then_inc(tail_kept, 1)
                if n == 1:
                    v.wait_ge(tail_kept, tail_number(b, "out1") + 1)
                    v.sem_inc(out_ready, 1)

            def statistics(b):
                for t in range(QT):
                    v.bn_stats(stats[:, bass.ds(QT * b + t, 1), :].rearrange("p o c -> p (o c)"),
                               x[:, bass.ds(QT * b + t, 1), :].rearrange("p o c -> p (o c)"))

            PROJECTION = [(split_heads, 0), (split_heads, 1), (add_out, 0), (add_out, 1)]

            def step(b, hh, next_b, next_hh, last_b):
                def beside(work):
                    if next_b is not None:
                        for what, n in work:
                            do(2 * next_b + next_hh, next_hh, what, n)

                beside(LEAD)
                if last_b is not None:
                    divide(last_b, 1 - hh, 1)
                for i in range(2 * UNIT_HEADS):
                    beside(BESIDE[i])
                    if i == OUTPUTS_AFTER:
                        divide(b, hh, 0)
                    if i == MAXIMA_AFTER and next_b is not None:
                        negate(next_b, next_hh)
                    if i == STATISTICS_AFTER and hh == 0 and last_b is not None:
                        statistics(last_b)
                    if last_b is not None and i in (PROJECT_AFTER[1:] if hh == 0 else PROJECT_AFTER[:1]):
                        part, n = PROJECTION[PROJECT_AFTER.index(i)]
                        part(last_b, n)

            def finish(b):
                divide(b, 1, 1)
                for part, n in PROJECTION[1:]:
                    part(b, n)
                statistics(b)

            unit_loop(v, front, step, finish)

        @block.tensor
        def _(pe):
            def early(n):
                g, k = (n - 4) // DK, n % DK
                if n >= 4:
                    pe.wait_ge(normed[g], QT)
                if n >= 7:
                    pe.wait_ge(early_kept, n - 2)
                for j in range(4):
                    if n < 3:
                        k, half, which = (4 * n + j) // 6, (4 * n + j) // 3 % 2, (4 * n + j) % 3
                        block_in = w_raw[:, 2 * which + half, k * P:(k + 1) * P]
                    elif n == 3:
                        block_in = w_raw[:, 6 + j % 2, j // 2 * P:(j // 2 + 1) * P]
                    else:
                        block_in = x[:, g * QT + j, k * P:(k + 1) * P]
                    last = pe.transpose(early_bank(n)[:, j * P:(j + 1) * P], block_in, const.identity[:])
                last.then_inc(early_made, 1)

            pe.wait_ge(w_loaded, 32)
            for n in (*range(4), *rows_turns(0)):
                early(n)
            pe.wait_ge(early_kept, 6)

            def three(out, hi_hi, hi_lo, lo_hi, first=True, end=True):
                for n, (w, m) in enumerate((hi_hi, hi_lo, lo_hi)):
                    last = pe.matmul(out, w, m, start=(first and n == 0), stop=(end and n == 2))
                return last

            def use(u, k, kept=-1):
                before = k - BANKS
                if before in K_TURNS:
                    pe.wait_ge(k_turned, QT * u + K_TURNS.index(before) + 1)
                elif before >= 0:
                    kept = max(kept, before)
                elif kept < 0:
                    pe.wait_ge(front_kept, KEPT * u + k + 1)
                if kept >= 0:
                    pe.wait_ge(front_kept, kept_after(u, kept))

            def project(u, hh, t):
                use(u, QKV[t])
                out = front_bank(QKV[t])[:, 0:3 * P]
                at = slice(t * P, (t + 1) * P)
                for k in range(DK):
                    tiles = slice((2 * k + hh) * 3, (2 * k + hh + 1) * 3)
                    hi, lo = (w[:, tiles, :].rearrange("p a c -> p (a c)") for w in (w_hi, w_lo))
                    last = three(out, (xt[:, 0, k, at], hi), (xt[:, 0, k, at], lo), (xt[:, 1, k, at], hi),
                                 first=(k == 0), end=(k == DK - 1))
                last.then_inc(front_made, 1)

            def turn(u, hh, t):
                pe.wait_ge(stacked, QT * u + t + 1)
                for part in range(2):
                    use(u, TURN[t] + part, QKV[t] if part == 0 else -1)
                    for a in range(PAIRS):
                        last = pe.transpose(front_bank(TURN[t] + part)[:, a * P:(a + 1) * P],
                                            row_stack[t % 2][:, part, 2 * a:2 * a + 2, :].rearrange("p h c -> p (h c)"),
                                            const.identity[:])
                    last.then_inc(front_made, 1)

            def scores(u, hh, n):
                qt, heads = SCORES[n]
                tiles = max(2, qt + 1)
                if n == 0 or SCORES[n - 1][0] != qt:
                    pe.wait_ge(k_turned, QT * u + tiles)
                    use(u, SCORED[n], TURN[tiles - 1])
                else:
                    use(u, SCORED[n])
                keys = max(2 * P, (qt + 1) * P)
                for i, h in enumerate(heads):
                    out = front_bank(SCORED[n])[:, i * keys:(i + 1) * keys]
                    pe.matmul(out, q_stack[hh][:, h // 2, qt * P:(qt + 1) * P], k_stack[hh][:, h % 2, h // 2, 0:keys],
                              start=True, stop=False)
                    last = pe.matmul(out[:, qt * P:(qt + 1) * P], const.identity_bf[:], const.hide_later[:], start=False, stop=True)
                last.then_inc(front_made, 1)

            def turn_max(b, hh):
                pe.wait_ge(minus_ready, 2 * b + hh + 1)
                if b is not FIRST or hh > 0:
                    pe.wait_ge(tail_kept, maxima_number(b, hh))
                for qt in range(QT):
                    last = pe.transpose(tail_bank[0:4 * PAIRS, qt * P:(qt + 1) * P],
                                        minus_max[:, qt].rearrange("p o c a -> p (o c a)"), const.identity[:])
                last.then_inc(tail_made, 1)

            def do(u, hh, what, n):
                if what == "project" and n == 0 and hh == 0 and u is not FIRST:
                    pe.wait_ge(xt_loaded, 8 * u)
                {"project": project, "turn": turn, "scores": scores}[what](u, hh, n)

            def key_scores(b, hh, i):
                h, half = i // 2, i % 2
                q, k = q_stack[hh][:, h // 2, :], k_stack[hh][:, h % 2, h // 2, :]
                pe.wait_ge(exped, 2 * UNIT_HEADS * (2 * b + hh) + i + 1)
                for j, (kt, q0) in enumerate(KEY_TILES[2 * half:2 * half + 2]):
                    at = 512 * j if half == 0 else 1024 + 256 * j
                    out = ps_keys[:, at:at + SEQ - q0]
                    here = h == UNIT_HEADS - 1
                    last = pe.matmul(out, k[:, kt * P:(kt + 1) * P], q[:, q0:SEQ], start=True, stop=not here)
                    if here:
                        last = pe.matmul(out[:, kt * P - q0:(kt + 1) * P - q0], const.identity_bf[:], const.hide_later_t[:],
                                         start=False, stop=True)
                last.then_inc(keys_made, 1)

            def values(b, hh, g, kt):
                u = 2 * b + hh
                if kt == 0:
                    if g == 1:
                        pe.wait_ge(exped, 2 * UNIT_HEADS * (u + 1) + 2)
                    pe.wait_ge(o_t_kept, 2 * u + g + 1)
                pe.wait_ge(cleared, 2 * QT * u + QT * g + kt + 1)
                at = sum(SEQ - q0 for _, q0 in KEY_TILES[:kt])
                q0 = KEY_TILES[kt][1]
                for j in range(GROUP):
                    last = pe.matmul(ps_pv[32 * j:32 * j + 32, kt * P:SEQ], v_ones[hh][:, kt, g * GROUP + j, :],
                                     probs[g][:, j, at + kt * P - q0:at + SEQ - q0], start=(kt == 0), stop=(kt == QT - 1),
                                     skip_group_check=True)
                if kt == QT - 1:
                    last.then_inc(pv_made, 1)

            def all_values(b, hh):
                for kt in range(QT):
                    values(b, hh, 1, kt)

            def turn_o(b, hh, g):
                pe.wait_ge(o_t_kept, 2 * (2 * b + hh) + g + 2)
                pe.wait_ge(tail_kept, tail_number(b, f"outputs{hh}{g}"))
                for qt in range(QT):
                    last = pe.transpose(tail_bank[:, qt * P:(qt + 1) * P], o_t[g][:, qt * P:(qt + 1) * P], const.identity[:])
                last.then_inc(tail_made, 1)

            def turn_heads(b, k):
                pe.wait_ge(tail_kept, tail_number(b, f"heads{k}"))
                for qt in range(QT):
                    last = pe.transpose(tail_bank[:, qt * P:(qt + 1) * P], heads_out[:, qt, k * P:(k + 1) * P],
                                        const.identity[:])
                last.then_inc(tail_made, 1)

            def project_out(b, n):
                pe.wait_ge(tail_kept, tail_number(b, f"out{n}"))
                for i in range(2):
                    at = slice((2 * n + i) * P, (2 * n + i + 1) * P)
                    for k in range(DK):
                        hi, lo = (w[:, 12 + 2 * k:14 + 2 * k, :].rearrange("p a c -> p (a c)") for w in (w_hi, w_lo))
                        last = three(tail_bank[:, i * D:(i + 1) * D], (heads_t_hi[:, k, at], hi),
                                     (heads_t_hi[:, k, at], lo), (heads_t_lo[:, k, at], hi), first=(k == 0), end=(k == DK - 1))
                last.then_inc(tail_made, 1)

            PROJECTION = [(turn_heads, 0), (turn_heads, 1), (project_out, 0), (project_out, 1)]

            def front(b, hh):
                front_alone(lambda what, n: do(2 * b + hh, hh, what, n), lambda g: None,
                            lambda g: [early(n) for n in rows_turns(g)])
                pe.wait_ge(early_kept, 12)

            def step(b, hh, next_b, next_hh, last_b):
                def beside(work):
                    if next_b is not None:
                        for what, n in work:
                            do(2 * next_b + next_hh, next_hh, what, n)

                beside(LEAD[:1])
                turn_max(b, hh)
                if last_b is not None:
                    all_values(last_b, 1 - hh)
                beside(LEAD[1:])
                if last_b is not None:
                    turn_o(last_b, 1 - hh, 1)
                pe.wait_ge(max_in, 64 * (2 * b + hh + 2))
                for i in range(2 * UNIT_HEADS):
                    key_scores(b, hh, i)
                    beside(BESIDE[i])
                    if i in VALUES_AFTER:
                        values(b, hh, 0, VALUES_AFTER.index(i))
                    if i == OUTPUTS_AFTER:
                        turn_o(b, hh, 0)
                    if last_b is not None and i in (PROJECT_AFTER[1:] if hh == 0 else PROJECT_AFTER[:1]):
                        part, n = PROJECTION[PROJECT_AFTER.index(i)]
                        part(last_b, n)

            def finish(b):
                all_values(b, 1)
                turn_o(b, 1, 1)
                for part, n in PROJECTION[1:]:
                    part(b, n)

            unit_loop(pe, front, step, finish)



def macaron_kernel(nc, hidden, w_qkv, w_o, Wg, w1, w2, out):
    x_rows = hidden.rearrange("b s c -> (b s) c")
    out_rows = out.rearrange("b s c -> (b s) c")
    after_first = nc.dram_tensor("after_first", (TOK, D), F32, kind="Internal").ap()
    normed_rows = nc.dram_tensor("normed_rows", (TOK, D), F32, kind="Internal").ap()
    with ExitStack() as stack:
        const = Constants(nc, stack.enter_context)
        x = stack.enter_context(nc.sbuf_tensor("x", [P, T, D], F32))
        stats = stack.enter_context(nc.sbuf_tensor("stats", [P, T, 6], F32))
        rows_stored = stack.enter_context(nc.semaphore("rows_stored"))
        feed_forward(nc, const, "first", x, stats, x_rows, after_first, normed_rows, Wg, w1, w2, True, None)
        attention(nc, const, x, stats, after_first, out_rows, w_qkv, w_o, rows_stored)
        feed_forward(nc, const, "second", x, stats, None, out_rows, normed_rows, Wg, w1, w2, False, rows_stored)


_INS = ["L0_attn_hidden_states", "L0_attn_w_qkv", "L0_attn_w_o", "L0_ffn_Wg", "L0_ffn_w1", "L0_ffn_w2"]
_OUT = ((BATCH, SEQ, D), "float32")


def kernel(**inputs):
    import numpy as _np
    import concourse.bacc as _bacc
    from concourse import mybir as _mybir
    from concourse.bass_utils import run_bass_kernel_spmd as _run

    nc = _bacc.Bacc("TRN2", target_bir_lowering=False, num_devices=1)
    arrays, args = {}, []
    for name in _INS:
        a = _np.ascontiguousarray(inputs[name])
        arrays[f"in_{name}_dram"] = a
        args.append(nc.dram_tensor(f"in_{name}_dram", a.shape, _mybir.dt.from_np(a.dtype), kind="ExternalInput").ap())
    shape, dtype = _OUT
    args.append(nc.dram_tensor("out_0_dram", shape, _mybir.dt.from_np(_np.dtype(dtype)), kind="ExternalOutput").ap())
    macaron_kernel(nc, *args)
    r = _run(nc, [arrays], core_ids=[0])
    return r.results[0]["out_0_dram"]
```
